# Optimizing a Trainium2 kernel written in Bass

```python
import numpy as np
import jax
import jax.numpy as jnp

def _softmax(x, axis=-1):
    return jax.nn.softmax(x, axis=axis)

def _gelu(x):
    return jax.nn.gelu(x, approximate=True)

def _silu(x):
    return jax.nn.silu(x)

def _sigmoid(x):
    return jax.nn.sigmoid(x)

def _layernorm(x, axis=-1, eps=1e-05):
    m = jnp.mean(x, axis=axis, keepdims=True)
    v = jnp.var(x, axis=axis, keepdims=True)
    return (x - m) / jnp.sqrt(v + eps)

def _scatter_add(tgt, idx, src, axis=0):
    return tgt.at[idx].add(src)

def _segment_sum(src, seg, n):
    return jax.ops.segment_sum(src, seg, n)
kernel_name = 'mk_seq_postln_d4_jaxref_r8_66d21c'

def setup_inputs(seed: int=0):
    np.random.seed(seed)
    _w = jnp.asarray

    def _L0_attn_setup():
        import jax, jax.numpy as jnp
        import numpy as np
        EPS = 0.0001
        key = jax.random.key(seed)
        ks = jax.random.split(key, 6)
        B, T, DIM, H, S = (8, 256, 128, 16, 64)
        D = DIM // H
        tokens = jax.random.normal(ks[0], (B, T, DIM), dtype=jnp.float32)
        norm_w = jnp.ones((DIM,), dtype=jnp.float32)
        a = jnp.tile(jnp.eye(S, dtype=jnp.float32)[None], (H, 1, 1))
        b = jax.random.normal(ks[1], (H, D, S), dtype=jnp.float32) * 0.02
        c = jax.random.normal(ks[2], (H, S, D), dtype=jnp.float32) * 0.02
        skip = jnp.ones((H, D), dtype=jnp.float32)
        w_out = jax.random.normal(ks[3], (DIM, DIM), dtype=jnp.float32) * (1.0 / np.sqrt(DIM))
        b_out = jnp.zeros((DIM,), dtype=jnp.float32)
        return {'tokens': tokens, 'norm_w': norm_w, 'a': a, 'b': b, 'c': c, 'skip': skip, 'w_out': w_out, 'b_out': b_out}
    _L0_attn_in = _L0_attn_setup()

    def _L0_ffn_setup():
        import jax, jax.numpy as jnp
        import numpy as np
        HIDDEN = 128
        NUM_EXPERTS = 8
        TOP_K = 2
        key = jax.random.key(seed)
        k_x, k_r, k_w1, k_w2 = jax.random.split(key, 4)
        x = jax.random.normal(k_x, (4, 256, HIDDEN), dtype=jnp.float32)
        router_w = jax.random.normal(k_r, (NUM_EXPERTS, HIDDEN), dtype=jnp.float32) * HIDDEN ** (-0.5)
        w1 = jax.random.normal(k_w1, (NUM_EXPERTS, HIDDEN, 2 * HIDDEN), dtype=jnp.float32) * HIDDEN ** (-0.5)
        w2 = jax.random.normal(k_w2, (NUM_EXPERTS, 2 * HIDDEN, HIDDEN), dtype=jnp.float32) * (2 * HIDDEN) ** (-0.5)
        return {'x': x, 'router_w': router_w, 'w1': w1, 'w2': w2}
    _L0_ffn_in = _L0_ffn_setup()

    def _L1_attn_setup():
        import jax, jax.numpy as jnp
        import numpy as np
        import math
        N_HEAD = 16
        N_LATENTS = 64
        CHUNK = 128
        ROPE_THETA = 10000.0

        def _rope_cos_sin(T, D, theta):
            inv = 1.0 / theta ** (jnp.arange(0, D, 2, dtype=jnp.float32) / D)
            ang = jnp.arange(T, dtype=jnp.float32)[:, None] * inv[None, :]
            return (jnp.cos(ang), jnp.sin(ang))

        def _apply_rope(k, cos, sin):
            B, T, H, D = k.shape
            kr = k.reshape(B, T, H, D // 2, 2)
            a, b = (kr[..., 0], kr[..., 1])
            c = cos[None, :, None, :]
            s = sin[None, :, None, :]
            out = jnp.stack([a * c - b * s, a * s + b * c], axis=-1)
            return out.reshape(B, T, H, D).astype(k.dtype)
        key = jax.random.key(seed)
        ks = jax.random.split(key, 6)
        B, T, C = (8, 512, 128)
        H, L = (N_HEAD, N_LATENTS)
        D = C // H
        std_in = 1.0 / math.sqrt(C)
        return {'x': jax.random.normal(ks[0], (B, T, C), jnp.float32), 'latent_queries': jax.random.normal(ks[1], (1, L, H, D), jnp.float32) * (1.0 / math.sqrt(D)), 'W_k': jax.random.normal(ks[2], (C, C), jnp.float32) * std_in, 'W_v': jax.random.normal(ks[3], (C, C), jnp.float32) * std_in, 'W_g': jax.random.normal(ks[4], (H * L, C), jnp.float32) * std_in, 'W_p': jax.random.normal(ks[5], (C, C), jnp.float32) * std_in}
    _L1_attn_in = _L1_attn_setup()

    def _L1_ffn_setup():
        import jax, jax.numpy as jnp
        import numpy as np
        from jax import lax
        HIDDEN = 128
        INTER = 64
        E = 64
        K = 6
        G = 8
        TG = 4
        NSH = 2
        ISH = INTER * NSH

        def _moe_forward(hidden_states, gate_w, gate_bias, eg_w, eu_w, ed_w, sg_w, su_w, sd_w):
            B, S, H = hidden_states.shape
            x = hidden_states.reshape(-1, H)
            T = x.shape[0]
            shared = jax.nn.silu(x @ sg_w.T) * (x @ su_w.T) @ sd_w.T
            logits = x @ gate_w.T
            scores = jax.nn.sigmoid(logits) + gate_bias
            group_scores = scores.reshape(T, G, E // G).max(axis=-1)
            _, sel_groups = lax.top_k(group_scores, TG)
            group_mask = jnp.zeros((T, G), scores.dtype).at[jnp.arange(T)[:, None], sel_groups].set(1.0)
            mask = jnp.repeat(group_mask, E // G, axis=1)
            masked_scores = scores * mask
            topk_w, topk_i = lax.top_k(masked_scores, K)
            topk_w = topk_w / (topk_w.sum(axis=-1, keepdims=True) + 1e-08)
            comb = jnp.zeros((T, E), x.dtype).at[jnp.arange(T)[:, None], topk_i].add(topk_w)
            h = jax.nn.silu(jnp.einsum('th,eih->eti', x, eg_w)) * jnp.einsum('th,eih->eti', x, eu_w)
            routed = jnp.einsum('eti,ehi,te->th', h, ed_w, comb)
            return (shared + routed).reshape(B, S, H)
        key = jax.random.key(seed)
        ks = jax.random.split(key, 9)
        s = 0.02
        return {'hidden_states': jax.random.normal(ks[0], (1, 128, HIDDEN), jnp.float32), 'gate_w': jax.random.normal(ks[1], (E, HIDDEN), jnp.float32) * s, 'gate_bias': jnp.zeros((E,), jnp.float32), 'eg_w': jax.random.normal(ks[2], (E, INTER, HIDDEN), jnp.float32) * s, 'eu_w': jax.random.normal(ks[3], (E, INTER, HIDDEN), jnp.float32) * s, 'ed_w': jax.random.normal(ks[4], (E, HIDDEN, INTER), jnp.float32) * s, 'sg_w': jax.random.normal(ks[5], (ISH, HIDDEN), jnp.float32) * s, 'su_w': jax.random.normal(ks[6], (ISH, HIDDEN), jnp.float32) * s, 'sd_w': jax.random.normal(ks[7], (HIDDEN, ISH), jnp.float32) * s}
    _L1_ffn_in = _L1_ffn_setup()

    def _L2_attn_setup():
        import jax, jax.numpy as jnp
        import numpy as np
        HID = 128
        NH = 4
        DK = 32
        DV = 64
        C = 64
        EPS = 1e-05
        GLN = 16.0

        def _xavier(key, shape, gain=2 ** (-2.5)):
            fan_in, fan_out = shape
            lim = gain * np.sqrt(6.0 / (fan_in + fan_out))
            return jax.random.uniform(key, shape, jnp.float32, -lim, lim)

        def _chunk_simple_gla(q, k, v, g):
            B, H, N, dk = q.shape
            dv = v.shape[-1]
            nc = N // C
            scale = dk ** (-0.5)
            q = q.reshape(B, H, nc, C, dk) * scale
            k = k.reshape(B, H, nc, C, dk)
            v = v.reshape(B, H, nc, C, dv)
            g = g.reshape(B, H, nc, C)
            gc = jnp.cumsum(g, axis=-1)
            gt = gc[..., -1]
            dec = gc[..., :, None] - gc[..., None, :]
            mask = jnp.tril(jnp.ones((C, C), bool))
            A = jnp.einsum('bhntd,bhnsd->bhnts', q, k)
            A = A * jnp.where(mask, jnp.exp(jnp.where(mask, dec, 0.0)), 0.0)
            o_intra = jnp.einsum('bhnts,bhnsd->bhntd', A, v)
            qs = jnp.moveaxis(q, 2, 0)
            ks_ = jnp.moveaxis(k, 2, 0)
            vs = jnp.moveaxis(v, 2, 0)
            gcs = jnp.moveaxis(gc, 2, 0)
            gts = jnp.moveaxis(gt, 2, 0)
            S0 = jnp.zeros((B, H, dk, dv), q.dtype)

            def step(S, inp):
                qc, kc, vc, gcc, gtc = inp
                o_int = jnp.einsum('bhtd,bhde->bhte', qc * jnp.exp(gcc)[..., None], S)
                kd = kc * jnp.exp(gtc[..., None] - gcc)[..., None]
                S = jnp.exp(gtc)[..., None, None] * S + jnp.einsum('bhtd,bhte->bhde', kd, vc)
                return (S, o_int)
            _, o_inter = jax.lax.scan(step, S0, (qs, ks_, vs, gcs, gts))
            o = o_intra + jnp.moveaxis(o_inter, 0, 2)
            return o.reshape(B, H, N, dv)
        key = jax.random.key(seed)
        ks = jax.random.split(key, 8)
        x = jax.random.normal(ks[0], (4, 256, HID), jnp.float32)
        Wq = _xavier(ks[1], (HID, NH * DK))
        Wk = _xavier(ks[2], (HID, NH * DK))
        Wv = _xavier(ks[3], (HID, NH * DV))
        Wg = _xavier(ks[4], (HID, NH * DV))
        Wgk = _xavier(ks[5], (HID, NH))
        bgk = jnp.zeros((NH,), jnp.float32)
        Wo = _xavier(ks[6], (NH * DV, HID))
        gnorm_w = jnp.ones((DV,), jnp.float32)
        return {'x': x, 'Wq': Wq, 'Wk': Wk, 'Wv': Wv, 'Wg': Wg, 'Wgk': Wgk, 'bgk': bgk, 'Wo': Wo, 'gnorm_w': gnorm_w}
    _L2_attn_in = _L2_attn_setup()

    def _L2_ffn_setup():
        import jax, jax.numpy as jnp
        import numpy as np
        NUM_EXPERTS = 160
        TOP_K = 8
        ROUTED_SCALE = 2.5
        HIDDEN = 128
        INTER = 64
        key = jax.random.key(seed)
        ks = jax.random.split(key, 7)
        B, S = (1, 256)
        return {'hidden_states': jax.random.normal(ks[0], (B, S, HIDDEN), dtype=jnp.float32), 'router_w': jax.random.normal(ks[1], (NUM_EXPERTS, HIDDEN), dtype=jnp.float32) * 0.02, 'expert_bias': jnp.zeros((NUM_EXPERTS,), dtype=jnp.float32), 'w_gate': jax.random.normal(ks[2], (NUM_EXPERTS, INTER, HIDDEN), dtype=jnp.float32) * 0.02, 'w_down': jax.random.normal(ks[3], (NUM_EXPERTS, HIDDEN, INTER), dtype=jnp.float32) * 0.02, 'w_gate_shared': jax.random.normal(ks[4], (INTER, HIDDEN), dtype=jnp.float32) * 0.02, 'w_down_shared': jax.random.normal(ks[5], (HIDDEN, INTER), dtype=jnp.float32) * 0.02}
    _L2_ffn_in = _L2_ffn_setup()

    def _L3_attn_setup():
        import jax, jax.numpy as jnp
        import numpy as np
        DIM = 128
        DEPTH = 6
        HEADS = 8
        FF_MULT = 4
        LN_EPS = 1e-05
        LEAKY_SLOPE = 0.01

        def _layernorm(x, w, b):
            m = jnp.mean(x, axis=-1, keepdims=True)
            v = jnp.mean(jnp.square(x - m), axis=-1, keepdims=True)
            return (x - m) * jax.lax.rsqrt(v + LN_EPS) * w + b

        def _linear_attn(q, k, v):
            q = jax.nn.softmax(q, axis=-1)
            k = jax.nn.softmax(k, axis=-2)
            context = jnp.einsum('bhnd,bhne->bhde', k, v)
            return jnp.einsum('bhnd,bhde->bhne', q, context)
        key = jax.random.key(seed)
        ks = jax.random.split(key, 12)
        b, t = (2, 512)
        s = 0.02
        return {'x': jax.random.normal(ks[0], (b, t, DIM), dtype=jnp.float32), 'ln1_w': jnp.ones((DEPTH, DIM), jnp.float32), 'ln1_b': jnp.zeros((DEPTH, DIM), jnp.float32), 'wq': jax.random.normal(ks[1], (DEPTH, DIM, DIM), jnp.float32) * s, 'wk': jax.random.normal(ks[2], (DEPTH, DIM, DIM), jnp.float32) * s, 'wv': jax.random.normal(ks[3], (DEPTH, DIM, DIM), jnp.float32) * s, 'wo': jax.random.normal(ks[4], (DEPTH, DIM, DIM), jnp.float32) * s, 'bo': jnp.zeros((DEPTH, DIM), jnp.float32), 'ln2_w': jnp.ones((DEPTH, DIM), jnp.float32), 'ln2_b': jnp.zeros((DEPTH, DIM), jnp.float32), 'w1': jax.random.normal(ks[5], (DEPTH, DIM, FF_MULT * DIM), jnp.float32) * s, 'w2': jax.random.normal(ks[6], (DEPTH, FF_MULT * DIM, DIM), jnp.float32) * s}
    _L3_attn_in = _L3_attn_setup()

    def _L3_ffn_setup():
        import jax, jax.numpy as jnp
        import numpy as np
        B, T, D, E, H = (4, 256, 128, 4, 8)
        EPS = 1e-05

        def _uniform(k, shape, bound):
            return jax.random.uniform(k, shape, jnp.float32, -bound, bound)

        def _layernorm(x, w, b):
            mu = jnp.mean(x, axis=-1, keepdims=True)
            var = jnp.mean(jnp.square(x - mu), axis=-1, keepdims=True)
            return (x - mu) * jax.lax.rsqrt(var + EPS) * w + b
        key = jax.random.key(seed)
        ks = jax.random.split(key, 12)
        wb = np.sqrt(6.0 / D) / np.sqrt(6.0)
        wb = 1.0 / np.sqrt(D)
        return {'x': jax.random.normal(ks[0], (B, T, D), jnp.float32), 'router_prob': jax.random.uniform(ks[1], (B, T, E), jnp.float32), 'norm_w': jnp.ones((D,), jnp.float32), 'norm_b': jnp.zeros((D,), jnp.float32), 'q_w': _uniform(ks[2], (D, D), wb), 'q_b': _uniform(ks[3], (D,), wb), 'k_w': _uniform(ks[4], (D, D), wb), 'k_b': _uniform(ks[5], (D,), wb), 'v_w': _uniform(ks[6], (D, D), wb), 'v_b': _uniform(ks[7], (D,), wb), 'o_w': _uniform(ks[8], (D, D), wb), 'o_b': _uniform(ks[9], (D,), wb)}
    _L3_ffn_in = _L3_ffn_setup()
    _d = {'L0_attn_tokens': _L0_attn_in['tokens'], 'L0_attn_norm_w': _L0_attn_in['norm_w'], 'L0_attn_a': _L0_attn_in['a'], 'L0_attn_b': _L0_attn_in['b'], 'L0_attn_c': _L0_attn_in['c'], 'L0_attn_skip': _L0_attn_in['skip'], 'L0_attn_w_out': _L0_attn_in['w_out'], 'L0_attn_b_out': _L0_attn_in['b_out'], 'L0_ffn_router_w': _L0_ffn_in['router_w'], 'L0_ffn_w1': _L0_ffn_in['w1'], 'L0_ffn_w2': _L0_ffn_in['w2'], 'L1_attn_latent_queries': _L1_attn_in['latent_queries'], 'L1_attn_W_k': _L1_attn_in['W_k'], 'L1_attn_W_v': _L1_attn_in['W_v'], 'L1_attn_W_g': _L1_attn_in['W_g'], 'L1_attn_W_p': _L1_attn_in['W_p'], 'L1_ffn_gate_w': _L1_ffn_in['gate_w'], 'L1_ffn_gate_bias': _L1_ffn_in['gate_bias'], 'L1_ffn_eg_w': _L1_ffn_in['eg_w'], 'L1_ffn_eu_w': _L1_ffn_in['eu_w'], 'L1_ffn_ed_w': _L1_ffn_in['ed_w'], 'L1_ffn_sg_w': _L1_ffn_in['sg_w'], 'L1_ffn_su_w': _L1_ffn_in['su_w'], 'L1_ffn_sd_w': _L1_ffn_in['sd_w'], 'L2_attn_Wq': _L2_attn_in['Wq'], 'L2_attn_Wk': _L2_attn_in['Wk'], 'L2_attn_Wv': _L2_attn_in['Wv'], 'L2_attn_Wg': _L2_attn_in['Wg'], 'L2_attn_Wgk': _L2_attn_in['Wgk'], 'L2_attn_bgk': _L2_attn_in['bgk'], 'L2_attn_Wo': _L2_attn_in['Wo'], 'L2_attn_gnorm_w': _L2_attn_in['gnorm_w'], 'L2_ffn_router_w': _L2_ffn_in['router_w'], 'L2_ffn_expert_bias': _L2_ffn_in['expert_bias'], 'L2_ffn_w_gate': _L2_ffn_in['w_gate'], 'L2_ffn_w_down': _L2_ffn_in['w_down'], 'L2_ffn_w_gate_shared': _L2_ffn_in['w_gate_shared'], 'L2_ffn_w_down_shared': _L2_ffn_in['w_down_shared'], 'L3_attn_ln1_w': _L3_attn_in['ln1_w'], 'L3_attn_ln1_b': _L3_attn_in['ln1_b'], 'L3_attn_wq': _L3_attn_in['wq'], 'L3_attn_wk': _L3_attn_in['wk'], 'L3_attn_wv': _L3_attn_in['wv'], 'L3_attn_wo': _L3_attn_in['wo'], 'L3_attn_bo': _L3_attn_in['bo'], 'L3_attn_ln2_w': _L3_attn_in['ln2_w'], 'L3_attn_ln2_b': _L3_attn_in['ln2_b'], 'L3_attn_w1': _L3_attn_in['w1'], 'L3_attn_w2': _L3_attn_in['w2'], 'L3_ffn_router_prob': _L3_ffn_in['router_prob'], 'L3_ffn_norm_w': _L3_ffn_in['norm_w'], 'L3_ffn_norm_b': _L3_ffn_in['norm_b'], 'L3_ffn_q_w': _L3_ffn_in['q_w'], 'L3_ffn_q_b': _L3_ffn_in['q_b'], 'L3_ffn_k_w': _L3_ffn_in['k_w'], 'L3_ffn_k_b': _L3_ffn_in['k_b'], 'L3_ffn_v_w': _L3_ffn_in['v_w'], 'L3_ffn_v_b': _L3_ffn_in['v_b'], 'L3_ffn_o_w': _L3_ffn_in['o_w'], 'L3_ffn_o_b': _L3_ffn_in['o_b']}
    _x0 = _d['L0_attn_tokens']
    _d['L0_attn_tokens'] = jax.random.normal(jax.random.fold_in(jax.random.key(seed), 1), (8, 256, 128), dtype=_x0.dtype)
    del _x0
    return _d

def reference(L0_attn_tokens, L0_attn_norm_w, L0_attn_a, L0_attn_b, L0_attn_c, L0_attn_skip, L0_attn_w_out, L0_attn_b_out, L0_ffn_router_w, L0_ffn_w1, L0_ffn_w2, L1_attn_latent_queries, L1_attn_W_k, L1_attn_W_v, L1_attn_W_g, L1_attn_W_p, L1_ffn_gate_w, L1_ffn_gate_bias, L1_ffn_eg_w, L1_ffn_eu_w, L1_ffn_ed_w, L1_ffn_sg_w, L1_ffn_su_w, L1_ffn_sd_w, L2_attn_Wq, L2_attn_Wk, L2_attn_Wv, L2_attn_Wg, L2_attn_Wgk, L2_attn_bgk, L2_attn_Wo, L2_attn_gnorm_w, L2_ffn_router_w, L2_ffn_expert_bias, L2_ffn_w_gate, L2_ffn_w_down, L2_ffn_w_gate_shared, L2_ffn_w_down_shared, L3_attn_ln1_w, L3_attn_ln1_b, L3_attn_wq, L3_attn_wk, L3_attn_wv, L3_attn_wo, L3_attn_bo, L3_attn_ln2_w, L3_attn_ln2_b, L3_attn_w1, L3_attn_w2, L3_ffn_router_prob, L3_ffn_norm_w, L3_ffn_norm_b, L3_ffn_q_w, L3_ffn_q_b, L3_ffn_k_w, L3_ffn_k_b, L3_ffn_v_w, L3_ffn_v_b, L3_ffn_o_w, L3_ffn_o_b):

    def _L0_attn_ref(tokens, norm_w, a, b, c, skip, w_out, b_out):
        import jax, jax.numpy as jnp
        import numpy as np
        EPS = 0.0001
        B, T, DIM = tokens.shape
        H, D, S = b.shape
        ms = jnp.mean(jnp.square(tokens), axis=-1, keepdims=True)
        x = tokens * jax.lax.rsqrt(ms + EPS) * norm_w
        x = x.reshape(B, T, H, D)
        a_t = jnp.tanh(a)
        state0 = jnp.zeros((B, H, S), dtype=tokens.dtype)

        def step(state, x_t):
            state = jnp.tanh(jnp.einsum('bhs,hst->bht', state, a_t) + jnp.einsum('bhd,hds->bhs', x_t, b))
            mixed = jnp.einsum('bhs,hsd->bhd', state, c) + skip[None] * x_t
            return (state, mixed)
        xs = jnp.moveaxis(x, 1, 0)
        _, outs = jax.lax.scan(step, state0, xs)
        outs = jnp.moveaxis(outs, 0, 1).reshape(B, T, DIM)
        return tokens + outs @ w_out.T + b_out

    def _L0_ffn_ref(x, router_w, w1, w2):
        import jax, jax.numpy as jnp
        import numpy as np
        HIDDEN = 128
        NUM_EXPERTS = 8
        TOP_K = 2
        bsz, seq, hidden = x.shape
        tokens = x.reshape(-1, hidden)
        logits = tokens @ router_w.T
        topk_vals, topk_idx = jax.lax.top_k(logits, TOP_K)
        weights = jax.nn.softmax(topk_vals, axis=-1)
        h = jnp.einsum('td,edf->etf', tokens, w1)
        h = jax.nn.gelu(h, approximate=False)
        out_all = jnp.einsum('etf,efd->etd', h, w2)
        out_ted = jnp.transpose(out_all, (1, 0, 2))
        gathered = jnp.take_along_axis(out_ted, topk_idx[:, :, None], axis=1)
        output = jnp.sum(weights[:, :, None] * gathered, axis=1)
        return output.reshape(bsz, seq, hidden)

    def _L1_attn_ref(x, latent_queries, W_k, W_v, W_g, W_p):
        import jax, jax.numpy as jnp
        import numpy as np
        import math
        N_HEAD = 16
        N_LATENTS = 64
        CHUNK = 128
        ROPE_THETA = 10000.0

        def _rope_cos_sin(T, D, theta):
            inv = 1.0 / theta ** (jnp.arange(0, D, 2, dtype=jnp.float32) / D)
            ang = jnp.arange(T, dtype=jnp.float32)[:, None] * inv[None, :]
            return (jnp.cos(ang), jnp.sin(ang))

        def _apply_rope(k, cos, sin):
            B, T, H, D = k.shape
            kr = k.reshape(B, T, H, D // 2, 2)
            a, b = (kr[..., 0], kr[..., 1])
            c = cos[None, :, None, :]
            s = sin[None, :, None, :]
            out = jnp.stack([a * c - b * s, a * s + b * c], axis=-1)
            return out.reshape(B, T, H, D).astype(k.dtype)
        B, T, C = x.shape
        H, L, cs = (N_HEAD, N_LATENTS, CHUNK)
        D = C // H
        scale = 1.0 / math.sqrt(D)
        k = (x @ W_k.T).reshape(B, T, H, D)
        v = (x @ W_v.T).reshape(B, T, H, D)
        cos, sin = _rope_cos_sin(T, D, ROPE_THETA)
        k = _apply_rope(k, cos, sin)
        gates = jax.nn.softmax((x @ W_g.T).reshape(B, T, H, L) * scale, axis=-1)
        q = jnp.transpose(latent_queries, (0, 2, 1, 3))
        nc = T // cs
        kc = jnp.transpose(k, (0, 2, 1, 3)).reshape(B, H, nc, cs, D)
        vc = jnp.transpose(v, (0, 2, 1, 3)).reshape(B, H, nc, cs, D)
        scores = jnp.einsum('zhld,bhncd->bhnlc', q, kc) * scale
        causal = jnp.arange(cs)[None, :] <= jnp.arange(L)[:, None]
        scores = jnp.where(causal[None, None, None], scores, -jnp.inf)
        probs = jax.nn.softmax(scores, axis=-1)
        attn = jnp.einsum('bhnlc,bhncd->bhld', probs, vc)
        weighted = jnp.einsum('bhld,bthl->bthd', attn, gates)
        out = weighted.reshape(B, T, C) @ W_p.T
        return out

    def _L1_ffn_ref(hidden_states, gate_w, gate_bias, eg_w, eu_w, ed_w, sg_w, su_w, sd_w):
        import jax, jax.numpy as jnp
        import numpy as np
        from jax import lax
        HIDDEN = 128
        INTER = 64
        E = 64
        K = 6
        G = 8
        TG = 4
        NSH = 2
        ISH = INTER * NSH

        def _moe_forward(hidden_states, gate_w, gate_bias, eg_w, eu_w, ed_w, sg_w, su_w, sd_w):
            B, S, H = hidden_states.shape
            x = hidden_states.reshape(-1, H)
            T = x.shape[0]
            shared = jax.nn.silu(x @ sg_w.T) * (x @ su_w.T) @ sd_w.T
            logits = x @ gate_w.T
            scores = jax.nn.sigmoid(logits) + gate_bias
            group_scores = scores.reshape(T, G, E // G).max(axis=-1)
            _, sel_groups = lax.top_k(group_scores, TG)
            group_mask = jnp.zeros((T, G), scores.dtype).at[jnp.arange(T)[:, None], sel_groups].set(1.0)
            mask = jnp.repeat(group_mask, E // G, axis=1)
            masked_scores = scores * mask
            topk_w, topk_i = lax.top_k(masked_scores, K)
            topk_w = topk_w / (topk_w.sum(axis=-1, keepdims=True) + 1e-08)
            comb = jnp.zeros((T, E), x.dtype).at[jnp.arange(T)[:, None], topk_i].add(topk_w)
            h = jax.nn.silu(jnp.einsum('th,eih->eti', x, eg_w)) * jnp.einsum('th,eih->eti', x, eu_w)
            routed = jnp.einsum('eti,ehi,te->th', h, ed_w, comb)
            return (shared + routed).reshape(B, S, H)
        return _moe_forward(hidden_states, gate_w, gate_bias, eg_w, eu_w, ed_w, sg_w, su_w, sd_w)

    def _L2_attn_ref(x, Wq, Wk, Wv, Wg, Wgk, bgk, Wo, gnorm_w):
        import jax, jax.numpy as jnp
        import numpy as np
        HID = 128
        NH = 4
        DK = 32
        DV = 64
        C = 64
        EPS = 1e-05
        GLN = 16.0

        def _xavier(key, shape, gain=2 ** (-2.5)):
            fan_in, fan_out = shape
            lim = gain * np.sqrt(6.0 / (fan_in + fan_out))
            return jax.random.uniform(key, shape, jnp.float32, -lim, lim)

        def _chunk_simple_gla(q, k, v, g):
            B, H, N, dk = q.shape
            dv = v.shape[-1]
            nc = N // C
            scale = dk ** (-0.5)
            q = q.reshape(B, H, nc, C, dk) * scale
            k = k.reshape(B, H, nc, C, dk)
            v = v.reshape(B, H, nc, C, dv)
            g = g.reshape(B, H, nc, C)
            gc = jnp.cumsum(g, axis=-1)
            gt = gc[..., -1]
            dec = gc[..., :, None] - gc[..., None, :]
            mask = jnp.tril(jnp.ones((C, C), bool))
            A = jnp.einsum('bhntd,bhnsd->bhnts', q, k)
            A = A * jnp.where(mask, jnp.exp(jnp.where(mask, dec, 0.0)), 0.0)
            o_intra = jnp.einsum('bhnts,bhnsd->bhntd', A, v)
            qs = jnp.moveaxis(q, 2, 0)
            ks_ = jnp.moveaxis(k, 2, 0)
            vs = jnp.moveaxis(v, 2, 0)
            gcs = jnp.moveaxis(gc, 2, 0)
            gts = jnp.moveaxis(gt, 2, 0)
            S0 = jnp.zeros((B, H, dk, dv), q.dtype)

            def step(S, inp):
                qc, kc, vc, gcc, gtc = inp
                o_int = jnp.einsum('bhtd,bhde->bhte', qc * jnp.exp(gcc)[..., None], S)
                kd = kc * jnp.exp(gtc[..., None] - gcc)[..., None]
                S = jnp.exp(gtc)[..., None, None] * S + jnp.einsum('bhtd,bhte->bhde', kd, vc)
                return (S, o_int)
            _, o_inter = jax.lax.scan(step, S0, (qs, ks_, vs, gcs, gts))
            o = o_intra + jnp.moveaxis(o_inter, 0, 2)
            return o.reshape(B, H, N, dv)
        B, N, _ = x.shape
        q = (x @ Wq).reshape(B, N, NH, DK).transpose(0, 2, 1, 3)
        k = (x @ Wk).reshape(B, N, NH, DK).transpose(0, 2, 1, 3)
        v = (x @ Wv).reshape(B, N, NH, DV).transpose(0, 2, 1, 3)
        gk = (x @ Wgk + bgk).transpose(0, 2, 1)
        gk = jax.nn.log_sigmoid(gk) / GLN
        o = _chunk_simple_gla(q, k, v, gk)
        o = o.transpose(0, 2, 1, 3)
        g = (x @ Wg).reshape(B, N, NH, DV)
        on = o * jax.lax.rsqrt(jnp.mean(o * o, axis=-1, keepdims=True) + EPS) * gnorm_w
        o = on * (g * jax.nn.sigmoid(g))
        o = o.reshape(B, N, NH * DV)
        return o @ Wo

    def _L2_ffn_ref(hidden_states, router_w, expert_bias, w_gate, w_down, w_gate_shared, w_down_shared):
        import jax, jax.numpy as jnp
        import numpy as np
        NUM_EXPERTS = 160
        TOP_K = 8
        ROUTED_SCALE = 2.5
        HIDDEN = 128
        INTER = 64
        B, S, H = hidden_states.shape
        x = hidden_states.reshape(-1, H)
        T = x.shape[0]
        logits = x @ router_w.T + expert_bias[None, :]
        probs = jax.nn.sigmoid(logits)
        top_w, top_idx = jax.lax.top_k(probs, TOP_K)
        top_w = top_w / (jnp.sum(top_w, axis=-1, keepdims=True) + 1e-09)
        top_w = top_w * ROUTED_SCALE
        combine = jnp.zeros((T, NUM_EXPERTS), dtype=x.dtype)
        combine = combine.at[jnp.arange(T)[:, None], top_idx].set(top_w)
        h1 = jax.nn.silu(jnp.einsum('th,eih->eti', x, w_gate))
        h1w = h1 * combine.T[:, :, None]
        routed = jnp.einsum('eti,ehi->th', h1w, w_down)
        shared = jax.nn.silu(x @ w_gate_shared.T) @ w_down_shared.T
        return (routed + shared).reshape(B, S, H)

    def _L3_attn_ref(x, ln1_w, ln1_b, wq, wk, wv, wo, bo, ln2_w, ln2_b, w1, w2):
        import jax, jax.numpy as jnp
        import numpy as np
        DIM = 128
        DEPTH = 6
        HEADS = 8
        FF_MULT = 4
        LN_EPS = 1e-05
        LEAKY_SLOPE = 0.01

        def _layernorm(x, w, b):
            m = jnp.mean(x, axis=-1, keepdims=True)
            v = jnp.mean(jnp.square(x - m), axis=-1, keepdims=True)
            return (x - m) * jax.lax.rsqrt(v + LN_EPS) * w + b

        def _linear_attn(q, k, v):
            q = jax.nn.softmax(q, axis=-1)
            k = jax.nn.softmax(k, axis=-2)
            context = jnp.einsum('bhnd,bhne->bhde', k, v)
            return jnp.einsum('bhnd,bhde->bhne', q, context)
        b, t, e = x.shape
        h, dh = (HEADS, e // HEADS)
        for i in range(DEPTH):
            xn = _layernorm(x, ln1_w[i], ln1_b[i])
            q = (xn @ wq[i]).reshape(b, t, h, dh).transpose(0, 2, 1, 3)
            k = (xn @ wk[i]).reshape(b, t, h, dh).transpose(0, 2, 1, 3)
            v = (xn @ wv[i]).reshape(b, t, h, dh).transpose(0, 2, 1, 3)
            attn = _linear_attn(q, k, v)
            attn = attn.transpose(0, 2, 1, 3).reshape(b, t, e)
            x = attn @ wo[i] + bo[i] + x
            xn = _layernorm(x, ln2_w[i], ln2_b[i])
            hdn = xn @ w1[i]
            hdn = jnp.where(hdn >= 0, hdn, LEAKY_SLOPE * hdn)
            x = hdn @ w2[i] + x
        return x

    def _L3_ffn_ref(x, router_prob, norm_w, norm_b, q_w, q_b, k_w, k_b, v_w, v_b, o_w, o_b):
        import jax, jax.numpy as jnp
        import numpy as np
        B, T, D, E, H = (4, 256, 128, 4, 8)
        EPS = 1e-05

        def _uniform(k, shape, bound):
            return jax.random.uniform(k, shape, jnp.float32, -bound, bound)

        def _layernorm(x, w, b):
            mu = jnp.mean(x, axis=-1, keepdims=True)
            var = jnp.mean(jnp.square(x - mu), axis=-1, keepdims=True)
            return (x - mu) * jax.lax.rsqrt(var + EPS) * w + b
        e_cnt = router_prob.shape[2]
        b, t, d = x.shape
        n = t // e_cnt
        h = H
        scale = d ** (-0.5)
        qs, ks_, vs = ([], [], [])
        for e in range(e_cnt):
            xe = x[:, e * n:(e + 1) * n, :]
            xn = _layernorm(xe, norm_w, norm_b)
            m = d // 2 ** e
            xm = xn[..., :m]
            qs.append(jnp.einsum('bnm,dm->bnd', xm, q_w[:, :m]) + q_b)
            ks_.append(jnp.einsum('bnm,dm->bnd', xm, k_w[:, :m]) + k_b)
            vs.append(jnp.einsum('bnm,dm->bnd', xm, v_w[:, :m]) + v_b)
        q = jnp.concatenate(qs, axis=1)
        k = jnp.concatenate(ks_, axis=1)
        v = jnp.concatenate(vs, axis=1)
        dh = d // h
        q = q.reshape(b, t, h, dh).transpose(0, 2, 1, 3)
        k = k.reshape(b, t, h, dh).transpose(0, 2, 1, 3)
        v = v.reshape(b, t, h, dh).transpose(0, 2, 1, 3)
        attn = jnp.einsum('bhqd,bhkd->bhqk', q, k) * scale
        attn = jax.nn.softmax(attn, axis=-1)
        attn_out = jnp.einsum('bhqk,bhkd->bhqd', attn, v)
        attn_out = attn_out.transpose(0, 2, 1, 3).reshape(b, t, d)
        outs = []
        for e in range(e_cnt):
            sl = slice(e * n, (e + 1) * n)
            m = d // 2 ** e
            xm = attn_out[:, sl, :m]
            out = jnp.einsum('bnm,om->bno', xm, o_w[:m, :m]) + o_b[:m]
            pad = d - m
            if pad:
                out = jnp.pad(out, ((0, 0), (0, 0), (0, pad)))
            outs.append(out + x[:, sl, :])
        return jnp.concatenate(outs, axis=1)
    x = L0_attn_tokens
    x = _layernorm(x + _L0_attn_ref(x, L0_attn_norm_w, L0_attn_a, L0_attn_b, L0_attn_c, L0_attn_skip, L0_attn_w_out, L0_attn_b_out), axis=-1)
    x = _layernorm(x + _L0_ffn_ref(x, L0_ffn_router_w, L0_ffn_w1, L0_ffn_w2), axis=-1)
    x = _layernorm(x + _L1_attn_ref(x, L1_attn_latent_queries, L1_attn_W_k, L1_attn_W_v, L1_attn_W_g, L1_attn_W_p), axis=-1)
    x = _layernorm(x + _L1_ffn_ref(x, L1_ffn_gate_w, L1_ffn_gate_bias, L1_ffn_eg_w, L1_ffn_eu_w, L1_ffn_ed_w, L1_ffn_sg_w, L1_ffn_su_w, L1_ffn_sd_w), axis=-1)
    x = _layernorm(x + _L2_attn_ref(x, L2_attn_Wq, L2_attn_Wk, L2_attn_Wv, L2_attn_Wg, L2_attn_Wgk, L2_attn_bgk, L2_attn_Wo, L2_attn_gnorm_w), axis=-1)
    x = _layernorm(x + _L2_ffn_ref(x, L2_ffn_router_w, L2_ffn_expert_bias, L2_ffn_w_gate, L2_ffn_w_down, L2_ffn_w_gate_shared, L2_ffn_w_down_shared), axis=-1)
    x = _layernorm(x + _L3_attn_ref(x, L3_attn_ln1_w, L3_attn_ln1_b, L3_attn_wq, L3_attn_wk, L3_attn_wv, L3_attn_wo, L3_attn_bo, L3_attn_ln2_w, L3_attn_ln2_b, L3_attn_w1, L3_attn_w2), axis=-1)
    x = _layernorm(x + _L3_ffn_ref(x, L3_ffn_router_prob, L3_ffn_norm_w, L3_ffn_norm_b, L3_ffn_q_w, L3_ffn_q_b, L3_ffn_k_w, L3_ffn_k_b, L3_ffn_v_w, L3_ffn_v_b, L3_ffn_o_w, L3_ffn_o_b), axis=-1)
    return x

_drawn_inputs = setup_inputs


def setup_inputs(seed=0):
    import zlib

    import numpy as np

    out = dict(_drawn_inputs(seed))
    spreads = {'L0_attn_norm_w': (1.0, 0.2),
     'L0_attn_skip': (1.0, 0.2),
     'L0_attn_b_out': (0.0, 0.1),
     'L1_ffn_gate_bias': (0.0, 0.8),
     'L2_attn_bgk': (0.0, 0.8),
     'L2_attn_gnorm_w': (1.0, 0.6),
     'L2_ffn_expert_bias': (0.0, 0.666),
     'L3_attn_ln1_w': (1.0, 0.6),
     'L3_attn_ln1_b': (0.0, 0.8),
     'L3_attn_bo': (0.0, 0.1),
     'L3_attn_ln2_w': (1.0, 0.6),
     'L3_attn_ln2_b': (0.0, 0.8),
     'L3_ffn_norm_w': (1.0, 0.6),
     'L3_ffn_norm_b': (0.0, 0.8)}
    factors = {'L0_attn_a': 4.217,
     'L0_attn_b': 3.318,
     'L1_attn_latent_queries': 3.863,
     'L1_attn_W_k': 3.398,
     'L1_attn_W_g': 3.928,
     'L1_ffn_gate_w': 8.0,
     'L1_ffn_eg_w': 8.0,
     'L1_ffn_eu_w': 8.0,
     'L1_ffn_ed_w': 8.0,
     'L1_ffn_sg_w': 8.0,
     'L1_ffn_su_w': 8.0,
     'L1_ffn_sd_w': 8.0,
     'L2_attn_Wq': 3.944,
     'L2_attn_Wk': 3.891,
     'L2_attn_Wv': 3.912,
     'L2_attn_Wg': 3.922,
     'L2_attn_Wgk': 8.0,
     'L2_attn_Wo': 3.913,
     'L2_ffn_router_w': 3.689,
     'L2_ffn_w_gate': 3.543,
     'L2_ffn_w_down': 3.54,
     'L2_ffn_w_gate_shared': 3.118,
     'L2_ffn_w_down_shared': 3.145,
     'L3_attn_wq': 8.0,
     'L3_attn_wk': 8.0,
     'L3_ffn_q_w': 8.0,
     'L3_ffn_q_b': 8.0,
     'L3_ffn_k_w': 8.0,
     'L3_ffn_k_b': 8.0,
     'L3_ffn_v_w': 2.832,
     'L3_ffn_v_b': 6.886,
     'L3_ffn_o_w': 2.908,
     'L3_ffn_o_b': 3.014}
    for name, (base, spread) in spreads.items():
        noise = np.random.default_rng([zlib.crc32(name.encode()), seed]).standard_normal(out[name].shape)
        drawn = base * np.exp(spread * noise) if base else spread * noise
        out[name] = jnp.asarray(drawn.astype(out[name].dtype))
    for name, factor in factors.items():
        out[name] = (out[name] * factor).astype(out[name].dtype)
    return out
```

```python
from contextlib import ExitStack

import numpy as np
import concourse.bass as bass
from concourse import mybir

STAGES = '01234567'

F32 = mybir.dt.float32
BF16 = mybir.dt.bfloat16
F16 = mybir.dt.float16
ALU = mybir.AluOpType
ACT = mybir.ActivationFunctionType
AX = mybir.AxisListType

B, T, C = 8, 256, 128
N = B * T
P = 128
NT = N // P
NQ = 4
QW = N // NQ
LN_EPS = 1e-5


class Sems:

    def __init__(self, nc):
        self.nc, self.n, self.held = nc, 0, []

    def new(self, *names):
        out = []
        for name in names:
            guard = self.nc.semaphore(f"{name}_{self.n}")
            out.append(guard.__enter__())
            self.held.append((guard, out[-1]))
            self.n += 1
        return out if len(out) > 1 else out[0]

    def clear(self, first=0):
        nums = sorted(s.num for _, s in self.held[first:])
        run = 0
        for n in range(1, len(nums) + 1):
            if n == len(nums) or nums[n] != nums[n - 1] + 1:
                self.nc.gpsimd.sem_clear(range(nums[run], nums[n - 1] + 1))
                run = n
        self.nc.all_engine_barrier()

    def give_back(self):
        self.clear()
        for guard, _ in self.held:
            guard.__exit__(None, None, None)
        self.held = []


class State:
    pass


def layernorm_phase(nc, S, src, dst, eps=LN_EPS, gain=None, shift=None, out=None, sync=None, pool=None):
    rows_in, stats_s, aggr_s, std_s, rstd_s, shift_s, normed_dve, normed_act, back, stored, turned, high_s = S.sems.new(
        "ln_rows_in", "ln_stats", "ln_aggr", "ln_std", "ln_rstd", "ln_shift", "ln_normed_dve", "ln_normed_act",
        "ln_back", "ln_stored", "ln_turned", "ln_high")
    G = NT // 4
    HT = NT // 2
    order = [0, 1, 2, 3]
    ps, ident = S.psum, S.ident
    with (nc.sbuf_tensor(f"ln_stat{S.sems.n}", [P, NT, 6], F32) as stats,
          nc.sbuf_tensor(f"ln_mv{S.sems.n}", [P, NT, 2], F32) as mv,
          nc.sbuf_tensor(f"ln_sd{S.sems.n}", [P, NT], F32) as std,
          nc.sbuf_tensor(f"ln_rs{S.sems.n}", [P, NT], F32) as rstd,
          nc.sbuf_tensor(f"ln_nm{S.sems.n}", [P, NT], F32) as shifts,
          nc.sbuf_tensor(f"ln_x{S.sems.n}", [P, NT, C], F32) as rows,
          nc.Block(no_gpsimd_drain=True) as block):

        def wait_normed(engine, g):
            engine.wait_ge(normed_act if g % 2 else normed_dve, g // 2 + 1)

        @block.tensor
        def _(pe):
            for g in range(G):
                for j in range(4):
                    i = 4 * g + j
                    last = nc.tensor.transpose(ps[:, g, j * C:(j + 1) * C], src[:, i * P:(i + 1) * P], ident[:])
                last.then_inc(rows_in, 1)
            if out is None:
                for g in order:
                    wait_normed(pe, g)
                    for j in range(4):
                        last = nc.tensor.transpose(ps[:, G + g, j * P:(j + 1) * P], rows[:, 4 * g + j, :], ident[:])
                    last.then_inc(back, 1)

        @block.vector
        def _(dve):
            def statistics(h):
                for g in (2 * h, 2 * h + 1):
                    dve.wait_ge(rows_in, g + 1)
                    for j in range(4):
                        last = nc.vector.bn_stats(stats[:, 4 * g + j, :], ps[:, g, j * C:(j + 1) * C])
                last.then_inc(stats_s, 1)

            def aggregate(h):
                dve.wait_ge(stats_s, h + 1)
                for i in range(h * HT, (h + 1) * HT):
                    last = nc.vector.bn_aggr(mv[:, i, :], stats[:, i, :])
                last.then_inc(aggr_s, 1)

            def scales(h):
                half, theirs = slice(h * HT, (h + 1) * HT), slice(h * HT + 4, (h + 1) * HT)
                dve.wait_ge(std_s, h + 1)
                nc.vector.reciprocal(rstd[:, half], std[:, half]).then_inc(rstd_s, 1)
                dve.wait_ge(rstd_s, h + 1)
                nc.vector.scalar_tensor_tensor(out=shifts[:, theirs], in0=mv[:, theirs, 0], scalar=-1.0,
                                               in1=rstd[:, theirs], op0=ALU.mult, op1=ALU.mult).then_inc(shift_s, 1)

            def normalise(g):
                for i in range(4 * g, 4 * g + 4):
                    last = nc.vector.tensor_scalar(rows[:, i, :], ps[:, g, i % 4 * C:(i % 4 + 1) * C], mv[:, i, 0:1],
                                                   rstd[:, i:i + 1], ALU.subtract, ALU.mult)
                last.then_inc(normed_dve, 1)

            statistics(0)
            aggregate(0)
            statistics(1)
            scales(0)
            aggregate(1)
            normalise(0)
            scales(1)
            normalise(2)
            if out is None:
                for n, g in enumerate(order):
                    cut = slice(g * QW, (g + 1) * QW)
                    dve.wait_ge(turned, n + 1)
                    nc.vector.tensor_copy(S.x_hi[:, cut], dst[:, cut]).then_inc(high_s, 1)
                    dve.wait_ge(high_s, n + 1)
                    nc.vector.tensor_tensor(S.x_lo[:, cut], dst[:, cut], S.x_hi[:, cut], ALU.subtract)

        @block.scalar
        def _(act):
            for h in range(2):
                half = slice(h * HT, (h + 1) * HT)
                act.wait_ge(aggr_s, h + 1)
                nc.scalar.activation(std[:, half], mv[:, half, 1], ACT.Sqrt, bias=S.eps_ap(eps)).then_inc(std_s, 1)
                g = 2 * h + 1
                act.wait_ge(shift_s, h + 1)
                for i in range(4 * g, 4 * g + 4):
                    last = nc.scalar.activation(rows[:, i, :], ps[:, g, i % 4 * C:(i % 4 + 1) * C], ACT.Identity,
                                                bias=shifts[:, i:i + 1], scale=rstd[:, i:i + 1])
                last.then_inc(normed_act, 1)
            if out is None:
                for n, g in enumerate(order):
                    act.wait_ge(back, n + 1)
                    q = dst[:, g * QW:(g + 1) * QW]
                    if gain is None:
                        nc.scalar.activation(q, ps[:, G + g, :], ACT.Copy).then_inc(turned, 1)
                    else:
                        nc.scalar.activation(q, ps[:, G + g, :], ACT.Identity, bias=shift, scale=gain).then_inc(turned, 1)

        @block.gpsimd
        def _(engine):
            if pool is not None:
                pool(engine)

        @block.sync
        def _(sp):
            if sync is not None:
                sync(sp)
            if out is not None:
                rows_out = out.rearrange("b t c -> (b t) c").rearrange("(i p) c -> p i c", p=P)
                for g in range(G):
                    wait_normed(sp, g)
                    sp.dma_start(rows_out[:, 4 * g:4 * g + 4, :], rows[:, 4 * g:4 * g + 4, :]).then_inc(stored, 16)
                sp.wait_ge(stored, 16 * G)


def load_phase(nc, S, A):
    got, rows_up, x_s = S.sems.new("load_got", "load_rows_up", "load_x")
    ps = S.psum
    with (nc.sbuf_tensor("load_rows", [P, NT, C], F32) as rows,
          nc.Block(no_gpsimd_drain=True) as block):

        @block.sync
        def _(sp):
            sp.dma_start(S.ident[:], A["c_ident"]).then_inc(got, 16)
            sp.dma_start(S.identb[:], A["c_identb"]).then_inc(got, 16)
            sp.dma_start(rows[:], A["L0_attn_tokens"].rearrange("b t c -> (b t) c")
                         .rearrange("(i p) c -> p i c", p=P)).then_inc(got, 16)

        @block.vector
        def _(dve):
            for i, e in enumerate(S.eps):
                nc.vector.memset(S.epsilons[:, i:i + 1], e)
            dve.wait_ge(x_s, 4)
            nc.vector.tensor_copy(S.x_hi[:], S.xT[:]).then_inc(x_s, 1)
            dve.wait_ge(x_s, 5)
            nc.vector.tensor_tensor(S.x_lo[:], S.xT[:], S.x_hi[:], ALU.subtract)

        @block.tensor
        def _(pe):
            pe.wait_ge(got, 48)
            for g in range(4):
                for j in range(4):
                    last = nc.tensor.transpose(ps[:, g, j * P:(j + 1) * P], rows[:, 4 * g + j, :], S.ident[:])
                last.then_inc(rows_up, 1)

        @block.scalar
        def _(act):
            for g in range(4):
                act.wait_ge(rows_up, g + 1)
                nc.scalar.activation(S.xT[:, g * QW:(g + 1) * QW], ps[:, g, :], ACT.Copy).then_inc(x_s, 1)


def l0_attn(nc, S, A):
    H, D, SS = 16, 8, 64
    NP = H // 2
    GP = NP // 2
    K = 16
    NCH = T // K
    ps = S.psum
    with (nc.sbuf_tensor("rn_a", [P, NP, P], F32) as a_raw,
          nc.sbuf_tensor("rn_at", [P, NP, P], F32) as a_t,
          nc.sbuf_tensor("rn_b", [P, NP, P], F32) as b_w,
          nc.sbuf_tensor("rn_c", [P, NP, P], F32) as c_w,
          nc.sbuf_tensor("rn_wo", [P, P], F32) as w_o,
          nc.sbuf_tensor("rn_cols", [P, 3], F32) as cols,
          nc.sbuf_tensor("rn_xn", [P, N], F32) as xnT,
          nc.sbuf_tensor("rn_o", [P, N], F32) as outsT,
          nc.sbuf_tensor("rn_s_hi", [P, 2 * K, NP * B], F16) as s_hi,
          nc.sbuf_tensor("rn_s_lo", [P, 2 * K, NP * B], F16) as s_lo,
          nc.sbuf_tensor("rn_s_full", [P, 2, 2, GP * B], F32) as s_full,
          nc.sbuf_tensor("rn_xn_hi", [P, N], F16) as xn_hi,
          nc.sbuf_tensor("rn_xn_lo", [P, N], F16) as xn_lo,
          nc.sbuf_tensor("rn_weights", [P, 6, NP, P], F16) as w_parts,
          nc.sbuf_tensor("rn_sq", [P, N], F32) as sq):
        at_hi, at_lo, b_hi, b_lo, c_hi, c_lo = [w_parts[:, n] for n in range(6)]
        norm_w, skip, b_out = cols[:, 0:1], cols[:, 1:2], cols[:, 2:3]

        got, sq_s, sums, std_s, rstd_s, xr_s, rows_s = S.sems.new(
            "rms_got", "rms_sq", "rms_sums", "rms_std", "rms_rstd", "rms_scaled", "rms_rows")
        with (nc.sbuf_tensor("rms_ms", [P, NT], F32) as ms,
              nc.sbuf_tensor("rms_sd", [P, NT], F32) as sd,
              nc.sbuf_tensor("rms_rs", [P, NT], F32) as rs,
              nc.sbuf_tensor("rms_rows", [P, NT, C], F32) as rows,
              nc.Block(no_gpsimd_drain=True) as block):

            @block.sync
            def _(sp):
                sp.dma_start(a_raw[:], A["L0_attn_a"]).then_inc(got, 16)
                sp.dma_start(b_w[:], A["L0_attn_b"]).then_inc(got, 16)
                sp.dma_start(c_w[:], A["L0_attn_c"]).then_inc(got, 16)
                sp.dma_start(w_o[:], A["L0_attn_w_out"]).then_inc(got, 16)
                sp.dma_start(cols[:], A["L0_attn_cols"]).then_inc(got, 16)
                sp.wait_ge(got, 80)

            @block.tensor
            def _(pe):
                for g in range(4):
                    for j in range(4):
                        i = 4 * g + j
                        last = nc.tensor.transpose(ps[:, g, j * C:(j + 1) * C], S.xT[:, i * P:(i + 1) * P], S.ident[:])
                    last.then_inc(sums, 1)
                for g in range(4):
                    pe.wait_ge(xr_s, g + 1)
                    for j in range(4):
                        last = nc.tensor.transpose(ps[:, 4 + g, j * P:(j + 1) * P], rows[:, 4 * g + j, :], S.ident[:])
                    last.then_inc(rows_s, 1)

            @block.scalar
            def _(act):
                for g in range(4):
                    act.wait_ge(sums, g + 1)
                    for j in range(4):
                        i = 4 * g + j
                        last = nc.scalar.activation(sq[:, i * C:(i + 1) * C], ps[:, g, j * C:(j + 1) * C], ACT.Square,
                                                    accum_out=ms[:, i:i + 1])
                last.then_inc(sq_s, 1)
                act.wait_ge(sq_s, 1)
                nc.scalar.activation(sd[:], ms[:], ACT.Sqrt, bias=S.eps_ap(1e-4), scale=1.0 / C).then_inc(std_s, 1)
                act.wait_ge(got, 80)
                nc.scalar.activation(a_t[:], a_raw[:], ACT.Tanh)
                for g in range(4):
                    act.wait_ge(rows_s, g + 1)
                    nc.scalar.activation(xnT[:, g * QW:(g + 1) * QW], ps[:, 4 + g, :], ACT.Identity, scale=norm_w)

            @block.vector
            def _(dve):
                dve.wait_ge(std_s, 1)
                nc.vector.reciprocal(rs[:], sd[:]).then_inc(rstd_s, 1)
                dve.wait_ge(rstd_s, 1)
                for g in range(4):
                    for j in range(4):
                        i = 4 * g + j
                        last = nc.vector.tensor_scalar(rows[:, i, :], ps[:, g, j * C:(j + 1) * C], rs[:, i:i + 1], None,
                                                       ALU.mult)
                    last.then_inc(xr_s, 1)

        parts_s = S.sems.new("rnn_parts")
        with nc.Block(no_gpsimd_drain=True) as block:

            @block.vector
            def _(dve):
                for n, (hi, lo, full) in enumerate([(at_hi, at_lo, a_t), (b_hi, b_lo, b_w), (c_hi, c_lo, c_w),
                                                    (xn_hi[:], xn_lo[:], xnT)]):
                    nc.vector.tensor_copy(hi, full[:]).then_inc(parts_s, 1)
                    dve.wait_ge(parts_s, n + 1)
                    nc.vector.tensor_tensor(lo, full[:], hi, ALU.subtract)

        mm_done = S.sems.new("rnn_mm_first", "rnn_mm_second")
        hi_done = S.sems.new("rnn_hi_first", "rnn_hi_second")
        full_done = S.sems.new("rnn_full_first", "rnn_full_second")
        lo_done = S.sems.new("rnn_lo_first", "rnn_lo_second")
        outs_ready, outs_used = S.sems.new("rnn_outs_ready", "rnn_outs_used")
        xn_v = xnT[:].rearrange("p (b t) -> p t b", b=B)
        xn_hv = xn_hi[:].rearrange("p (b t r) -> p r t b", b=B, r=2)
        xn_lv = xn_lo[:].rearrange("p (b t r) -> p r t b", b=B, r=2)
        outs_v = outsT[:].rearrange("p (b t) -> p t b", b=B)
        W = GP * B

        def bank(g, r):
            return ps[:, 2 * g + r, :].rearrange("p (t c b) -> p t c b", t=K, c=GP)

        with nc.Block(no_gpsimd_drain=True) as block:

            @block.tensor
            def _(pe):
                with pe.Fori(0, NCH // 2) as i:
                    for g in range(2):
                        for r in range(2):
                            for c in range(GP):
                                n = g * GP + c
                                for w, m in ((b_hi, xn_hv), (b_lo, xn_hv), (b_hi, xn_lv)):
                                    nc.tensor.matmul(bank(g, r)[:, :, c, :], w[:, n, :], m[:, r, bass.ds(i * K, K), :],
                                                     start=(c == 0 and w is b_hi and m is xn_hv), stop=False,
                                                     skip_group_check=True)
                    for q in range(2):
                        step0 = i * (2 * K) + q * K
                        for t in range(q * K, (q + 1) * K):
                            prev = (t - 1) % (2 * K)
                            for g in range(2):
                                sums = bank(g, t % 2)[:, t // 2]
                                pe.wait_ge(hi_done[g], i * (2 * K) + (t + 1))
                                for w in (at_hi, at_lo):
                                    for c in range(GP):
                                        n = g * GP + c
                                        nc.tensor.matmul(sums[:, c, :], w[:, n, :], s_hi[:, prev, n * B:(n + 1) * B],
                                                         start=False, stop=False, skip_group_check=True)
                                pe.wait_ge(lo_done[g], i * (2 * K) + (t + 1))
                                for c in range(GP):
                                    n = g * GP + c
                                    last = nc.tensor.matmul(sums[:, c, :], at_hi[:, n, :], s_lo[:, prev, n * B:(n + 1) * B],
                                                            start=False, stop=(c == GP - 1), skip_group_check=True)
                                last.then_inc(mm_done[g], 1)
                        pe.wait_ge(outs_used, i * 2 + (q + 1))
                        for g in range(2):
                            pe.wait_ge(lo_done[g], step0 + (K + 1))
                        for w, m in ((c_hi, s_hi), (c_lo, s_hi), (c_hi, s_lo)):
                            for c in range(NP):
                                last = nc.tensor.matmul(ps[:, 4 + q, 0:K * B].rearrange("p (t b) -> p t b", b=B), w[:, c, :],
                                                        m[:, q * K:(q + 1) * K, c * B:(c + 1) * B],
                                                        start=(c == 0 and w is c_hi and m is s_hi),
                                                        stop=(c == NP - 1 and m is s_lo))
                        last.then_inc(outs_ready, 1)

            @block.scalar
            def _(act):
                with act.Fori(0, NCH // 2) as i:
                    for q in range(2):
                        for t in range(K):
                            for g in range(2):
                                act.wait_ge(mm_done[g], i * (2 * K) + (q * K + t + 1))
                                u = (q * K + t) // 2
                                sums = ps[:, 2 * g + t % 2, u * W:(u + 1) * W]
                                nc.scalar.activation(s_hi[:, q * K + t, g * W:(g + 1) * W], sums, ACT.Tanh)\
                                    .then_inc(hi_done[g], 1)
                                nc.scalar.activation(s_full[:, g, t % 2, :], sums, ACT.Tanh).then_inc(full_done[g], 1)

            @block.vector
            def _(dve):
                for g in range(2):
                    nc.vector.memset(s_hi[:, 2 * K - 1, g * W:(g + 1) * W], 0.0).then_inc(hi_done[g], 1)
                    nc.vector.memset(s_lo[:, 2 * K - 1, g * W:(g + 1) * W], 0.0).then_inc(lo_done[g], 1)
                dve.sem_inc(outs_used, 2)
                with dve.Fori(0, NCH // 2) as i:
                    for q in range(2):
                        at = bass.ds(i * (2 * K) + q * K, K)
                        for t in range(K):
                            for g in range(2):
                                dve.wait_ge(full_done[g], i * (2 * K) + (q * K + t + 1))
                                cut = slice(g * W, (g + 1) * W)
                                nc.vector.tensor_tensor(s_lo[:, q * K + t, cut], s_full[:, g, t % 2, :],
                                                        s_hi[:, q * K + t, cut], ALU.subtract).then_inc(lo_done[g], 1)
                        dve.wait_ge(outs_ready, i * 2 + (q + 1))
                        nc.vector.scalar_tensor_tensor(out=outs_v[:, at, :], in0=xn_v[:, at, :], scalar=skip,
                                                       in1=ps[:, 4 + q, 0:K * B].rearrange("p (t b) -> p t b", b=B),
                                                       op0=ALU.mult, op1=ALU.add).then_inc(outs_used, 1)

        y_ready, xb_s = S.sems.new("l0_y_ready", "l0_xb")
        with nc.Block(no_gpsimd_drain=True) as block:

            @block.tensor
            def _(pe):
                for g in range(NQ):
                    nc.tensor.matmul(ps[:, g, :], w_o[:], outsT[:, g * QW:(g + 1) * QW], start=True, stop=True)\
                        .then_inc(y_ready, 1)

            @block.vector
            def _(dve):
                nc.vector.tensor_scalar(sq[:], S.xT[:], 2.0, b_out, ALU.mult, ALU.add).then_inc(xb_s, 1)
                dve.wait_ge(xb_s, 1)
                for g in range(NQ):
                    dve.wait_ge(y_ready, g + 1)
                    cut = slice(g * QW, (g + 1) * QW)
                    nc.vector.tensor_tensor(S.rT[:, cut], sq[:, cut], ps[:, g, :], ALU.add)


GE = 42
SENTINEL, TAKEN = -1e30, -2e30


def route_phase(nc, S, tag, E, w_router, top_k, score, weigh, combT, bias=None, groups=None):
    NG = combT.shape[1]
    ps = S.psum
    EX = combT.shape[1] * GE
    got, logits_s, score_s, step_s, exp_s, diff_s, comb_up, comb_out = S.sems.new(
        *(f"{tag}_{n}" for n in ("got", "logits", "score", "step", "exp", "diff", "comb_up", "comb_out")))
    with (nc.sbuf_tensor(f"{tag}_w", [P, E], F32) as wr,
          nc.sbuf_tensor(f"{tag}_bias", [P, E], F32) as bias_sb,
          nc.sbuf_tensor(f"{tag}_sc", [P, NT, E + 8], F32) as sc,
          nc.sbuf_tensor(f"{tag}_raw", [P, NT, E], F32) as raw,
          nc.sbuf_tensor(f"{tag}_rep", [P, NT, E + 8], F32) as replaced,
          nc.sbuf_tensor(f"{tag}_top", [P, NT, 8], F32) as top,
          nc.sbuf_tensor(f"{tag}_want", [P, NT, 8], F32) as want,
          nc.sbuf_tensor(f"{tag}_gsc", [P, NT, 16], F32) as gsc,
          nc.sbuf_tensor(f"{tag}_gmask", [P, NT, 8], F32) as gmask,
          nc.sbuf_tensor(f"{tag}_sum", [P, NT], F32) as total,
          nc.sbuf_tensor(f"{tag}_rec", [P, NT], F32) as rec,
          nc.sbuf_tensor(f"{tag}_comb", [P, NT, EX], F32) as comb,
          nc.sbuf_tensor(f"{tag}_parts", [P, NT, NG, 3, GE], BF16) as parts,
          nc.Block(no_gpsimd_drain=True) as block):
        comb_v = comb[:].rearrange("p i (g e) -> p i g e", e=GE)

        @block.sync
        def _(sp):
            sp.dma_start(wr[:], w_router).then_inc(got, 16)
            if bias is not None:
                sp.dma_start(bias_sb[:], bias).then_inc(got, 16)
            sp.wait_ge(got, 32 if bias is not None else 16)

        @block.tensor
        def _(pe):
            pe.wait_ge(got, 32 if bias is not None else 16)
            for i in range(NT):
                last = nc.tensor.matmul(ps[:, i // 2, (i % 2) * E:(i % 2 + 1) * E], S.xT[:, i * P:(i + 1) * P], wr[:],
                                        start=True, stop=True)
                if i % 2:
                    last.then_inc(logits_s, 1)
            pe.wait_ge(comb_up, 1)
            n = 0
            for g in range(NG):
                for half in range(2):
                    if n >= 8:
                        pe.wait_ge(comb_out, n - 7)
                    else:
                        pe.wait_ge(score_s, 8)
                    bank = ps[:, n % 8, :].bitcast(BF16)
                    for j in range(8):
                        last = nc.tensor.transpose(bank[0:3 * GE, j * P:(j + 1) * P],
                                                   parts[:, 8 * half + j, g].rearrange("p a e -> p (a e)"), S.identb[:])
                    last.then_inc(diff_s, 1)
                    n += 1

        @block.scalar
        def _(act):
            for b in range(NT // 2):
                act.wait_ge(logits_s, b + 1)
                dst = raw[:, 2 * b:2 * b + 2, :]
                src = ps[:, b, 0:2 * E].rearrange("p (i e) -> p i e", e=E)
                nc.scalar.activation(dst, src, ACT.Sigmoid if score == "sigmoid_bias" else ACT.Copy).then_inc(score_s, 1)
            if score == "bias_sigmoid":
                act.wait_ge(exp_s, 1)
                nc.scalar.activation(sc[:, :, 0:E], raw[:], ACT.Sigmoid).then_inc(exp_s, 1)
            if weigh == "softmax":
                act.wait_ge(exp_s, 1)
                nc.scalar.activation(raw[:], raw[:], ACT.Exp).then_inc(exp_s, 1)
            for n in range(2 * NG):
                act.wait_ge(diff_s, n + 1)
                nc.scalar.activation(combT[0:3 * GE, n // 2, (n % 2) * 1024:(n % 2 + 1) * 1024],
                                     ps[:, n % 8, :].bitcast(BF16)[0:3 * GE, :], ACT.Copy).then_inc(comb_out, 1)

        @block.vector
        def _(dve):
            count = [0]

            def step(ins):
                count[0] += 1
                ins.then_inc(step_s, 1)
                dve.wait_ge(step_s, count[0])

            def choose(values, width, k, into):
                for i in range(NT):
                    last = nc.vector.max(top[:, i, :], values[:, i, 0:width])
                step(last)
                nc.vector.tensor_copy(want[:, :, 0:k], top[:, :, 0:k])
                step(nc.vector.memset(want[:, :, k:8], SENTINEL) if k < 8 else nc.vector.memset(gmask[:, :, 0:1], 0.0))
                for i in range(NT):
                    last = nc.vector.match_replace(into[:, i, :], want[:, i, :], values[:, i, :], TAKEN)
                step(last)

            nc.vector.memset(comb[:, :, E:EX], 0.0)
            nc.vector.memset(sc[:, :, E:E + 8], SENTINEL)
            nc.vector.memset(gsc[:, :, 8:16], SENTINEL)
            dve.wait_ge(score_s, NT // 2)
            if bias is not None:
                dve.wait_ge(got, 32)
                wide = bias_sb[:].unsqueeze(1).broadcast_to([P, NT, E])
            if score == "bias_sigmoid":
                nc.vector.tensor_tensor(raw[:], raw[:], wide, ALU.add).then_inc(exp_s, 1)
                dve.wait_ge(exp_s, 2)
            elif score == "sigmoid_bias":
                step(nc.vector.tensor_tensor(raw[:], raw[:], wide, ALU.add))
                step(nc.vector.tensor_reduce(gsc[:, :, 0:8], raw[:].rearrange("p i (g e) -> p i g e", g=8), AX.X, ALU.max))
                choose(gsc, 8, groups, replaced[:, :, 0:16])
                step(nc.vector.tensor_tensor(gmask[:], replaced[:, :, 0:8], gsc[:, :, 0:8], ALU.not_equal))
                step(nc.vector.tensor_tensor(sc[:, :, 0:E].rearrange("p i (g e) -> p i g e", g=8),
                                             raw[:].rearrange("p i (g e) -> p i g e", g=8),
                                             gmask[:].unsqueeze(3).broadcast_to([P, NT, 8, E // 8]), ALU.mult))
            else:
                step(nc.vector.tensor_copy(sc[:, :, 0:E], raw[:]))
            choose(sc, E, top_k, replaced)
            chosen = comb[:, :, 0:E]
            step(nc.vector.tensor_tensor(chosen, replaced[:, :, 0:E], sc[:, :, 0:E], ALU.not_equal))
            if weigh == "softmax":
                nc.vector.tensor_tensor(raw[:], raw[:], top[:, :, 0:1].broadcast_to([P, NT, E]), ALU.subtract)\
                    .then_inc(exp_s, 1)
                dve.wait_ge(exp_s, 2)
                step(nc.vector.tensor_tensor(chosen, chosen, raw[:], ALU.mult))
                step(nc.vector.tensor_reduce(total[:], chosen, AX.X, ALU.add))
                small, factor = 0.0, 1.0
            else:
                step(nc.vector.tensor_tensor(chosen, chosen, sc[:, :, 0:E], ALU.mult))
                step(nc.vector.tensor_reduce(total[:], top[:, :, 0:top_k], AX.X, ALU.add))
                small, factor = weigh
            step(nc.vector.tensor_scalar(total[:], total[:], small, None, ALU.add))
            step(nc.vector.reciprocal(rec[:], total[:]))
            step(nc.vector.tensor_scalar(rec[:], rec[:], factor, None, ALU.mult))
            step(nc.vector.tensor_tensor(chosen, chosen, rec[:].unsqueeze(2).broadcast_to([P, NT, E]), ALU.mult))
            if score != "logits":
                step(nc.vector.memset(comb[:, :, E:E + S.shared[tag]], 1.0))
            step(nc.vector.tensor_copy(parts[:, :, :, 0, :], comb_v))
            step(nc.vector.tensor_tensor(comb_v, comb_v, parts[:, :, :, 0, :], ALU.subtract))
            step(nc.vector.tensor_copy(parts[:, :, :, 1, :], comb_v))
            step(nc.vector.tensor_tensor(comb_v, comb_v, parts[:, :, :, 1, :], ALU.subtract))
            nc.vector.tensor_copy(parts[:, :, :, 2, :], comb_v).then_inc(comb_up, 1)


def experts_phase(nc, S, tag, weights, selector, combT, func, gated, UB):
    U, _, COLS = weights.shape
    NSEL = selector.shape[1]
    LAG = 3
    ps = S.psum
    acc = [ps[:, n, :] for n in range(NQ)]
    sel_got = S.sems.new(f"{tag}_sel_got")
    gate_done, up_done, comb_done, act_done, hu_done, hw_done, hi_done, lo_done, down_done, split_hi, split_done, split_start = S.sems.new(*(f"{tag}_{n}" for n in ("gate", "up", "combed", "act", "hu", "hw", "hi", "lo", "down",
                                                     "split_hi", "split", "split_start")))
    slot_got = [S.sems.new(f"{tag}_slot{s}") for s in range(UB)]
    x_hi, x_lo = S.x_hi, S.x_lo
    with (nc.sbuf_tensor(f"{tag}_sel", [P, NSEL, P], BF16) as sel,
          nc.sbuf_tensor(f"{tag}_stage", [P, UB, COLS], F32) as stage,
          nc.sbuf_tensor(f"{tag}_whi", [P, UB, COLS], F16) as w_hi,
          nc.sbuf_tensor(f"{tag}_wlo", [P, UB, COLS], F16) as w_lo,
          nc.sbuf_tensor(f"{tag}_h", [P, 2, QW], F32) as h,
          nc.sbuf_tensor(f"{tag}_hu", [P, 2, QW], F32) as hu,
          nc.sbuf_tensor(f"{tag}_hw", [P, 2, QW], F32) as hw,
          nc.sbuf_tensor(f"{tag}_hwhi", [P, 4, QW], F16) as hw_hi,
          nc.sbuf_tensor(f"{tag}_hwlo", [P, 4, QW], F16) as hw_lo):

        with nc.Block(no_gpsimd_drain=True) as block:

            @block.sync
            def _(sp):
                sp.dma_start(sel[0:3 * GE], selector).then_inc(sel_got, 16)
                sp.wait_ge(sel_got, 16)

            @block.gpsimd
            def _(pool):
                nc.gpsimd.memset(w_hi[:, UB - 1, :], 0.0)
                nc.gpsimd.memset(w_lo[:, UB - 1, :], 0.0)
                nc.gpsimd.memset(hw[:, 1, :], 0.0)
                nc.gpsimd.memset(hw_hi[:, 1:4, :], 0.0)
                nc.gpsimd.memset(hw_lo[:, 1:4, :], 0.0)

            @block.tensor
            def _(pe):
                for n in range(NQ):
                    nc.tensor.matmul(acc[n], S.ident[:], S.xT[:, n * QW:(n + 1) * QW], start=True, stop=False,
                                     skip_group_check=True)

        runs = []
        for g in range((U + NSEL - 1) // NSEL):
            runs.append((g * NSEL, (min(U, (g + 1) * NSEL) - g * NSEL) // UB, g))
        assert sum(r[1] for r in runs) * UB == U

        with nc.Block(no_gpsimd_drain=True) as block:

            @block.sync
            def _(sp):
                for u0, bodies, _ in runs:
                    with sp.Fori(0, bodies) as j:
                        for s in range(UB):
                            sp.wait_ge(split_done, j * UB + (u0 + s + 1))
                            sp.dma_start(stage[:, s, :], weights[bass.ds(j * UB + (u0 + s), 1)]
                                         .rearrange("u p c -> p (u c)")).then_inc(slot_got[s], 16)

            @block.gpsimd
            def _(pool):
                pool.sem_inc(split_done, UB)
                for u0, bodies, _ in runs:
                    with pool.Fori(0, bodies) as j:
                        for s in range(UB):
                            u = j * UB + (u0 + s)
                            pool.wait_ge(down_done, j * (4 * UB) + 4 * (u0 + s) + LAG)
                            pool.wait_ge(slot_got[s], j * 16 + (u0 // UB * 16 + 16))
                            pool.sem_inc(split_start, 1)
                            nc.gpsimd.tensor_copy(w_hi[:, s, :], stage[:, s, :]).then_inc(split_hi, 1)
                            pool.wait_ge(split_hi, u + 1)
                            nc.gpsimd.tensor_tensor(w_lo[:, s, :], stage[:, s, :], w_hi[:, s, :], ALU.subtract)\
                                .then_inc(split_done, 1)

            @block.tensor
            def _(pe):
                pe.sem_inc(down_done, 4 * (UB - 1))

                def product(out, cols, s, n):
                    cut = slice(n * QW, (n + 1) * QW)
                    for a, b in ((w_hi, x_hi), (w_hi, x_lo), (w_lo, x_hi)):
                        last = nc.tensor.matmul(out, a[:, s, cols], b[:, cut], start=(a is w_hi and b is x_hi),
                                                stop=(a is w_lo))
                    return last

                def down(s, n, k4):
                    for a, b in ((w_hi, hw_hi), (w_hi, hw_lo), (w_lo, hw_hi)):
                        last = nc.tensor.matmul(acc[n], a[:, s, COLS - P:COLS], b[:, k4, :], start=False, stop=False,
                                                skip_group_check=True)
                    return last.then_inc(down_done, 1)

                for u0, bodies, g in runs:
                    with pe.Fori(0, bodies) as j:
                        for s in range(UB):
                            pe.wait_ge(split_done, j * UB + (u0 + s + 1 + UB))
                            for n in range(NQ):
                                k = 4 * s + n
                                kk = j * (4 * UB) + (4 * u0 + k)
                                R = 3 * k if gated else None
                                hb = ps[:, 4 + (R % 4 if gated else k % 2), :]
                                cb = ps[:, 4 + ((R + 2) % 4 if gated else 2 + k % 2), :]
                                pe.wait_ge(hw_done, kk + 1)
                                product(hb, slice(0, P), s, n).then_inc(gate_done, 1)
                                if gated:
                                    pe.wait_ge(act_done, kk + 1)
                                    product(ps[:, 4 + (R + 1) % 4, :], slice(P, 2 * P), s, n).then_inc(up_done, 1)
                                    pe.wait_ge(hu_done, kk + 1)
                                nc.tensor.matmul(cb, sel[0:3 * GE, bass.ds(j * UB + s, 1), :].rearrange("p u m -> p (u m)"),
                                                 combT[0:3 * GE, g, n * QW:(n + 1) * QW], start=True, stop=True)\
                                    .then_inc(comb_done, 1)
                                pe.wait_ge(lo_done, kk + 1)
                                down((s if n >= LAG else s - 1) % UB, (n - LAG) % NQ, (k - LAG) % 4)
                for n in range(NQ - LAG, NQ):
                    pe.wait_ge(lo_done, 4 * U + n)
                    down(UB - 1, n, n)

            @block.scalar
            def _(act):
                act.sem_inc(act_done, 1)

                def high(k):
                    nc.scalar.activation(hw_hi[:, k % 4, :], hw[:, k % 2, :], ACT.Copy).then_inc(hi_done, 1)

                for u0, bodies, _ in runs:
                    with act.Fori(0, bodies) as j:
                        for k in range(4 * UB):
                            kk = j * (4 * UB) + (4 * u0 + k)
                            act.wait_ge(gate_done, kk + 1)
                            nc.scalar.activation(h[:, k % 2, :], ps[:, 4 + (3 * k % 4 if gated else k % 2), :], func)\
                                .then_inc(act_done, 1)
                            act.wait_ge(hw_done, kk + 2)
                            high(k - 1)
                act.wait_ge(hw_done, 4 * U + 2)
                high(4 * U - 1)
                act.wait_ge(down_done, 4 * (UB - 1) + 4 * U + LAG)
                for n in range(NQ):
                    nc.scalar.activation(S.rT[:, n * QW:(n + 1) * QW], acc[n], ACT.Copy)

            @block.vector
            def _(dve):
                dve.sem_inc(hw_done, 2)
                dve.sem_inc(lo_done, LAG - 1)
                if gated:
                    dve.sem_inc(hu_done, 1)

                def low(k):
                    nc.vector.tensor_tensor(hw_lo[:, k % 4, :], hw[:, k % 2, :], hw_hi[:, k % 4, :], ALU.subtract)\
                        .then_inc(lo_done, 1)

                for u0, bodies, _ in runs:
                    with dve.Fori(0, bodies) as j:
                        for k in range(4 * UB):
                            kk = j * (4 * UB) + (4 * u0 + k)
                            src = h
                            dve.wait_ge(act_done, kk + 2)
                            dve.wait_ge(lo_done, kk + 2)
                            if gated:
                                dve.wait_ge(up_done, kk + 1)
                                nc.vector.tensor_tensor(hu[:, k % 2, :], h[:, k % 2, :], ps[:, 4 + (3 * k + 1) % 4, :],
                                                        ALU.mult).then_inc(hu_done, 1)
                                src = hu
                                dve.wait_ge(hu_done, kk + 2)
                            dve.wait_ge(comb_done, kk + 1)
                            cb = ps[:, 4 + ((3 * k + 2) % 4 if gated else 2 + k % 2), :]
                            nc.vector.tensor_tensor(hw[:, k % 2, :], src[:, k % 2, :], cb, ALU.mult).then_inc(hw_done, 1)
                            dve.wait_ge(hi_done, kk + 1)
                            low(k - 1)
                dve.wait_ge(hi_done, 4 * U + 1)
                low(4 * U - 1)


def moe(nc, S, tag, E, weights, selector, func, gated, UB, **route):
    U = weights.shape[0]
    NG = (U + selector.shape[1] - 1) // selector.shape[1]
    with nc.sbuf_tensor(f"{tag}_combT", [P, NG, N], BF16) as combT:
        route_phase(nc, S, f"{tag}r", E, combT=combT, **route)
        experts_phase(nc, S, tag, weights, selector, combT, func, gated, UB)


def l0_ffn(nc, S, A):
    moe(nc, S, "m0", 8, A["m0_w"], A["c_sel_halves"], ACT.Gelu, False, 4,
        w_router=A["m0_router"], top_k=2, score="logits", weigh="softmax")


def l1_ffn(nc, S, A):
    moe(nc, S, "m1", 64, A["m1_w"], A["c_sel_pairs"], ACT.Silu, True, 3,
        w_router=A["m1_router"], top_k=6, score="sigmoid_bias", weigh=(1e-8, 1.0), bias=A["m1_bias"], groups=4)


def l2_ffn(nc, S, A):
    moe(nc, S, "m2", 160, A["m2_w"], A["c_sel_pairs"], ACT.Silu, False, 3,
        w_router=A["m2_router"], top_k=8, score="bias_sigmoid", weigh=(1e-9, 2.5), bias=A["m2_bias"])


def pipeline(eng, n, lag, step, unroll=2, head=None):
    head = head or max(4, unroll)
    for k in range(head):
        step(0, k)
    with eng.Fori(0, (n - head) // unroll) as j:
        for k in range(head, head + unroll):
            step(j, k)
    for k in range(n, n + lag):
        step(0, k)


def live(j, k, n):
    return not isinstance(j, int) or 0 <= k < n


def wait(eng, sem, j, k, unroll=2):
    if not isinstance(j, int):
        eng.wait_ge(sem, j * unroll + k)
    elif k > 0:
        eng.wait_ge(sem, k)


def split_on(dve, sem, count, hi, lo, full):
    nc = dve.bass
    nc.vector.tensor_copy(hi, full).then_inc(sem, 1)
    dve.wait_ge(sem, count)
    return nc.vector.tensor_tensor(lo, full, hi, ALU.subtract)


def products(nc, out, lhs, rhs, first=True, last=True, skip=False):
    (a_hi, a_lo), (b_hi, b_lo) = lhs, rhs
    nc.tensor.matmul(out, a_hi, b_hi, start=first, stop=False, skip_group_check=skip)
    nc.tensor.matmul(out, a_hi, b_lo, start=False, stop=False, skip_group_check=skip)
    return nc.tensor.matmul(out, a_lo, b_hi, start=False, stop=last, skip_group_check=skip)


def l1_attn(nc, S, A):
    H, L, D, CH = 16, 64, 8, 128
    NCH = T // CH
    NP = H // 2
    VW = 2 * D + 2
    SC = D ** -0.5
    ps = S.psum
    WN = 4 * P + H * L + NP * P
    with (nc.sbuf_tensor("la_w", [P, WN], F32) as w,
          nc.sbuf_tensor("la_whi", [P, WN], F16) as w_hi,
          nc.sbuf_tensor("la_wlo", [P, WN], F16) as w_lo,
          nc.sbuf_tensor("la_rope", [P, 2, NCH * L], F32) as rope,
          nc.sbuf_tensor("la_mask", [P, 512], BF16) as mask,
          nc.sbuf_tensor("la_own", [P, 2 * D], F32) as own,
          nc.sbuf_tensor("la_khi", [P, B, NCH, L], F16) as k_hi,
          nc.sbuf_tensor("la_klo", [P, B, NCH, L], F16) as k_lo,
          nc.sbuf_tensor("la_vhi", [P, B, NP, NCH, VW], F16) as v_hi,
          nc.sbuf_tensor("la_vlo", [P, B, NP, NCH, VW], F16) as v_lo,
          nc.sbuf_tensor("la_athi", [P, B, NP, VW], F16) as at_hi,
          nc.sbuf_tensor("la_atlo", [P, B, NP, VW], F16) as at_lo,
          nc.sbuf_tensor("la_wT", [P, N], F32) as wT):

        def cols(a, n=P):
            return w_hi[:, a:a + n], w_lo[:, a:a + n]

        W_K, W_KR, W_V, W_P = (cols(n * P) for n in range(4))
        W_G = [cols(4 * P + n * 512, 512) for n in range(2)]
        Q = [cols(4 * P + H * L + n * P) for n in range(NP)]

        got, parts_s, k_up, v_up, v_high, rope_s, done_s = S.sems.new(
            "la_got", "la_parts", "la_kup", "la_vup", "la_vhigh", "la_rope", "la_kv")
        with (nc.sbuf_tensor("la_kc", [P, 2, 512], F32) as kc,
              nc.sbuf_tensor("la_kr", [P, 2, 512], F32) as kr,
              nc.Block(no_gpsimd_drain=True) as block):
            seen = [x[:].rearrange("p (b n c) -> p b n c", b=B, n=NCH)[:, :, :, 0:L] for x in (S.x_hi, S.x_lo)]

            @block.sync
            def _(sp):
                for dst, src in ((w[:], "la_w"), (rope[:], "la_rope"), (mask[:], "la_mask"), (own[:], "la_own"),
                                 (at_hi[:], "la_ones_hi"), (at_lo[:], "la_zeros")):
                    sp.dma_start(dst, A[src]).then_inc(got, 16)
                sp.wait_ge(got, 96)

            @block.tensor
            def _(pe):
                pe.wait_ge(parts_s, 2)
                for half in range(2):
                    cut = slice(4 * half, 4 * half + 4)
                    for n, wk in enumerate((W_K, W_KR)):
                        last = products(nc, ps[:, 2 * half + n, :], wk, (seen[0][:, cut], seen[1][:, cut]))
                    last.then_inc(k_up, 1)
                for b in range(B):
                    if b >= 4:
                        pe.wait_ge(done_s, b - 3)
                    for n in range(NCH):
                        last = products(nc, ps[n * L:(n + 1) * L, 4 + b % 4, 0:P], (seen[0][:, b, n], seen[1][:, b, n]),
                                        W_V)
                    last.then_inc(v_up, 1)

            @block.scalar
            def _(act):
                for b in range(B):
                    act.wait_ge(v_up, b + 1)
                    for n in range(NCH):
                        r = slice(n * L, (n + 1) * L)
                        last = nc.scalar.activation(v_hi[r, b, :, n, 0:2 * D],
                                                    ps[r, 4 + b % 4, 0:P].rearrange("p (c d) -> p c d", c=NP), ACT.Copy)
                    last.then_inc(v_high, 1)

            @block.vector
            def _(dve):
                for n in range(NCH):
                    r, other = slice(n * L, (n + 1) * L), slice((1 - n) * L, (2 - n) * L)
                    nc.vector.memset(v_hi[other, :, :, n, :], 0.0)
                    nc.vector.memset(v_lo[other, :, :, n, :], 0.0)
                    nc.vector.memset(v_hi[r, :, :, n, 2 * D:VW], 1.0)
                    nc.vector.memset(v_lo[r, :, :, n, 2 * D:VW], 0.0)
                dve.wait_ge(got, 96)
                split_on(dve, parts_s, 1, w_hi[:], w_lo[:], w[:]).then_inc(parts_s, 1)
                n = 0
                for half in range(2):
                    dve.wait_ge(k_up, half + 1)
                    for m, t in enumerate((kc, kr)):
                        nc.vector.tensor_tensor(t[:, half, :].rearrange("p (b n) -> p b n", b=4),
                                                ps[:, 2 * half + m, :].rearrange("p (b n) -> p b n", b=4),
                                                rope[:, m:m + 1, :].broadcast_to([P, 4, NCH * L]), ALU.mult)\
                            .then_inc(rope_s, 1)
                    n += 2
                    dve.wait_ge(rope_s, n)
                    nc.vector.tensor_tensor(kc[:, half, :], kc[:, half, :], kr[:, half, :], ALU.add).then_inc(rope_s, 1)
                    n += 1
                    dve.wait_ge(rope_s, n)
                    flat = [t[:, 4 * half:4 * half + 4].rearrange("p b n c -> p (b n c)") for t in (k_hi, k_lo)]
                    n += 1
                    split_on(dve, rope_s, n, flat[0], flat[1], kc[:, half, :])
                for b in range(B):
                    dve.wait_ge(v_high, b + 1)
                    for n in range(NCH):
                        r = slice(n * L, (n + 1) * L)
                        last = nc.vector.tensor_tensor(v_lo[r, b, :, n, 0:2 * D],
                                                       ps[r, 4 + b % 4, 0:P].rearrange("p (c d) -> p c d", c=NP),
                                                       v_hi[r, b, :, n, 0:2 * D], ALU.subtract)
                    last.then_inc(done_s, 1)

        s_up, mx_s, sub_s, exp_s, t_up, t_hi, t_lo, o_up, at_s, small = S.sems.new(
            *(f"lb_{n}" for n in ("s_up", "max", "sub", "exp", "t_up", "t_hi", "t_lo", "o_up", "at", "small")))
        with (nc.sbuf_tensor("lb_mx", [P, 2, NP * NCH], F32) as mx,
              nc.sbuf_tensor("lb_z", [P, 2, 1024], F32) as z,
              nc.sbuf_tensor("lb_e", [P, 2, 1024], F32) as e,
              nc.sbuf_tensor("lb_thi", [P, 2, 1024], F16) as pt_hi,
              nc.sbuf_tensor("lb_tlo", [P, 2, 1024], F16) as pt_lo,
              nc.sbuf_tensor("lb_rec", [P, NP, NCH], F32) as rec,
              nc.sbuf_tensor("lb_o", [P, NP, NCH, 2 * D], F32) as o,
              nc.Block(no_gpsimd_drain=True) as block):

            def scores(q):
                return ps[:, 2 * q:2 * q + 2, :].rearrange("p a n -> p (a n)")

            turned = ps[:, 4:6, :].rearrange("p a n -> p (a n)")

            @block.tensor
            def _(pe):
                def step(j, k):
                    if live(j, k, B):
                        q = k % 2
                        wait(pe, sub_s, j, k - 1)
                        keys = [t[:, bass.ds(j * 2 + k, 1)].rearrange("p b n c -> p (b n c)") for t in (k_hi, k_lo)]
                        for m in range(2):
                            nc.tensor.matmul(ps[:, 2 * q + m, :], S.identb[:], mask[:], start=True, stop=False,
                                             skip_group_check=True)
                            for c in range(4):
                                last = products(nc, ps[:, 2 * q + m, c * P:(c + 1) * P], Q[4 * m + c], keys,
                                                first=False, last=(c == 3), skip=True)
                        last.then_inc(s_up, 1)
                    if live(j, k - 1, B):
                        wait(pe, exp_s, j, k)
                        wait(pe, t_lo, j, k - 1)
                        for c in range(NP):
                            last = nc.tensor.transpose(ps[:, 4 + c // 4, c % 4 * P:(c % 4 + 1) * P],
                                                       e[:, (k - 1) % 2, c * P:(c + 1) * P], S.ident[:])
                        last.then_inc(t_up, 1)
                    if live(j, k - 2, B):
                        wait(pe, t_lo, j, k - 1)
                        wait(pe, at_s, j, k - 3)
                        for c in range(NP):
                            lhs = [t[:, k % 2, c * P:(c + 1) * P] for t in (pt_hi, pt_lo)]
                            rhs = [t[:, bass.ds(j * 2 + (k - 2), 1), c].rearrange("p b n v -> p (b n v)")
                                   for t in (v_hi, v_lo)]
                            last = products(nc, ps[:, 6 + k % 2, c * NCH * VW:(c + 1) * NCH * VW], lhs, rhs)
                        last.then_inc(o_up, 1)
                pipeline(pe, B, 2, step)

            @block.scalar
            def _(act):
                def step(j, k):
                    if live(j, k, B):
                        wait(act, sub_s, j, k + 1)
                        wait(act, t_up, j, k - 1)
                        nc.scalar.activation(e[:, k % 2, :], z[:, k % 2, :], ACT.Exp, scale=SC).then_inc(exp_s, 1)
                    if live(j, k - 1, B):
                        wait(act, t_up, j, k)
                        wait(act, o_up, j, k - 2)
                        nc.scalar.activation(pt_hi[:, (k - 1) % 2, :], turned, ACT.Copy).then_inc(t_hi, 1)
                pipeline(act, B, 1, step)

            @block.vector
            def _(dve):
                def step(j, k):
                    if live(j, k, B):
                        q = k % 2
                        wait(dve, s_up, j, k + 1)
                        s4 = scores(q).rearrange("p (c n) -> p c n", n=L)
                        nc.vector.tensor_reduce(mx[:, q, :], s4, AX.X, ALU.max).then_inc(mx_s, 1)
                        wait(dve, mx_s, j, k + 1)
                        wait(dve, exp_s, j, k - 1)
                        nc.vector.tensor_tensor(z[:, q, :].rearrange("p (c n) -> p c n", n=L), s4,
                                                mx[:, q, :].unsqueeze(2).broadcast_to([P, NP * NCH, L]), ALU.subtract)\
                            .then_inc(sub_s, 1)
                    if live(j, k - 1, B):
                        q = (k - 1) % 2
                        wait(dve, t_hi, j, k)
                        nc.vector.tensor_tensor(pt_lo[:, q, :], turned, pt_hi[:, q, :], ALU.subtract).then_inc(t_lo, 1)
                    if live(j, k - 2, B):
                        q = k % 2
                        sums = ps[:, 6 + q, 0:NP * NCH * VW].rearrange("p (c n v) -> p c n v", c=NP, n=NCH)
                        wait(dve, o_up, j, k - 1)
                        nc.vector.reciprocal(rec[:], sums[:, :, :, 2 * D]).then_inc(small, 1)
                        many(dve, 1, j, k)
                        nc.vector.tensor_tensor(o[:], sums[:, :, :, 0:2 * D],
                                                rec[:].unsqueeze(3).broadcast_to([P, NP, NCH, 2 * D]), ALU.mult)\
                            .then_inc(small, 1)
                        many(dve, 2, j, k)
                        nc.vector.tensor_tensor(o[:, :, 0, :], o[:, :, 0, :], o[:, :, 1, :], ALU.add).then_inc(small, 1)
                        many(dve, 3, j, k)
                        nc.vector.tensor_tensor(o[:, :, 1, :], o[:, :, 0, :], own[:].unsqueeze(1).broadcast_to([P, NP, 2 * D]),
                                                ALU.mult).then_inc(small, 1)
                        many(dve, 4, j, k)
                        hi, lo = [t[:, bass.ds(j * 2 + (k - 2), 1), :, 0:2 * D].rearrange("p b c v -> p (b c) v")
                                  for t in (at_hi, at_lo)]
                        nc.vector.tensor_copy(hi, o[:, :, 1, :]).then_inc(small, 1)
                        many(dve, 5, j, k)
                        nc.vector.tensor_tensor(lo, o[:, :, 1, :], hi, ALU.subtract).then_inc(at_s, 1)

                def many(dve, n, j, k):
                    dve.wait_ge(small, j * 10 + (5 * (k - 2) + n))

                pipeline(dve, B, 2, step)

        g_up, mx_s, sub_s, exp_s, t_up, t_hi, t_lo, o_up, rec_s, row_s, w_up, w_out = S.sems.new(
            *(f"lc_{n}" for n in ("g_up", "max", "sub", "exp", "t_up", "t_hi", "t_lo", "o_up", "rec", "row", "w_up",
                                  "w_out")))
        with (nc.sbuf_tensor("lc_mx", [P, 2, H], F32) as mx,
              nc.sbuf_tensor("lc_z", [P, 2, 1024], F32) as z,
              nc.sbuf_tensor("lc_e", [P, 2, 1024], F32) as e,
              nc.sbuf_tensor("lc_thi", [P, 2, 1024], F16) as et_hi,
              nc.sbuf_tensor("lc_tlo", [P, 2, 1024], F16) as et_lo,
              nc.sbuf_tensor("lc_rec", [P, 2, NP, 2], F32) as rec,
              nc.sbuf_tensor("lc_row", [P, 2, P], F32) as row,
              nc.Block(no_gpsimd_drain=True) as block):
            turned = ps[:, 4:6, :].rearrange("p a n -> p (a n)")

            @block.tensor
            def _(pe):
                def step(j, k):
                    if live(j, k, NT):
                        wait(pe, sub_s, j, k - 1)
                        x = [t[:, bass.ds(j * (2 * P) + k * P, P)] for t in (S.x_hi, S.x_lo)]
                        for m in range(2):
                            last = products(nc, ps[:, 2 * (k % 2) + m, :], x, W_G[m])
                        last.then_inc(g_up, 1)
                    if live(j, k - 1, NT):
                        wait(pe, exp_s, j, k)
                        wait(pe, t_lo, j, k - 1)
                        for c in range(NP):
                            last = nc.tensor.transpose(ps[:, 4 + c // 4, c % 4 * P:(c % 4 + 1) * P],
                                                       e[:, (k - 1) % 2, c * P:(c + 1) * P], S.ident[:])
                        last.then_inc(t_up, 1)
                    if live(j, k - 2, NT):
                        wait(pe, t_lo, j, k - 1)
                        wait(pe, row_s, j, k - 2)
                        seq = j + (k - 2) // 2
                        for c in range(NP):
                            lhs = [t[:, k % 2, c * P:(c + 1) * P] for t in (et_hi, et_lo)]
                            rhs = [t[:, bass.ds(seq, 1), c].rearrange("p b v -> p (b v)") for t in (at_hi, at_lo)]
                            last = products(nc, ps[:, 6, c * VW:(c + 1) * VW], lhs, rhs)
                        last.then_inc(o_up, 1)
                    if live(j, k - 3, NT):
                        wait(pe, row_s, j, k - 2)
                        wait(pe, w_out, j, k - 3)
                        nc.tensor.transpose(ps[:, 7, 0:P], row[:, (k - 3) % 2, :], S.ident[:]).then_inc(w_up, 1)
                pipeline(pe, NT, 3, step)

            @block.scalar
            def _(act):
                def step(j, k):
                    if live(j, k, NT):
                        wait(act, sub_s, j, k + 1)
                        wait(act, t_up, j, k - 1)
                        nc.scalar.activation(e[:, k % 2, :], z[:, k % 2, :], ACT.Exp, scale=SC).then_inc(exp_s, 1)
                    if live(j, k - 1, NT):
                        wait(act, t_up, j, k)
                        wait(act, o_up, j, k - 2)
                        nc.scalar.activation(et_hi[:, (k - 1) % 2, :], turned, ACT.Copy).then_inc(t_hi, 1)
                    if live(j, k - 3, NT):
                        wait(act, w_up, j, k - 2)
                        nc.scalar.activation(wT[:, bass.ds(j * (2 * P) + (k - 3) * P, P)], ps[:, 7, 0:P], ACT.Copy)\
                            .then_inc(w_out, 1)
                pipeline(act, NT, 3, step)

            @block.vector
            def _(dve):
                def step(j, k):
                    if live(j, k, NT):
                        q = k % 2
                        wait(dve, g_up, j, k + 1)
                        g3 = ps[:, 2 * q:2 * q + 2, :].rearrange("p a (c n) -> p (a c) n", n=L)
                        nc.vector.tensor_reduce(mx[:, q, :], g3, AX.X, ALU.max).then_inc(mx_s, 1)
                        wait(dve, mx_s, j, k + 1)
                        wait(dve, exp_s, j, k - 1)
                        nc.vector.tensor_tensor(z[:, q, :].rearrange("p (c n) -> p c n", n=L), g3,
                                                mx[:, q, :].unsqueeze(2).broadcast_to([P, H, L]), ALU.subtract)\
                            .then_inc(sub_s, 1)
                    if live(j, k - 1, NT):
                        q = (k - 1) % 2
                        wait(dve, t_hi, j, k)
                        nc.vector.tensor_tensor(et_lo[:, q, :], turned, et_hi[:, q, :], ALU.subtract).then_inc(t_lo, 1)
                    if live(j, k - 2, NT):
                        q = k % 2
                        mix = ps[:, 6, 0:NP * VW].rearrange("p (c v) -> p c v", c=NP)
                        wait(dve, o_up, j, k - 1)
                        nc.vector.reciprocal(rec[:, q], mix[:, :, 2 * D:VW]).then_inc(rec_s, 1)
                        wait(dve, rec_s, j, k - 1)
                        wait(dve, w_up, j, k - 3)
                        nc.vector.tensor_tensor(row[:, q, :].rearrange("p (c h d) -> p c h d", c=NP, h=2),
                                                mix[:, :, 0:2 * D].rearrange("p c (h d) -> p c h d", h=2),
                                                rec[:, q].unsqueeze(3).broadcast_to([P, NP, 2, D]), ALU.mult)\
                            .then_inc(row_s, 1)
                pipeline(dve, NT, 2, step)

        wp_s, y_up = S.sems.new("ld_parts", "ld_y_up")
        with (nc.sbuf_tensor("ld_hi", [P, N], F16) as wt_hi,
              nc.sbuf_tensor("ld_lo", [P, N], F16) as wt_lo,
              nc.Block(no_gpsimd_drain=True) as block):

            @block.vector
            def _(dve):
                split_on(dve, wp_s, 1, wt_hi[:], wt_lo[:], wT[:]).then_inc(wp_s, 1)
                for n in range(NQ):
                    cut = slice(n * QW, (n + 1) * QW)
                    dve.wait_ge(y_up, n + 1)
                    nc.vector.tensor_tensor(S.rT[:, cut], S.xT[:, cut], ps[:, n, :], ALU.add)

            @block.tensor
            def _(pe):
                pe.wait_ge(wp_s, 2)
                for n in range(NQ):
                    cut = slice(n * QW, (n + 1) * QW)
                    products(nc, ps[:, n, :], W_P, (wt_hi[:, cut], wt_lo[:, cut])).then_inc(y_up, 1)


def l2_attn(nc, S, A):
    H, DK, DV = 4, 32, 64
    HV = H * DV
    TB = T // P
    PAIRS = 3 * P
    ps = S.psum
    WN = 2 * P + 2 * HV + H
    with ExitStack() as ctx:
        def sb(name, shape, dt):
            return ctx.enter_context(nc.sbuf_tensor(name, shape, dt))

        q_hi = sb("lg_qhi", [P, H, N], F16)
        q_lo = sb("lg_qlo", [P, H, N], F16)
        k_hi = sb("lg_khi", [P, N], F16)
        k_lo = sb("lg_klo", [P, N], F16)
        v_hi = sb("lg_vhi", [P, NT, HV], F16)
        v_lo = sb("lg_vlo", [P, NT, HV], F16)
        gate = sb("lg_gate", [P, NT, HV], F32)
        og = sb("lg_og", [P, NT, HV], F32)
        sq = sb("lg_sq", [P, 2, TB * HV], F32)
        ms = sb("lg_ms", [P, NT, H], F32)
        g_hi = sb("lg_ghi", [P, B, TB, H], F16)
        g_lo = sb("lg_glo", [P, B, TB, H], F16)
        G = sb("lg_G", [P, TB, B, H], F32)
        wo = sb("lg_wo", [P, 2, P], F32)
        wo_hi = sb("lg_wohi", [P, 2, P], F16)
        wo_lo = sb("lg_wolo", [P, 2, P], F16)
        norm_w = sb("lg_norm", [P, 1], F32)
        tri = sb("lg_tri", [P, 2 * PAIRS], F16)
        mask = sb("lg_mask", [P, PAIRS], BF16)

        got, zero_s, parts_s, qk_up, qk_hi, qk_lo, v_up, v_high, v_done, z_s, e_s, log_s, cum_s = S.sems.new(
            *(f"lg_{n}" for n in ("got", "zero", "parts", "qk_up", "qk_hi", "qk_lo", "v_up", "v_high", "v_done", "z",
                                  "e", "log", "cum")))
        with (nc.sbuf_tensor("lg_w", [P, WN], F32) as w,
              nc.sbuf_tensor("lg_whi", [P, WN], F16) as w_hi,
              nc.sbuf_tensor("lg_wlo", [P, WN], F16) as w_lo,
              nc.sbuf_tensor("lg_bgk", [P, H], F32) as bgk,
              nc.sbuf_tensor("lg_z", [P, NT, H], F32) as z,
              nc.sbuf_tensor("lg_abs", [P, NT, H], F32) as za,
              nc.sbuf_tensor("lg_e", [P, NT, H], F32) as e,
              nc.sbuf_tensor("lg_l", [P, NT, H], F32) as lg,
              nc.Block(no_gpsimd_drain=True) as block):

            def cols(a, n):
                return w_hi[:, a:a + n], w_lo[:, a:a + n]

            W_Q, W_K, W_V, W_G = cols(0, P), cols(P, P), cols(2 * P, HV + H), cols(2 * P + HV + H, HV)

            @block.sync
            def _(sp):
                for dst, src in ((w[:], "lg_w"), (bgk[:], "lg_bgk"), (wo[:], "lg_wo"), (norm_w[:], "lg_norm"),
                                 (tri[:], "lg_tri"), (mask[:], "lg_mask")):
                    sp.dma_start(dst, A[src]).then_inc(got, 16)
                sp.wait_ge(got, 96)

            @block.gpsimd
            def _(pool):
                nc.gpsimd.memset(q_hi[:].rearrange("p h n -> p (h n)").bitcast(F32), 0.0).then_inc(zero_s, 1)
                nc.gpsimd.memset(q_lo[:].rearrange("p h n -> p (h n)").bitcast(F32), 0.0).then_inc(zero_s, 1)

            @block.tensor
            def _(pe):
                pe.wait_ge(parts_s, 2)
                for n in range(NQ):
                    x = [t[:, n * QW:(n + 1) * QW] for t in (S.x_hi, S.x_lo)]
                    products(nc, ps[:, n, :], W_Q, x)
                    products(nc, ps[:, 4 + n, :], W_K, x).then_inc(qk_up, 1)
                for i in range(NT):
                    x = [t[:, i * P:(i + 1) * P] for t in (S.x_hi, S.x_lo)]
                    a = 2 * (i % 4)
                    if i < 4:
                        pe.wait_ge(qk_lo, NQ)
                    else:
                        pe.wait_ge(v_done, i - 3)
                    products(nc, ps[:, a, 0:HV + H], x, W_V)
                    products(nc, ps[:, a + 1, 0:HV], x, W_G).then_inc(v_up, 1)
                pe.wait_ge(log_s, 6)
                g2 = [t[:].rearrange("p b a h -> p a b h") for t in (g_hi, g_lo)]
                for a in range(TB):
                    out = ps[:, a, 0:B * H].rearrange("p (b h) -> p b h", b=B)
                    terms = [(tri[:, 0:P], a)] + [(tri[:, P:2 * P], 0)] * a
                    for m, (lhs, src) in enumerate(terms):
                        for n, g in enumerate(g2):
                            last = nc.tensor.matmul(out, lhs, g[:, src], start=(m == n == 0),
                                                    stop=(m == len(terms) - 1 and n == 1))
                last.then_inc(cum_s, 1)

            @block.scalar
            def _(act):
                act.wait_ge(zero_s, 2)
                for n in range(NQ):
                    cut = slice(n * QW, (n + 1) * QW)
                    act.wait_ge(qk_up, n + 1)
                    for h in range(H):
                        r = slice(h * DK, (h + 1) * DK)
                        nc.scalar.activation(q_hi[r, h, cut], ps[r, n, :], ACT.Copy)
                    nc.scalar.activation(k_hi[:, cut], ps[:, 4 + n, :], ACT.Copy).then_inc(qk_hi, 1)
                for i in range(NT):
                    act.wait_ge(v_up, i + 1)
                    a = 2 * (i % 4)
                    nc.scalar.activation(v_hi[:, i, :], ps[:, a, 0:HV], ACT.Copy)
                    nc.scalar.activation(gate[:, i, :], ps[:, a + 1, 0:HV], ACT.Silu).then_inc(v_high, 1)
                act.wait_ge(z_s, 1)
                nc.scalar.activation(e[:], za[:], ACT.Exp).then_inc(e_s, 1)
                act.wait_ge(e_s, 1)
                nc.scalar.activation(lg[:], e[:], ACT.Ln, bias=S.one).then_inc(e_s, 1)

            @block.vector
            def _(dve):
                dve.wait_ge(got, 96)
                split_on(dve, parts_s, 1, w_hi[:], w_lo[:], w[:]).then_inc(parts_s, 1)
                nc.vector.tensor_scalar(wo[:], wo[:], norm_w[:, 0:1], None, ALU.mult).then_inc(log_s, 1)
                dve.wait_ge(log_s, 1)
                split_on(dve, log_s, 2, wo_hi[:], wo_lo[:], wo[:])
                for n in range(NQ):
                    cut = slice(n * QW, (n + 1) * QW)
                    dve.wait_ge(qk_hi, n + 1)
                    for h in range(H):
                        r = slice(h * DK, (h + 1) * DK)
                        nc.vector.tensor_tensor(q_lo[r, h, cut], ps[r, n, :], q_hi[r, h, cut], ALU.subtract)
                    nc.vector.tensor_tensor(k_lo[:, cut], ps[:, 4 + n, :], k_hi[:, cut], ALU.subtract).then_inc(qk_lo, 1)
                for i in range(NT):
                    a = 2 * (i % 4)
                    dve.wait_ge(v_high, i + 1)
                    nc.vector.tensor_tensor(z[:, i, :], ps[:, a, HV:HV + H], bgk[:], ALU.add)
                    nc.vector.tensor_tensor(v_lo[:, i, :], ps[:, a, 0:HV], v_hi[:, i, :], ALU.subtract).then_inc(v_done, 1)
                dve.wait_ge(v_done, NT)
                nc.vector.scalar_tensor_tensor(out=za[:], in0=z[:], scalar=-1.0, in1=z[:], op0=ALU.mult,
                                               op1=ALU.min).then_inc(z_s, 1)
                dve.wait_ge(z_s, 1)
                nc.vector.tensor_scalar(z[:], z[:], 0.0, None, ALU.min).then_inc(z_s, 1)
                dve.wait_ge(z_s, 2)
                dve.wait_ge(e_s, 2)
                nc.vector.tensor_tensor(z[:], z[:], lg[:], ALU.subtract).then_inc(log_s, 1)
                dve.wait_ge(log_s, 3)
                nc.vector.tensor_scalar(z[:], z[:], 1.0 / 16, None, ALU.mult).then_inc(log_s, 1)
                dve.wait_ge(log_s, 4)
                flat = [t[:].rearrange("p b a h -> p (b a) h") for t in (g_hi, g_lo)]
                split_on(dve, log_s, 5, flat[0], flat[1], z[:]).then_inc(log_s, 1)
                dve.wait_ge(cum_s, 1)
                for a in range(TB):
                    nc.vector.tensor_copy(G[:, a].rearrange("p b h -> p (b h)"), ps[:, a, 0:B * H])

        gs_up, dec_s, exp_s, at_s, hi_s, lo_s, o_up, sq_s, og_s = S.sems.new(
            *(f"lh_{n}" for n in ("gs_up", "dec", "exp", "at", "hi", "lo", "o_up", "sq", "og")))
        U = 2 * H
        with (nc.sbuf_tensor("lh_dec", [P, 2, PAIRS], F32) as dec,
              nc.sbuf_tensor("lh_d", [P, 2, PAIRS], F32) as d,
              nc.sbuf_tensor("lh_at", [P, 2, PAIRS], F32) as at,
              nc.sbuf_tensor("lh_athi", [P, 4, PAIRS], F16) as at_hi,
              nc.sbuf_tensor("lh_atlo", [P, 4, PAIRS], F16) as at_lo,
              nc.Block(no_gpsimd_drain=True) as block):

            @block.tensor
            def _(pe):
                def step(j, k):
                    if live(j, k, B * H):
                        seq, h = j * 2 + k // H, k % H
                        decay, score = ps[:, k % 2, 0:PAIRS], ps[:, 2 + k % 2, :]
                        wait(pe, at_s, j, k - 1, U)
                        nc.tensor.matmul(decay, S.identb[:], mask[:], start=True, stop=False, skip_group_check=True)
                        for a in range(TB):
                            for n, g in enumerate((g_hi, g_lo)):
                                col = g[:, bass.ds(seq, 1), a, h:h + 1].rearrange("p b h -> p (b h)").broadcast_to([P, P])
                                last = nc.tensor.matmul(decay[:, a * P:PAIRS], col,
                                                        tri[:, a * PAIRS + a * P:(a + 1) * PAIRS],
                                                        start=False, stop=(a == n == 1), skip_group_check=True)
                        for a in range(TB):
                            lhs = [t[:, bass.ds(seq * T + a * P, P)] for t in (k_hi, k_lo)]
                            rhs = [t[:, h, bass.ds(seq * T + a * P, T - a * P)] for t in (q_hi, q_lo)]
                            last = products(nc, score[:, a * T:a * T + T - a * P], lhs, rhs)
                        last.then_inc(gs_up, 1)
                    if live(j, k - 3, B * H):
                        seq, h, c = j * 2 + (k - 3) // H, (k - 3) % H, (k - 3) % 4
                        wait(pe, lo_s, j, k - 2, U)
                        if h == 0:
                            wait(pe, og_s, j, (k - 3) // H - 1, 2)
                        bank = ps[:, 4 + ((k - 3) // H) % 2, :]
                        for a, terms in enumerate((((0, 0),), ((1, 0), (2, 1)))):
                            out = bank[:, (a * H + h) * DV:(a * H + h + 1) * DV]
                            for m, (pair, src) in enumerate(terms):
                                lhs = [t[:, c, pair * P:(pair + 1) * P] for t in (at_hi, at_lo)]
                                rhs = [t[:, bass.ds(seq * TB + src, 1), h * DV:(h + 1) * DV]
                                       .rearrange("p i v -> p (i v)") for t in (v_hi, v_lo)]
                                last = products(nc, out, lhs, rhs, first=(m == 0), last=(m == len(terms) - 1))
                        last.then_inc(o_up, 1)
                pipeline(pe, B * H, 3, step, U)

            @block.scalar
            def _(act):
                def step(j, k):
                    if live(j, k, B * H):
                        wait(act, dec_s, j, k + 1, U)
                        wait(act, at_s, j, k - 1, U)
                        nc.scalar.activation(d[:, k % 2, :], dec[:, k % 2, :], ACT.Exp).then_inc(exp_s, 1)
                    if live(j, k - 1, B * H):
                        wait(act, at_s, j, k, U)
                        wait(act, o_up, j, k - 4, U)
                        nc.scalar.activation(at_hi[:, (k - 1) % 4, :], at[:, (k - 1) % 2, :], ACT.Copy).then_inc(hi_s, 1)
                    if k % H == 3 and live(j, k - 4, B * H):
                        b = (k - 4) // H
                        wait(act, o_up, j, H * (b + 1), U)
                        wait(act, og_s, j, b - 1, 2)
                        nc.scalar.activation(sq[:, b % 2, :], ps[:, 4 + b % 2, :], ACT.Square).then_inc(sq_s, 1)
                pipeline(act, B * H, 4, step, U)

            @block.vector
            def _(dve):
                def step(j, k):
                    if live(j, k, B * H):
                        wait(dve, gs_up, j, k + 1, U)
                        wait(dve, exp_s, j, k - 1, U)
                        seq, h = j * 2 + k // H, k % H
                        for a, (lo, hi) in enumerate(((0, T), (T, PAIRS))):
                            mine = G[:, a, bass.ds(seq, 1), h:h + 1].rearrange("p b h -> p (b h)")
                            last = nc.vector.tensor_scalar(dec[:, k % 2, lo:hi], ps[:, k % 2, lo:hi], mine, 0.0,
                                                           ALU.subtract, ALU.min)
                        last.then_inc(dec_s, 1)
                    if live(j, k - 1, B * H):
                        c = (k - 1) % 2
                        wait(dve, exp_s, j, k, U)
                        wait(dve, lo_s, j, k - 2, U)
                        nc.vector.scalar_tensor_tensor(out=at[:, c, :], in0=ps[:, 2 + c, 0:PAIRS], scalar=DK ** -0.5,
                                                       in1=d[:, c, :], op0=ALU.mult, op1=ALU.mult).then_inc(at_s, 1)
                    if live(j, k - 2, B * H):
                        wait(dve, hi_s, j, k - 1, U)
                        nc.vector.tensor_tensor(at_lo[:, (k - 2) % 4, :], at[:, k % 2, :], at_hi[:, (k - 2) % 4, :],
                                                ALU.subtract).then_inc(lo_s, 1)
                    if k % H == 3 and live(j, k - 4, B * H):
                        b = (k - 4) // H
                        wait(dve, sq_s, j, b + 1, 2)
                        two = bass.ds(j * (2 * TB) + b * TB, TB)
                        nc.vector.tensor_reduce(ms[:, two, :].rearrange("p i h -> p (i h)"),
                                                sq[:, b % 2, :].rearrange("p (i v) -> p i v", v=DV), AX.X, ALU.add)
                        nc.vector.tensor_tensor(og[:, two, :].rearrange("p i v -> p (i v)"), ps[:, 4 + b % 2, :],
                                                gate[:, two, :].rearrange("p i v -> p (i v)"), ALU.mult).then_inc(og_s, 1)
                pipeline(dve, B * H, 4, step, U)

        sd_s, rs_s, on_s, t_up, t_hi, t_lo, y_up = S.sems.new(
            *(f"li_{n}" for n in ("std", "rstd", "on", "t_up", "t_hi", "t_lo", "y_up")))
        with (nc.sbuf_tensor("li_sd", [P, NT, H], F32) as sd,
              nc.sbuf_tensor("li_rs", [P, NT, H], F32) as rs,
              nc.sbuf_tensor("li_hi", [P, NQ, 2, QW], F16) as on_hi,
              nc.sbuf_tensor("li_lo", [P, NQ, 2, QW], F16) as on_lo,
              nc.Block(no_gpsimd_drain=True) as block):

            @block.scalar
            def _(act):
                nc.scalar.activation(sd[:], ms[:], ACT.Sqrt, bias=S.eps_ap(1e-5), scale=1.0 / DV).then_inc(sd_s, 1)
                for n in range(NQ):
                    act.wait_ge(t_up, n + 1)
                    nc.scalar.activation(on_hi[:, n], ps[:, 2 * (n % 2):2 * (n % 2) + 2, :], ACT.Copy).then_inc(t_hi, 1)

            @block.vector
            def _(dve):
                dve.wait_ge(sd_s, 1)
                nc.vector.reciprocal(rs[:], sd[:]).then_inc(rs_s, 1)
                dve.wait_ge(rs_s, 1)
                for n in range(NQ):
                    four = slice(4 * n, 4 * n + 4)
                    o4 = og[:, four, :].rearrange("p i (h v) -> p (i h) v", h=H)
                    nc.vector.tensor_tensor(o4, o4, rs[:, four, :].rearrange("p i h -> p (i h)").unsqueeze(2)
                                            .broadcast_to([P, 4 * H, DV]), ALU.mult).then_inc(on_s, 1)
                for n in range(NQ):
                    dve.wait_ge(t_hi, n + 1)
                    nc.vector.tensor_tensor(on_lo[:, n], ps[:, 2 * (n % 2):2 * (n % 2) + 2, :], on_hi[:, n],
                                            ALU.subtract).then_inc(t_lo, 1)
                for n in range(NQ):
                    cut = slice(n * QW, (n + 1) * QW)
                    dve.wait_ge(y_up, n + 1)
                    nc.vector.tensor_tensor(S.rT[:, cut], S.xT[:, cut], ps[:, 4 + n, :], ALU.add)

            @block.tensor
            def _(pe):
                for n in range(NQ):
                    pe.wait_ge(on_s, n + 1)
                    if n >= 2:
                        pe.wait_ge(t_lo, n - 1)
                    for m in range(2):
                        for i in range(4):
                            last = nc.tensor.transpose(ps[:, 2 * (n % 2) + m, i * P:(i + 1) * P],
                                                       og[:, 4 * n + i, m * P:(m + 1) * P], S.ident[:])
                    last.then_inc(t_up, 1)
                for n in range(NQ):
                    pe.wait_ge(t_lo, n + 1)
                    for m in range(2):
                        last = products(nc, ps[:, 4 + n, :], (wo_hi[:, m, :], wo_lo[:, m, :]),
                                        (on_hi[:, n, m, :], on_lo[:, n, m, :]), first=(m == 0), last=(m == 1))
                    last.then_inc(y_up, 1)


def l3_attn(nc, S, A):
    DEPTH = A["lj_w"].shape[0]
    H, DH, FF = 8, 16, 4
    ps = S.psum
    WN = (4 + 2 * FF) * P
    with ExitStack() as ctx:
        def sb(name, shape, dt):
            return ctx.enter_context(nc.sbuf_tensor(name, shape, dt))

        x0 = sb("lj_x0", [P, N], F32)
        cols = sb("lj_cols", [P, DEPTH, 5], F32)
        own = sb("lj_own", [P, P], F32)
        w = sb("lj_w", [P, WN], F32)
        w_hi, w_lo = sb("lj_whi", [P, WN], F16), sb("lj_wlo", [P, WN], F16)
        W = [(w_hi[:, n * P:(n + 1) * P], w_lo[:, n * P:(n + 1) * P]) for n in range(4 + 2 * FF)]
        W_Q, W_K, W_V = W[:3]
        W_O = w[:, 3 * P:4 * P]

        got = S.sems.new("lj_got")
        with nc.Block(no_gpsimd_drain=True) as block:

            @block.sync
            def _(sp):
                sp.dma_start(cols[:], A["lj_cols"]).then_inc(got, 16)
                sp.dma_start(own[:], A["lj_own"]).then_inc(got, 16)
                sp.wait_ge(got, 32)

            @block.vector
            def _(dve):
                nc.vector.tensor_copy(x0[:], S.xT[:])

        first = len(S.sems.held)
        with nc.Fori(0, DEPTH) as layer:
            def column(n):
                return cols[:, bass.ds(layer, 1), n:n + 1].rearrange("p l c -> p (l c)")

            w_got, w_high = S.sems.new("lj_w_got", "lj_w_high")

            def load_weights(sp):
                sp.dma_start(w[:], A["lj_w"][bass.ds(layer, 1)].rearrange("l p n -> p (l n)")).then_inc(w_got, 16)
                sp.wait_ge(w_got, 16)

            def split_weights(pool):
                pool.wait_ge(w_got, 16)
                nc.gpsimd.tensor_copy(w_hi[:], w[:]).then_inc(w_high, 1)
                pool.wait_ge(w_high, 1)
                nc.gpsimd.tensor_tensor(w_lo[:], w[:], w_hi[:], ALU.subtract).then_inc(w_high, 1)
                pool.wait_ge(w_high, 2)

            layernorm_phase(nc, S, S.xT, S.rT, gain=column(0), shift=column(1), sync=load_weights, pool=split_weights)
            linear_attention(nc, S, W_Q, W_K, W_V, W_O, own, column(2), H, DH)
            layernorm_phase(nc, S, S.xT, S.rT, gain=column(3), shift=column(4))
            leaky_network(nc, S, W[4:4 + FF], W[4 + FF:])
            S.sems.clear(first)

        with nc.Block(no_gpsimd_drain=True) as block:

            @block.vector
            def _(dve):
                nc.vector.tensor_tensor(S.rT[:], S.xT[:], x0[:], ALU.add)


def linear_attention(nc, S, W_Q, W_K, W_V, W_O, own, b_o, H, DH):
    ps = S.psum
    k_up, k_max, k_exp, q_up, q_max, q_sub, q_exp, q_sum, q_rec, q_on, v_up, v_on = S.sems.new(
        *(f"lk_{n}" for n in ("k_up", "k_max", "k_exp", "q_up", "q_max", "q_sub", "q_exp", "q_sum", "q_rec", "q_on",
                              "v_up", "v_on")))
    kt_up, kt_on, c_up, c_on, qt_up, qt_on, w_up, k_rec, w_on, y_up = S.sems.new(
        *(f"ll_{n}" for n in ("kt_up", "kt_on", "c_up", "c_on", "qt_up", "qt_on", "w_up", "k_rec", "w_on", "y_up")))
    TB = T // P
    with ExitStack() as ctx:
        def sb(name, shape, dt):
            return ctx.enter_context(nc.sbuf_tensor(name, shape, dt))

        ke, q = sb("lk_ke", [P, N], F32), sb("lk_q", [P, NT * H, DH], F32)
        neg_max, k_sum, rec = sb("lk_nm", [P, B], F32), sb("lk_ks", [P, B], F32), sb("lk_rec", [P, B], F32)
        qm, qs, qr = sb("lk_qm", [P, NT * H], F32), sb("lk_qs", [P, NT * H], F32), sb("lk_qr", [P, NT * H], F32)
        v, kr, qt = sb("lk_v", [P, N], F32), sb("lk_kr", [P, N], F32), sb("lk_qt", [P, N], F32)
        c, cw = sb("lk_c", [P, B * P], F32), sb("lk_cw", [P, B * P], F32)
        block = ctx.enter_context(nc.Block(no_gpsimd_drain=True))
        x = (S.x_hi, S.x_lo)

        def cut(pair, n, width=QW):
            return tuple(t[:, n * width:(n + 1) * width] for t in pair)

        @block.tensor
        def _(pe):
            for n in range(NQ):
                products(nc, ps[:, n, :], W_K, cut(x, n)).then_inc(k_up, 1)
            for i in range(NT):
                last = products(nc, ps[:, 4 + i // 4, i % 4 * P:(i % 4 + 1) * P], cut(x, i, P), W_Q)
                if i % 4 == 3:
                    last.then_inc(q_up, 1)
            for i in range(NT):
                if i % 4 == 0:
                    pe.wait_ge(k_exp, 2 * (i // 4) + 2)
                last = products(nc, ps[:, i // 4, i % 4 * P:(i % 4 + 1) * P], cut(x, i, P), W_V)
                if i % 4 == 3:
                    last.then_inc(v_up, 1)
            for i in range(NT):
                if i % 4 == 0:
                    pe.wait_ge(q_sub, i // 4 + 1)
                last = nc.tensor.transpose(ps[:, 4 + i // 4, i % 4 * P:(i % 4 + 1) * P], ke[:, i * P:(i + 1) * P], S.ident[:])
                if i % 4 == 3:
                    last.then_inc(kt_up, 1)
            for b in range(B):
                if b == 0:
                    pe.wait_ge(v_on, NQ)
                if b % 2 == 0:
                    pe.wait_ge(kt_on, b // 2 + 1)
                for a in range(TB):
                    rows = slice((TB * b + a) * P, (TB * b + a + 1) * P)
                    last = nc.tensor.matmul(ps[:, b // 4, b % 4 * P:(b % 4 + 1) * P], v[:, rows], kr[:, rows],
                                            start=(a == 0), stop=(a == TB - 1))
                if b % 4 == 3:
                    last.then_inc(c_up, 1)
            for i in range(NT):
                if i % 4 == 0:
                    pe.wait_ge(q_on, i // 4 + 1)
                last = nc.tensor.transpose(ps[:, 4 + i // 4, i % 4 * P:(i % 4 + 1) * P],
                                           q[:, i * H:(i + 1) * H, :].rearrange("p h d -> p (h d)"), S.ident[:])
                if i % 4 == 3:
                    last.then_inc(qt_up, 1)
            for b in range(B):
                pe.wait_ge(c_on, b // 4 + 1)
                last = nc.tensor.matmul(ps[:, 2 + b // 4, b % 4 * P:(b % 4 + 1) * P], c[:, b * P:(b + 1) * P], W_O)
                if b % 4 == 3:
                    last.then_inc(w_up, 1)
            for b in range(B):
                if b % 4 == 0:
                    pe.wait_ge(w_on, b // 4 + 1)
                if b % 2 == 0:
                    pe.wait_ge(qt_on, b // 2 + 1)
                last = nc.tensor.matmul(ps[:, 4 + b // 2, b % 2 * T:(b % 2 + 1) * T], cw[:, b * P:(b + 1) * P],
                                        qt[:, b * T:(b + 1) * T])
                if b % 2:
                    last.then_inc(y_up, 1)

        @block.scalar
        def _(act):
            for b in range(B):
                act.wait_ge(k_max, b // 2 + 1)
                nc.scalar.activation(ke[:, b * T:(b + 1) * T], ps[:, b // 2, b % 2 * T:(b % 2 + 1) * T], ACT.Exp,
                                     bias=neg_max[:, b:b + 1], accum_out=k_sum[:, b:b + 1]).then_inc(k_exp, 1)
            for n in range(NQ):
                g = slice(n * 4 * H, (n + 1) * 4 * H)
                act.wait_ge(q_sub, n + 1)
                nc.scalar.activation(q[:, g, :], q[:, g, :], ACT.Exp).then_inc(q_exp, 1)
            for n in range(NQ):
                act.wait_ge(v_up, n + 1)
                nc.scalar.activation(v[:, n * QW:(n + 1) * QW], ps[:, n, :], ACT.Copy).then_inc(v_on, 1)
            for n in range(NQ):
                act.wait_ge(kt_up, n + 1)
                nc.scalar.activation(kr[:, n * QW:(n + 1) * QW], ps[:, 4 + n, :], ACT.Copy).then_inc(kt_on, 1)
            for n in range(NQ):
                act.wait_ge(qt_up, n + 1)
                nc.scalar.activation(qt[:, n * QW:(n + 1) * QW], ps[:, 4 + n, :], ACT.Copy).then_inc(qt_on, 1)

        @block.vector
        def _(dve):
            for n in range(NQ):
                dve.wait_ge(k_up, n + 1)
                nc.vector.tensor_reduce(neg_max[:, 2 * n:2 * n + 2], ps[:, n, :].rearrange("p (b t) -> p b t", b=2), AX.X,
                                        ALU.max, negate=True).then_inc(k_max, 1)
            for n in range(NQ):
                g = slice(n * 4 * H, (n + 1) * 4 * H)
                rows = ps[:, 4 + n, :].rearrange("p (g d) -> p g d", d=DH)
                dve.wait_ge(q_up, n + 1)
                nc.vector.tensor_reduce(qm[:, g], rows, AX.X, ALU.max).then_inc(q_max, 1)
                dve.wait_ge(q_max, n + 1)
                nc.vector.tensor_tensor(q[:, g, :], rows, qm[:, g].unsqueeze(2).broadcast_to([P, 4 * H, DH]), ALU.subtract)\
                    .then_inc(q_sub, 1)
            dve.wait_ge(q_exp, NQ)
            nc.vector.tensor_reduce(qs[:], q[:], AX.X, ALU.add).then_inc(q_sum, 1)
            dve.wait_ge(q_sum, 1)
            nc.vector.reciprocal(qr[:], qs[:]).then_inc(q_rec, 1)
            dve.wait_ge(q_rec, 1)
            for n in range(NQ):
                g = slice(n * 4 * H, (n + 1) * 4 * H)
                nc.vector.tensor_tensor(q[:, g, :], q[:, g, :], qr[:, g].unsqueeze(2).broadcast_to([P, 4 * H, DH]),
                                        ALU.mult).then_inc(q_on, 1)
            dve.wait_ge(k_exp, B)
            nc.vector.reciprocal(rec[:], k_sum[:]).then_inc(k_rec, 1)
            for m in range(2):
                dve.wait_ge(c_up, m + 1)
                nc.vector.tensor_tensor(c[:, m * QW:(m + 1) * QW].rearrange("p (b d) -> p b d", b=4),
                                        ps[:, m, :].rearrange("p (b d) -> p b d", b=4),
                                        own[:].unsqueeze(1).broadcast_to([P, 4, P]), ALU.mult).then_inc(c_on, 1)
            dve.wait_ge(k_rec, 1)
            for m in range(2):
                dve.wait_ge(w_up, m + 1)
                nc.vector.tensor_tensor(cw[:, m * QW:(m + 1) * QW].rearrange("p (b d) -> p b d", b=4),
                                               ps[:, 2 + m, :].rearrange("p (b d) -> p b d", b=4),
                                               rec[:, 4 * m:4 * m + 4].unsqueeze(2).broadcast_to([P, 4, P]), ALU.mult).then_inc(w_on, 1)
            for n in range(NQ):
                run = slice(n * QW, (n + 1) * QW)
                dve.wait_ge(y_up, n + 1)
                nc.vector.scalar_tensor_tensor(out=S.xT[:, run], in0=ps[:, 4 + n, :], scalar=b_o, in1=S.xT[:, run],
                                               op0=ALU.add, op1=ALU.add)


def leaky_network(nc, S, W1, W2):
    ps = S.psum
    FF = len(W1)
    M = NQ * FF
    LAG = 3
    up, slope_s, leaky_s, hi_s, lo_s, down_s = S.sems.new(
        *(f"lm_{n}" for n in ("up", "slope", "leaky", "hi", "lo", "down")))
    with (nc.sbuf_tensor("lm_slope", [P, 2, QW], F32) as slope,
          nc.sbuf_tensor("lm_h", [P, 4, QW], F32) as h,
          nc.sbuf_tensor("lm_hhi", [P, 4, QW], F16) as h_hi,
          nc.sbuf_tensor("lm_hlo", [P, 4, QW], F16) as h_lo,
          nc.Block(no_gpsimd_drain=True) as block):

        @block.tensor
        def _(pe):
            for k in range(M + LAG):
                if k < M:
                    cut = slice(k // FF * QW, (k // FF + 1) * QW)
                    if k >= 4:
                        pe.wait_ge(leaky_s, k - 3)
                    products(nc, ps[:, 4 + k % 4, :], W1[k % FF], (S.x_hi[:, cut], S.x_lo[:, cut])).then_inc(up, 1)
                if k >= LAG:
                    i = k - LAG
                    pe.wait_ge(lo_s, i + 1)
                    last = products(nc, ps[:, i // FF, :], W2[i % FF], (h_hi[:, i % 4, :], h_lo[:, i % 4, :]),
                                    first=(i % FF == 0), last=(i % FF == FF - 1))
                    last.then_inc(down_s, 1)

        @block.scalar
        def _(act):
            for k in range(M + 1):
                if k < M:
                    act.wait_ge(up, k + 1)
                    if k >= 2:
                        act.wait_ge(leaky_s, k - 1)
                    nc.scalar.activation(slope[:, k % 2, :], ps[:, 4 + k % 4, :], ACT.Copy, scale=0.01).then_inc(slope_s, 1)
                if k >= 1:
                    i = k - 1
                    act.wait_ge(leaky_s, i + 1)
                    if i >= 4:
                        act.wait_ge(down_s, i - 3)
                    nc.scalar.activation(h_hi[:, i % 4, :], h[:, i % 4, :], ACT.Copy).then_inc(hi_s, 1)

        @block.vector
        def _(dve):
            for k in range(M + 1):
                if k < M:
                    dve.wait_ge(slope_s, k + 1)
                    if k >= 4:
                        dve.wait_ge(lo_s, k - 3)
                    nc.vector.tensor_tensor(h[:, k % 4, :], ps[:, 4 + k % 4, :], slope[:, k % 2, :], ALU.max)\
                        .then_inc(leaky_s, 1)
                if k >= 1:
                    i = k - 1
                    dve.wait_ge(hi_s, i + 1)
                    nc.vector.tensor_tensor(h_lo[:, i % 4, :], h[:, i % 4, :], h_hi[:, i % 4, :], ALU.subtract)\
                        .then_inc(lo_s, 1)
            for n in range(NQ):
                cut = slice(n * QW, (n + 1) * QW)
                dve.wait_ge(down_s, FF * (n + 1))
                nc.vector.tensor_tensor(S.xT[:, cut], S.xT[:, cut], ps[:, n, :], ALU.add)


def l3_ffn(nc, S, A):
    H, DH, E = 8, 16, 4
    HG, QT = H // 4, T // E
    TB = T // P
    SC = C ** -0.5
    ps = S.psum
    WN = (2 * HG + 2) * E * P
    UN = B * H
    R = 2 * H
    with ExitStack() as ctx:
        def sb(name, shape, dt):
            return ctx.enter_context(nc.sbuf_tensor(name, shape, dt))

        w = sb("lq_w", [P, WN], F32)
        w_hi, w_lo = sb("lq_whi", [P, WN], F16), sb("lq_wlo", [P, WN], F16)
        cols = sb("lq_cols", [P, 2 + 2 * HG + E], F32)
        v_b = sb("lq_vb", [P, P], F32)
        x2 = sb("lq_x2", [P, N], F32)
        q32, k32, v32 = (sb(f"lq_{n}32", [P, 2 * T], F32) for n in "qkv")
        q_hi, q_lo, k_hi, k_lo, v_hi, v_lo = (sb(f"lq_{n}", [P, 2, 2 * T], F16) for n in ("qhi", "qlo", "khi", "klo", "vhi", "vlo"))
        neg = sb("lq_neg", [P, 4, TB], F32)
        sums = sb("lq_sums", [P, 2, TB, H], F32)
        rec = sb("lq_rec", [P, TB, H], F32)
        e = sb("lq_e", [P, 2, TB * T], F32)
        p_hi, p_lo = sb("lq_phi", [P, 4, TB * T], F16), sb("lq_plo", [P, 4, TB * T], F16)
        rows = sb("lq_rows", [P, TB, P], F32)
        o_hi, o_lo = sb("lq_ohi", [P, T], F16), sb("lq_olo", [P, T], F16)

        w_got, w_s = S.sems.new("lq_got", "lq_w_parts")

        def load(sp):
            sp.dma_start(cols[:], A["lq_cols"]).then_inc(w_got, 16)
            sp.dma_start(w[:], A["lq_w"]).then_inc(w_got, 16)
            sp.dma_start(v_b[:], A["lq_vb"]).then_inc(w_got, 16)
            sp.wait_ge(w_got, 48)

        def split(pool):
            pool.wait_ge(w_got, 48)
            nc.gpsimd.tensor_copy(w_hi[:], w[:]).then_inc(w_s, 1)
            pool.wait_ge(w_s, 1)
            nc.gpsimd.tensor_tensor(w_lo[:], w[:], w_hi[:], ALU.subtract).then_inc(w_s, 1)
            pool.wait_ge(w_s, 2)

        with nc.Block(no_gpsimd_drain=True) as block:

            @block.sync
            def _(sp):
                load(sp)

            @block.gpsimd
            def _(pool):
                split(pool)

            @block.vector
            def _(dve):
                nc.vector.tensor_scalar(x2[:], S.xT[:], 2.0, None, ALU.mult)
                dve.wait_ge(w_got, 48)
                nc.vector.tensor_scalar(cols[:, 2:2 + HG], cols[:, 2:2 + HG], SC, None, ALU.mult)

        layernorm_phase(nc, S, S.xT, S.rT, gain=cols[:, 0:1], shift=cols[:, 1:2])

        def weight(kind, n):
            at = (kind * HG * E if kind < 2 else 2 * HG * E + (kind - 2) * E) + n
            return w_hi[:, at * P:(at + 1) * P], w_lo[:, at * P:(at + 1) * P]

        q_up, q_ev, k_up, k_ev, v_up, v_ev, parts_hi, parts, s_up, mx_s, exp_s, t_up, hi_s, lo_s, o_up, rec_s, rows_s, ot_up, \
            ot_hi, ot_lo, y_up, y_ev = S.sems.new(*(f"lq_{n}" for n in (
                "q_up", "q_ev", "k_up", "k_ev", "v_up", "v_ev", "parts_hi", "parts", "s_up", "max", "exp", "t_up", "hi",
                "lo", "o_up", "rec", "rows", "ot_up", "ot_hi", "ot_lo", "y_up", "y_ev")))
        pool_start = S.sems.new("lq_pool_start")
        block = ctx.enter_context(nc.Block(no_gpsimd_drain=True))

        def start(j, k):
            return j * (2 * T) + k * T

        @block.tensor
        def _(pe):
            def step(j, k):
                if k % H == 0 and live(j, k, UN):
                    b = k // H
                    x = [[t[:, bass.ds(start(j, b) + n * QT, QT)] for t in (S.x_hi, S.x_lo)] for n in range(E)]
                    wait(pe, v_ev, j, b)
                    for kind, sem in ((0, q_up), (1, k_up)):
                        if kind:
                            wait(pe, y_ev, j, b - 2)
                        for n in range(E):
                            for a in range(HG):
                                last = products(nc, ps[:, 6 + kind, a * T + n * QT:a * T + (n + 1) * QT],
                                                weight(kind, n * HG + a), x[n])
                        last.then_inc(sem, 1)
                    wait(pe, q_ev, j, b + 1)
                    for i in range(TB):
                        xt = [t[:, bass.ds(start(j, b) + i * P, P)] for t in (S.x_hi, S.x_lo)]
                        at = (2 * HG * E + 2 * i) * P
                        last = products(nc, ps[:, 6, i * T:(i + 1) * T], xt, (w_hi[:, at:at + 2 * P], w_lo[:, at:at + 2 * P]))
                    last.then_inc(v_up, 1)
                if live(j, k - 8, UN):
                    u = k - 8
                    b, a, r = u // H, u % H // 4, slice(u % 4 * 32, u % 4 * 32 + 32)
                    wait(pe, exp_s, j, u - 1, R)
                    if u % H == 0:
                        wait(pe, parts, j, b + 1)
                    for i in range(TB):
                        last = products(nc, ps[:, u % 2, i * T:(i + 1) * T],
                                        [t[r, b % 2, a * T + i * P:a * T + (i + 1) * P] for t in (q_hi, q_lo)],
                                        [t[r, b % 2, a * T:(a + 1) * T] for t in (k_hi, k_lo)])
                    last.then_inc(s_up, 1)
                if live(j, k - 9, UN):
                    u = k - 9
                    wait(pe, exp_s, j, u + 1, R)
                    wait(pe, lo_s, j, u - 1, R)
                    for c in range(TB):
                        for i in range(TB):
                            last = nc.tensor.transpose(ps[:, 2 + u % 2, c * T + i * P:c * T + (i + 1) * P],
                                                       e[:, u % 2, i * T + c * P:i * T + (c + 1) * P], S.ident[:])
                    last.then_inc(t_up, 1)
                if live(j, k - 11, UN):
                    u = k - 11
                    b, h = u // H, u % H
                    wait(pe, lo_s, j, u + 1, R)
                    if h == 0:
                        wait(pe, ot_lo, j, b - 1)
                    for i in range(TB):
                        for c in range(TB):
                            last = products(nc, ps[:, 4 + b % 2, i * P + h * DH:i * P + (h + 1) * DH],
                                            [t[:, u % 4, c * T + i * P:c * T + (i + 1) * P] for t in (p_hi, p_lo)],
                                            [t[:, b % 2, c * P + h * DH:c * P + (h + 1) * DH] for t in (v_hi, v_lo)],
                                            first=(c == 0), last=(c == TB - 1))
                    last.then_inc(o_up, 1)
                if k % H == 4 and live(j, k - 20, UN):
                    b = k // H - 2
                    wait(pe, rows_s, j, b + 1)
                    for i in range(TB):
                        last = nc.tensor.transpose(ps[:, 4 + b % 2, T + i * P:T + (i + 1) * P], rows[:, i, :], S.ident[:])
                    last.then_inc(ot_up, 1)
                if k % H == 6 and live(j, k - 22, UN):
                    b = k // H - 2
                    wait(pe, ot_lo, j, b + 1)
                    wait(pe, k_ev, j, b + 3 if not isinstance(j, int) else min(b + 3, B))
                    for n in range(E):
                        cut = slice(n * QT, (n + 1) * QT)
                        last = products(nc, ps[:, 7, cut], weight(3, n), (o_hi[:, cut], o_lo[:, cut]))
                    last.then_inc(y_up, 1)
            pipeline(pe, UN, 23, step, R, 2 * R)

        @block.scalar
        def _(act):
            def step(j, k):
                if live(j, k - 8, UN):
                    u = k - 8
                    b, h = u // H, u % H
                    wait(act, mx_s, j, u + 1, R)
                    wait(act, t_up, j, u - 1, R)
                    if h == 0:
                        wait(act, rows_s, j, b - 1)
                    for i in range(TB):
                        last = nc.scalar.activation(e[:, u % 2, i * T:(i + 1) * T], ps[:, u % 2, i * T:(i + 1) * T], ACT.Exp,
                                                    bias=neg[:, u % 4, i:i + 1], accum_out=sums[:, b % 2, i, h:h + 1])
                    last.then_inc(exp_s, 1)
                if live(j, k - 9, UN):
                    u = k - 9
                    wait(act, t_up, j, u + 1, R)
                    wait(act, o_up, j, u - 3, R)
                    nc.scalar.activation(p_hi[:, u % 4, :], ps[:, 2 + u % 2, :], ACT.Copy).then_inc(hi_s, 1)
                if k % H == 5 and live(j, k - 21, UN):
                    b = k // H - 2
                    wait(act, ot_up, j, b + 1)
                    wait(act, y_up, j, b)
                    nc.scalar.activation(o_hi[:], ps[:, 4 + b % 2, T:2 * T], ACT.Copy).then_inc(ot_hi, 1)
            pipeline(act, UN, 23, step, R, 2 * R)

        @block.gpsimd
        def _(pool):
            def step(j, k):
                if k % H == 0 and live(j, k, UN):
                    b = k // H
                    wait(pool, v_ev, j, b + 1)
                    wait(pool, o_up, j, H * (b - 1), R)
                    pool.sem_inc(pool_start, 1)
                    nc.gpsimd.tensor_copy(q_hi[:, b % 2, :], q32[:])
                    nc.gpsimd.tensor_copy(k_hi[:, b % 2, :], k32[:])
                    nc.gpsimd.tensor_copy(v_hi[:, b % 2, 0:2 * P], v32[:, 0:2 * P]).then_inc(parts_hi, 1)
            pipeline(pool, UN, 0, step, R, 2 * R)

        @block.vector
        def _(dve):
            def step(j, k):
                if k % H == 0 and live(j, k, UN):
                    b = k // H
                    wait(dve, parts, j, b)
                    wait(dve, q_up, j, b + 1)
                    for a in range(HG):
                        cut = slice(a * T, (a + 1) * T)
                        last = nc.vector.tensor_scalar(q32[:, cut], ps[:, 6, cut], SC, cols[:, 2 + a:3 + a], ALU.mult, ALU.add)
                    last.then_inc(q_ev, 1)
                    wait(dve, k_up, j, b + 1)
                    for a in range(HG):
                        cut = slice(a * T, (a + 1) * T)
                        last = nc.vector.tensor_scalar(k32[:, cut], ps[:, 7, cut], cols[:, 2 + HG + a:3 + HG + a], None, ALU.add)
                    last.then_inc(k_ev, 1)
                    wait(dve, v_up, j, b + 1)
                    for n in range(2):
                        r = slice(n * QT, (n + 1) * QT)
                        last = nc.vector.tensor_tensor(v32[r, :2 * P].rearrange("p (i d) -> p i d", i=TB),
                                                       ps[r, 6, :].rearrange("p (i m) -> p i m", i=TB)[:, :, n * P:(n + 1) * P],
                                                       v_b[r].unsqueeze(1).broadcast_to([QT, TB, P]), ALU.add)
                    last.then_inc(v_ev, 1)
                if k % H == 3 and live(j, k - 3, UN):
                    b = k // H
                    wait(dve, parts_hi, j, b + 1)
                    for lo, hi, full in ((q_lo, q_hi, q32), (k_lo, k_hi, k32), (v_lo, v_hi, v32)):
                        m = 2 * P if full is v32 else 2 * T
                        last = nc.vector.tensor_tensor(lo[:, b % 2, 0:m], full[:, 0:m], hi[:, b % 2, 0:m], ALU.subtract)
                    last.then_inc(parts, 1)
                if live(j, k - 8, UN):
                    u = k - 8
                    wait(dve, s_up, j, u + 1, R)
                    nc.vector.tensor_reduce(neg[:, u % 4, :], ps[:, u % 2, :].rearrange("p (i n) -> p i n", i=TB), AX.X,
                                            ALU.max, negate=True).then_inc(mx_s, 1)
                if live(j, k - 10, UN):
                    u = k - 10
                    wait(dve, hi_s, j, u + 1, R)
                    nc.vector.tensor_tensor(p_lo[:, u % 4, :], ps[:, 2 + u % 2, :], p_hi[:, u % 4, :], ALU.subtract)\
                        .then_inc(lo_s, 1)
                if k % H == 3 and live(j, k - 19, UN):
                    b = k // H - 2
                    wait(dve, o_up, j, H * (b + 1), R)
                    nc.vector.reciprocal(rec[:], sums[:, b % 2]).then_inc(rec_s, 1)
                    wait(dve, rec_s, j, b + 1)
                    wait(dve, ot_up, j, b)
                    nc.vector.tensor_tensor(rows[:].rearrange("p i (h d) -> p (i h) d", h=H),
                                            ps[:, 4 + b % 2, 0:T].rearrange("p (g d) -> p g d", d=DH),
                                            rec[:].rearrange("p i h -> p (i h)").unsqueeze(2).broadcast_to([P, TB * H, DH]),
                                            ALU.mult).then_inc(rows_s, 1)
                if k % H == 5 and live(j, k - 21, UN):
                    b = k // H - 2
                    wait(dve, ot_hi, j, b + 1)
                    nc.vector.tensor_tensor(o_lo[:], ps[:, 4 + b % 2, T:2 * T], o_hi[:], ALU.subtract).then_inc(ot_lo, 1)
                if k % H == 7 and live(j, k - 23, UN):
                    b = k // H - 2
                    wait(dve, y_up, j, b + 1)
                    for n in range(E):
                        at = bass.ds(start(j, b) + n * QT, QT)
                        c = 2 + 2 * HG + n
                        last = nc.vector.scalar_tensor_tensor(out=S.rT[:, at], in0=ps[:, 7, n * QT:(n + 1) * QT],
                                                              scalar=cols[:, c:c + 1], in1=x2[:, at], op0=ALU.add,
                                                              op1=ALU.add)
                    last.then_inc(y_ev, 1)
            pipeline(dve, UN, 24, step, R, 2 * R)


def build(nc, A, out):
    S = State()
    S.sems = Sems(nc)
    S.eps = [1e-5, 1e-4, 1.0]
    with (nc.psum_tensor("ps", [P, 8, 512], F32) as ps,
          nc.sbuf_tensor("xT", [P, N], F32) as xT,
          nc.sbuf_tensor("rT", [P, N], F32) as rT,
          nc.sbuf_tensor("x_hi", [P, N], F16) as x_hi,
          nc.sbuf_tensor("x_lo", [P, N], F16) as x_lo,
          nc.sbuf_tensor("ident", [P, P], F32) as ident,
          nc.sbuf_tensor("identb", [P, P], BF16) as identb,
          nc.sbuf_tensor("epsilons", [P, 3], F32) as epsilons):
        S.psum, S.xT, S.rT, S.ident, S.identb, S.epsilons = ps, xT, rT, ident, identb, epsilons
        S.x_hi, S.x_lo = x_hi, x_lo
        S.eps_ap = lambda e: epsilons[:, S.eps.index(e):S.eps.index(e) + 1]
        S.one = S.eps_ap(1.0)
        load_phase(nc, S, A)
        table = {'0': l0_attn, '1': l0_ffn, '2': l1_attn, '4': l2_attn, '6': l3_attn, '7': l3_ffn, '3': l1_ffn, '5': l2_ffn}
        S.shared = {'m1r': 2, 'm2r': 1}
        for k in STAGES:
            table[k](nc, S, A)
            layernorm_phase(nc, S, rT, xT, out=out if k == STAGES[-1] else None)
            if k != STAGES[-1]:
                S.sems.give_back()


def layout(I):
    bf16 = mybir.dt.np(BF16)
    L = {}
    f = np.float32
    L["c_ident"] = np.eye(P, dtype=f)
    L["c_identb"] = np.eye(P, dtype=bf16)
    L["L0_attn_tokens"] = I["L0_attn_tokens"]
    a = np.zeros((2, 64, 8, 2, 64), f)
    b = np.zeros((16, 8, 8, 2, 64), f)
    c = np.zeros((2, 64, 8, 16, 8), f)
    for h in range(16):
        a[h % 2, :, h // 2, h % 2, :] = I["L0_attn_a"][h]
        b[h, :, h // 2, h % 2, :] = I["L0_attn_b"][h]
        c[h % 2, :, h // 2, h, :] = I["L0_attn_c"][h]
    L["L0_attn_a"] = a.reshape(P, 8, P)
    L["L0_attn_b"] = b.reshape(P, 8, P)
    L["L0_attn_c"] = c.reshape(P, 8, P)
    L["L0_attn_w_out"] = I["L0_attn_w_out"].T
    L["L0_attn_cols"] = np.stack([I["L0_attn_norm_w"], I["L0_attn_skip"].reshape(-1), I["L0_attn_b_out"]], axis=1)
    w1 = I["L0_ffn_w1"].reshape(8, P, 2, P).transpose(0, 2, 1, 3).reshape(16, P, P)
    w2 = I["L0_ffn_w2"].reshape(16, P, P)
    L["m0_w"] = np.concatenate([w1, w2], axis=2)
    L["m0_router"] = I["L0_ffn_router_w"].T

    def ups(w):
        return w.reshape(-1, P, P).transpose(0, 2, 1)

    def downs(w):
        return w.transpose(0, 2, 1).reshape(-1, P, P)

    eg = np.concatenate([I["L1_ffn_eg_w"].reshape(-1, P), I["L1_ffn_sg_w"]])
    eu = np.concatenate([I["L1_ffn_eu_w"].reshape(-1, P), I["L1_ffn_su_w"]])
    sd = I["L1_ffn_sd_w"].reshape(P, 2, 64).transpose(1, 0, 2)
    ed = np.concatenate([I["L1_ffn_ed_w"], sd])
    L["m1_w"] = np.concatenate([ups(eg), ups(eu), downs(ed)], axis=2)
    L["m1_router"] = I["L1_ffn_gate_w"].T
    L["m1_bias"] = np.repeat(I["L1_ffn_gate_bias"][None], P, axis=0)
    z = np.zeros((64, P), f)
    eg = np.concatenate([I["L2_ffn_w_gate"].reshape(-1, P), I["L2_ffn_w_gate_shared"], z])
    ed = np.concatenate([I["L2_ffn_w_down"], I["L2_ffn_w_down_shared"][None], z.reshape(1, P, 64)])
    L["m2_w"] = np.concatenate([ups(eg), downs(ed)], axis=2)
    L["m2_router"] = I["L2_ffn_router_w"].T
    L["m2_bias"] = np.repeat(I["L2_ffn_expert_bias"][None], P, axis=0)
    e = np.arange(3 * GE)[:, None, None] % GE
    m = np.arange(P)[None, None, :]
    L["c_sel_halves"] = (e == np.arange(16)[None, :, None] // 2 + 0 * m).astype(bf16)
    L["c_sel_pairs"] = (e == 2 * np.arange(GE // 2)[None, :, None] + m // 64).astype(bf16)
    w_k = I["L1_attn_W_k"]
    turned = w_k.reshape(64, 2, P)[:, ::-1].reshape(P, P)
    q = np.zeros((16, 8, 8, 2, 64), f)
    lat = I["L1_attn_latent_queries"][0]
    for h in range(16):
        q[h, :, h // 2, h % 2, :] = lat[:, h, :].T
    L["la_w"] = np.concatenate([w_k.T, turned.T, I["L1_attn_W_v"].T, I["L1_attn_W_p"].T, I["L1_attn_W_g"].T,
                                q.reshape(P, 8 * P)], axis=1)
    steps = (np.arange(2)[:, None] * P + np.arange(64)).reshape(-1)
    inv = (1.0 / 10000.0 ** (np.arange(0, 8, 2, dtype=f) / 8)).astype(f)
    ang = inv[np.arange(P) % 8 // 2][:, None] * steps[None, :].astype(f)
    sign = np.where(np.arange(P) % 2, 1.0, -1.0).astype(f)[:, None]
    L["la_rope"] = np.stack([np.cos(ang), np.sin(ang) * sign], axis=1).astype(f)
    seen = np.arange(64)[None, :] <= np.arange(P)[:, None] % 64
    L["la_mask"] = np.tile(np.where(seen, 0.0, -1e30), (1, 8)).astype(bf16)
    pair = (np.arange(P)[:, None] // 64 == np.arange(16)[None, :] // 8)
    L["la_own"] = pair.astype(f)
    ones = np.zeros((P, 8, 8, 18), np.float16)
    ones[:, :, :, 16:18] = pair[:, None, None, ::8]
    L["la_ones_hi"] = ones
    L["la_zeros"] = np.zeros((P, 8, 8, 18), np.float16)
    L["lg_w"] = np.concatenate([I["L2_attn_Wq"], I["L2_attn_Wk"], I["L2_attn_Wv"], I["L2_attn_Wgk"], I["L2_attn_Wg"]], axis=1)
    L["lg_bgk"] = np.repeat(I["L2_attn_bgk"][None], P, axis=0)
    L["lg_wo"] = I["L2_attn_Wo"].reshape(2, P, P).transpose(1, 0, 2)
    L["lg_norm"] = np.tile(I["L2_attn_gnorm_w"], 2)[:, None]
    upto = np.triu(np.ones((P, P), np.float16))
    one, none = np.ones((P, P), np.float16), np.zeros((P, P), np.float16)
    L["lg_tri"] = np.concatenate([upto, one, one, none, upto, upto], axis=1)
    later = np.where(upto > 0, 0.0, -1e30).astype(bf16)
    L["lg_mask"] = np.concatenate([later, none.astype(bf16), later], axis=1)
    L["lj_w"] = np.concatenate([I["L3_attn_wq"], I["L3_attn_wk"], I["L3_attn_wv"], I["L3_attn_wo"], I["L3_attn_w1"]]
                               + [I["L3_attn_w2"][:, n * P:(n + 1) * P] for n in range(4)], axis=2)
    L["lj_cols"] = np.stack([I["L3_attn_" + n] for n in ("ln1_w", "ln1_b", "bo", "ln2_w", "ln2_b")], axis=2)\
        .transpose(1, 0, 2)
    L["lj_own"] = (np.arange(P)[:, None] // 16 == np.arange(P)[None, :] // 16).astype(f)

    def spread(w):
        out = np.zeros((len(w), 2, 4, 32), f)
        out[..., :16] = w.reshape(-1, 2, 4, 16)
        return out.reshape(-1, 2 * P)

    def first(w, n, both=False):
        out = np.zeros_like(w)
        m = P >> n
        out[:m, :m if both else None] = w[:m, :m if both else None]
        return out

    L["lq_w"] = np.concatenate([first(spread(I["L3_ffn_" + s].T), n) for s in ("q_w", "k_w") for n in range(4)]
                               + [first(I["L3_ffn_v_w"].T, n) for n in range(4)]
                               + [first(I["L3_ffn_o_w"].T, n, True) for n in range(4)], axis=1)
    o_b = np.zeros((4, P), f)
    for n in range(4):
        o_b[n, :P >> n] = I["L3_ffn_o_b"][:P >> n]
    L["lq_cols"] = np.concatenate([I["L3_ffn_norm_w"][None], I["L3_ffn_norm_b"][None]]
                                  + [spread(I["L3_ffn_" + s][None]).reshape(2, P) for s in ("q_b", "k_b")] + [o_b]).T
    L["lq_vb"] = np.repeat(I["L3_ffn_v_b"][None], P, axis=0)
    return L


def kernel(**inputs):
    import concourse.bacc as _bacc
    from concourse.bass_utils import run_bass_kernel_spmd as _run

    I = {k: np.asarray(v) for k, v in inputs.items()}
    L = layout(I)
    nc = _bacc.Bacc("TRN2", target_bir_lowering=False, num_devices=1)
    arrays, A = {}, {}
    for name, a in L.items():
        a = np.ascontiguousarray(a)
        arrays[f"in_{name}"] = a
        A[name] = nc.dram_tensor(f"in_{name}", a.shape, mybir.dt.from_np(a.dtype), kind="ExternalInput").ap()
    out = nc.dram_tensor("out", (B, T, C), F32, kind="ExternalOutput").ap()
    build(nc, A, out)
    r = _run(nc, [arrays], core_ids=[0])
    return r.results[0]["out"]
```

```python
from contextlib import ExitStack

import numpy as np
import concourse.bass as bass
from concourse import mybir

STAGES = '01234567'

F32 = mybir.dt.float32
BF16 = mybir.dt.bfloat16
F16 = mybir.dt.float16
ALU = mybir.AluOpType
ACT = mybir.ActivationFunctionType
AX = mybir.AxisListType

B, T, C = 8, 256, 128
N = B * T
P = 128
NT = N // P
NQ = 4
QW = N // NQ
LN_EPS = 1e-5


class Sems:

    def __init__(self, nc):
        self.nc, self.n, self.held = nc, 0, []

    def new(self, *names):
        out = []
        for name in names:
            guard = self.nc.semaphore(f"{name}_{self.n}")
            out.append(guard.__enter__())
            self.held.append((guard, out[-1]))
            self.n += 1
        return out if len(out) > 1 else out[0]

    def clear(self, first=0):
        nums = sorted(s.num for _, s in self.held[first:])
        run = 0
        for n in range(1, len(nums) + 1):
            if n == len(nums) or nums[n] != nums[n - 1] + 1:
                self.nc.gpsimd.sem_clear(range(nums[run], nums[n - 1] + 1))
                run = n
        self.nc.all_engine_barrier()

    def give_back(self):
        self.clear()
        for guard, _ in self.held:
            guard.__exit__(None, None, None)
        self.held = []


class State:
    pass


def layernorm_phase(nc, S, src, dst, eps=LN_EPS, gain=None, shift=None, out=None, sync=None, pool=None):
    rows_in, stats_s, aggr_s, std_s, rstd_s, shift_s, normed_dve, normed_act, back, stored, turned, high_s = S.sems.new(
        "ln_rows_in", "ln_stats", "ln_aggr", "ln_std", "ln_rstd", "ln_shift", "ln_normed_dve", "ln_normed_act",
        "ln_back", "ln_stored", "ln_turned", "ln_high")
    G = NT // 4
    HT = NT // 2
    ps, ident = S.psum, S.ident
    with (nc.sbuf_tensor(f"ln_stat{S.sems.n}", [P, NT, 6], F32) as stats,
          nc.sbuf_tensor(f"ln_mv{S.sems.n}", [P, NT, 2], F32) as mv,
          nc.sbuf_tensor(f"ln_sd{S.sems.n}", [P, NT], F32) as std,
          nc.sbuf_tensor(f"ln_rs{S.sems.n}", [P, NT], F32) as rstd,
          nc.sbuf_tensor(f"ln_nm{S.sems.n}", [P, NT], F32) as shifts,
          nc.sbuf_tensor(f"ln_x{S.sems.n}", [P, NT, C], F32) as rows,
          nc.Block(no_gpsimd_drain=True) as block):

        def wait_normed(engine, g):
            engine.wait_ge(normed_act if g % 2 else normed_dve, g // 2 + 1)

        @block.tensor
        def _(pe):
            for g in range(G):
                for j in range(4):
                    i = 4 * g + j
                    last = nc.tensor.transpose(ps[:, g, j * C:(j + 1) * C], src[:, i * P:(i + 1) * P], ident[:])
                last.then_inc(rows_in, 1)
            if out is None:
                for g in range(G):
                    wait_normed(pe, g)
                    for j in range(4):
                        last = nc.tensor.transpose(ps[:, G + g, j * P:(j + 1) * P], rows[:, 4 * g + j, :], ident[:])
                    last.then_inc(back, 1)

        @block.vector
        def _(dve):
            def statistics(h):
                for g in (2 * h, 2 * h + 1):
                    dve.wait_ge(rows_in, g + 1)
                    for j in range(4):
                        last = nc.vector.bn_stats(stats[:, 4 * g + j, :], ps[:, g, j * C:(j + 1) * C])
                last.then_inc(stats_s, 1)

            def aggregate(h):
                dve.wait_ge(stats_s, h + 1)
                for i in range(h * HT, (h + 1) * HT):
                    last = nc.vector.bn_aggr(mv[:, i, :], stats[:, i, :])
                last.then_inc(aggr_s, 1)

            def scales(h):
                half, theirs = slice(h * HT, (h + 1) * HT), slice(h * HT + 4, (h + 1) * HT)
                dve.wait_ge(std_s, h + 1)
                nc.vector.reciprocal(rstd[:, half], std[:, half]).then_inc(rstd_s, 1)
                dve.wait_ge(rstd_s, h + 1)
                nc.vector.scalar_tensor_tensor(out=shifts[:, theirs], in0=mv[:, theirs, 0], scalar=-1.0,
                                               in1=rstd[:, theirs], op0=ALU.mult, op1=ALU.mult).then_inc(shift_s, 1)

            def normalise(g):
                for i in range(4 * g, 4 * g + 4):
                    last = nc.vector.tensor_scalar(rows[:, i, :], ps[:, g, i % 4 * C:(i % 4 + 1) * C], mv[:, i, 0:1],
                                                   rstd[:, i:i + 1], ALU.subtract, ALU.mult)
                last.then_inc(normed_dve, 1)

            statistics(0)
            aggregate(0)
            statistics(1)
            scales(0)
            aggregate(1)
            normalise(0)
            scales(1)
            normalise(2)
            if out is None:
                for g in range(G + 1):
                    if g < G:
                        cut = slice(g * QW, (g + 1) * QW)
                        dve.wait_ge(turned, g + 1)
                        nc.vector.tensor_copy(S.x_hi[:, cut], dst[:, cut]).then_inc(high_s, 1)
                    if g > 0:
                        cut = slice((g - 1) * QW, g * QW)
                        dve.wait_ge(high_s, g)
                        nc.vector.tensor_tensor(S.x_lo[:, cut], dst[:, cut], S.x_hi[:, cut], ALU.subtract)

        @block.scalar
        def _(act):
            for h in range(2):
                half = slice(h * HT, (h + 1) * HT)
                act.wait_ge(aggr_s, h + 1)
                nc.scalar.activation(std[:, half], mv[:, half, 1], ACT.Sqrt, bias=S.eps_ap(eps)).then_inc(std_s, 1)
                g = 2 * h + 1
                act.wait_ge(shift_s, h + 1)
                for i in range(4 * g, 4 * g + 4):
                    last = nc.scalar.activation(rows[:, i, :], ps[:, g, i % 4 * C:(i % 4 + 1) * C], ACT.Identity,
                                                bias=shifts[:, i:i + 1], scale=rstd[:, i:i + 1])
                last.then_inc(normed_act, 1)
            if out is None:
                for g in range(G):
                    act.wait_ge(back, g + 1)
                    q = dst[:, g * QW:(g + 1) * QW]
                    if gain is None:
                        nc.scalar.activation(q, ps[:, G + g, :], ACT.Copy).then_inc(turned, 1)
                    else:
                        nc.scalar.activation(q, ps[:, G + g, :], ACT.Identity, bias=shift, scale=gain).then_inc(turned, 1)

        @block.gpsimd
        def _(engine):
            if pool is not None:
                pool(engine)

        @block.sync
        def _(sp):
            if sync is not None:
                sync(sp)
            if out is not None:
                rows_out = out.rearrange("b t c -> (b t) c").rearrange("(i p) c -> p i c", p=P)
                for g in range(G):
                    wait_normed(sp, g)
                    sp.dma_start(rows_out[:, 4 * g:4 * g + 4, :], rows[:, 4 * g:4 * g + 4, :]).then_inc(stored, 16)
                sp.wait_ge(stored, 16 * G)


def load_phase(nc, S, A):
    got, rows_up = S.sems.new("load_got", "load_rows_up")
    ps = S.psum
    with (nc.sbuf_tensor("load_rows", [P, NT, C], F32) as rows,
          nc.Block(no_gpsimd_drain=True) as block):

        @block.sync
        def _(sp):
            sp.dma_start(S.ident[:], A["c_ident"]).then_inc(got, 16)
            sp.dma_start(S.identb[:], A["c_identb"]).then_inc(got, 16)
            sp.dma_start(rows[:], A["L0_attn_tokens"].rearrange("b t c -> (b t) c")
                         .rearrange("(i p) c -> p i c", p=P)).then_inc(got, 16)

        @block.vector
        def _(dve):
            for i, e in enumerate(S.eps):
                nc.vector.memset(S.epsilons[:, i:i + 1], e)

        @block.tensor
        def _(pe):
            pe.wait_ge(got, 48)
            for g in range(4):
                for j in range(4):
                    last = nc.tensor.transpose(ps[:, g, j * P:(j + 1) * P], rows[:, 4 * g + j, :], S.ident[:])
                last.then_inc(rows_up, 1)

        @block.scalar
        def _(act):
            for g in range(4):
                act.wait_ge(rows_up, g + 1)
                nc.scalar.activation(S.xT[:, g * QW:(g + 1) * QW], ps[:, g, :], ACT.Copy)


def l0_attn(nc, S, A):
    H, D, SS = 16, 8, 64
    NP = H // 2
    GP = NP // 2
    K = 16
    NCH = T // K
    ps = S.psum
    with (nc.sbuf_tensor("rn_a", [P, NP, P], F32) as a_raw,
          nc.sbuf_tensor("rn_at", [P, NP, P], F32) as a_t,
          nc.sbuf_tensor("rn_b", [P, NP, P], F32) as b_w,
          nc.sbuf_tensor("rn_c", [P, NP, P], F32) as c_w,
          nc.sbuf_tensor("rn_wo", [P, P], F32) as w_o,
          nc.sbuf_tensor("rn_cols", [P, 3], F32) as cols,
          nc.sbuf_tensor("rn_xn", [P, N], F32) as xnT,
          nc.sbuf_tensor("rn_o", [P, N], F32) as outsT,
          nc.sbuf_tensor("rn_s_hi", [P, 2 * K, NP * B], F16) as s_hi,
          nc.sbuf_tensor("rn_s_lo", [P, 2 * K, NP * B], F16) as s_lo,
          nc.sbuf_tensor("rn_s_full", [P, 2, 2, GP * B], F32) as s_full,
          nc.sbuf_tensor("rn_xn_hi", [P, N], F16) as xn_hi,
          nc.sbuf_tensor("rn_xn_lo", [P, N], F16) as xn_lo,
          nc.sbuf_tensor("rn_weights", [P, 6, NP, P], F16) as w_parts,
          nc.sbuf_tensor("rn_sq", [P, N], F32) as sq):
        at_hi, at_lo, b_hi, b_lo, c_hi, c_lo = [w_parts[:, n] for n in range(6)]
        norm_w, skip, b_out = cols[:, 0:1], cols[:, 1:2], cols[:, 2:3]

        got, pool_s, sq_s, sums, std_s, rstd_s, xr_s, rows_s = S.sems.new(
            "rms_got", "rnn_pool_parts", "rms_sq", "rms_sums", "rms_std", "rms_rstd", "rms_scaled", "rms_rows")
        with (nc.sbuf_tensor("rms_ms", [P, NT], F32) as ms,
              nc.sbuf_tensor("rms_sd", [P, NT], F32) as sd,
              nc.sbuf_tensor("rms_rs", [P, NT], F32) as rs,
              nc.sbuf_tensor("rms_rows", [P, NT, C], F32) as rows,
              nc.Block(no_gpsimd_drain=True) as block):

            @block.sync
            def _(sp):
                sp.dma_start(a_raw[:], A["L0_attn_a"]).then_inc(got, 16)
                sp.dma_start(b_w[:], A["L0_attn_b"]).then_inc(got, 16)
                sp.dma_start(c_w[:], A["L0_attn_c"]).then_inc(got, 16)
                sp.dma_start(w_o[:], A["L0_attn_w_out"]).then_inc(got, 16)
                sp.dma_start(cols[:], A["L0_attn_cols"]).then_inc(got, 16)
                sp.wait_ge(got, 80)

            @block.gpsimd
            def _(pool):
                pool.wait_ge(got, 80)
                for n, (hi, lo, full) in enumerate([(b_hi, b_lo, b_w), (c_hi, c_lo, c_w)]):
                    nc.gpsimd.tensor_copy(hi, full[:]).then_inc(pool_s, 1)
                    pool.wait_ge(pool_s, 2 * n + 1)
                    nc.gpsimd.tensor_tensor(lo, full[:], hi, ALU.subtract).then_inc(pool_s, 1)

            @block.tensor
            def _(pe):
                for g in range(4):
                    for j in range(4):
                        i = 4 * g + j
                        last = nc.tensor.transpose(ps[:, g, j * C:(j + 1) * C], S.xT[:, i * P:(i + 1) * P], S.ident[:])
                    last.then_inc(sums, 1)
                for g in range(4):
                    pe.wait_ge(xr_s, g + 1)
                    for j in range(4):
                        last = nc.tensor.transpose(ps[:, 4 + g, j * P:(j + 1) * P], rows[:, 4 * g + j, :], S.ident[:])
                    last.then_inc(rows_s, 1)

            @block.scalar
            def _(act):
                for g in range(4):
                    act.wait_ge(sums, g + 1)
                    for j in range(4):
                        i = 4 * g + j
                        last = nc.scalar.activation(sq[:, i * C:(i + 1) * C], ps[:, g, j * C:(j + 1) * C], ACT.Square,
                                                    accum_out=ms[:, i:i + 1])
                last.then_inc(sq_s, 1)
                act.wait_ge(sq_s, 1)
                nc.scalar.activation(sd[:], ms[:], ACT.Sqrt, bias=S.eps_ap(1e-4), scale=1.0 / C).then_inc(std_s, 1)
                act.wait_ge(got, 80)
                nc.scalar.activation(a_t[:], a_raw[:], ACT.Tanh)
                for g in range(4):
                    act.wait_ge(rows_s, g + 1)
                    nc.scalar.activation(xnT[:, g * QW:(g + 1) * QW], ps[:, 4 + g, :], ACT.Identity, scale=norm_w)

            @block.vector
            def _(dve):
                dve.wait_ge(std_s, 1)
                nc.vector.reciprocal(rs[:], sd[:]).then_inc(rstd_s, 1)
                dve.wait_ge(rstd_s, 1)
                for g in range(4):
                    for j in range(4):
                        i = 4 * g + j
                        last = nc.vector.tensor_scalar(rows[:, i, :], ps[:, g, j * C:(j + 1) * C], rs[:, i:i + 1], None,
                                                       ALU.mult)
                    last.then_inc(xr_s, 1)

        parts_s = S.sems.new("rnn_parts")
        with nc.Block(no_gpsimd_drain=True) as block:

            @block.vector
            def _(dve):
                for n, (hi, lo, full) in enumerate([(at_hi, at_lo, a_t), (xn_hi[:], xn_lo[:], xnT)]):
                    nc.vector.tensor_copy(hi, full[:]).then_inc(parts_s, 1)
                    dve.wait_ge(parts_s, n + 1)
                    nc.vector.tensor_tensor(lo, full[:], hi, ALU.subtract)

        mm_done = S.sems.new("rnn_mm_first", "rnn_mm_second")
        hi_done = S.sems.new("rnn_hi_first", "rnn_hi_second")
        full_done = S.sems.new("rnn_full_first", "rnn_full_second")
        lo_done = S.sems.new("rnn_lo_first", "rnn_lo_second")
        outs_ready, outs_used = S.sems.new("rnn_outs_ready", "rnn_outs_used")
        xn_v = xnT[:].rearrange("p (b t) -> p t b", b=B)
        xn_hv = xn_hi[:].rearrange("p (b t r) -> p r t b", b=B, r=2)
        xn_lv = xn_lo[:].rearrange("p (b t r) -> p r t b", b=B, r=2)
        outs_v = outsT[:].rearrange("p (b t) -> p t b", b=B)
        W = GP * B

        def bank(g, r):
            return ps[:, 2 * g + r, :].rearrange("p (t c b) -> p t c b", t=K, c=GP)

        with nc.Block(no_gpsimd_drain=True) as block:

            @block.tensor
            def _(pe):
                def project(q, ops):
                    for n in ops:
                        (w, m), c = ((c_hi, s_hi), (c_lo, s_hi), (c_hi, s_lo))[n // NP], n % NP
                        last = nc.tensor.matmul(ps[:, 4 + q, 0:K * B].rearrange("p (t b) -> p t b", b=B), w[:, c, :],
                                                m[:, q * K:(q + 1) * K, c * B:(c + 1) * B],
                                                start=(n == 0), stop=(n == 3 * NP - 1), skip_group_check=True)
                    if n == 3 * NP - 1:
                        last.then_inc(outs_ready, 1)

                def run(i, first=False):
                    for g in range(2):
                        pe.wait_ge(lo_done[g], i * (2 * K) + 1)
                        for r in range(2):
                            for c in range(GP):
                                n = g * GP + c
                                for w, m in ((b_hi, xn_hv), (b_lo, xn_hv), (b_hi, xn_lv)):
                                    nc.tensor.matmul(bank(g, r)[:, :, c, :], w[:, n, :], m[:, r, bass.ds(i * K, K), :],
                                                     start=(c == 0 and w is b_hi and m is xn_hv), stop=False,
                                                     skip_group_check=True)
                    for q in range(2):
                        before = not (first and q == 0)
                        if before:
                            pe.wait_ge(outs_used, i * 2 + (q + 1))
                        for t in range(q * K, (q + 1) * K):
                            prev = (t - 1) % (2 * K)
                            for g in range(2):
                                sums = bank(g, t % 2)[:, t // 2]
                                pe.wait_ge(hi_done[g], i * (2 * K) + (t + 1))
                                for w in (at_hi, at_lo):
                                    for c in range(GP):
                                        n = g * GP + c
                                        nc.tensor.matmul(sums[:, c, :], w[:, n, :], s_hi[:, prev, n * B:(n + 1) * B],
                                                         start=False, stop=False, skip_group_check=True)
                                slot = 2 * (t - q * K) + g
                                if before and 4 <= slot < 4 + 3 * NP:
                                    project(1 - q, [slot - 4])
                                pe.wait_ge(lo_done[g], i * (2 * K) + (t + 1))
                                for c in range(GP):
                                    n = g * GP + c
                                    last = nc.tensor.matmul(sums[:, c, :], at_hi[:, n, :], s_lo[:, prev, n * B:(n + 1) * B],
                                                            start=False, stop=(c == GP - 1), skip_group_check=True)
                                last.then_inc(mm_done[g], 1)

                pe.wait_ge(pool_s, 4)
                run(0, first=True)
                with pe.Fori(1, NCH // 2) as i:
                    run(i)
                for g in range(2):
                    pe.wait_ge(lo_done[g], T + 1)
                project(1, range(3 * NP))

            @block.scalar
            def _(act):
                with act.Fori(0, NCH // 2) as i:
                    for q in range(2):
                        for t in range(K):
                            for g in range(2):
                                act.wait_ge(mm_done[g], i * (2 * K) + (q * K + t + 1))
                                u = (q * K + t) // 2
                                sums = ps[:, 2 * g + t % 2, u * W:(u + 1) * W]
                                nc.scalar.activation(s_hi[:, q * K + t, g * W:(g + 1) * W], sums, ACT.Tanh)\
                                    .then_inc(hi_done[g], 1)
                                nc.scalar.activation(s_full[:, g, t % 2, :], sums, ACT.Tanh).then_inc(full_done[g], 1)

            @block.vector
            def _(dve):
                for g in range(2):
                    nc.vector.memset(s_hi[:, 2 * K - 1, g * W:(g + 1) * W], 0.0).then_inc(hi_done[g], 1)
                    nc.vector.memset(s_lo[:, 2 * K - 1, g * W:(g + 1) * W], 0.0).then_inc(lo_done[g], 1)
                dve.sem_inc(outs_used, 2)

                def outs(steps, q):
                    nc.vector.scalar_tensor_tensor(out=outs_v[:, steps, :], in0=xn_v[:, steps, :], scalar=skip,
                                                   in1=ps[:, 4 + q, 0:K * B].rearrange("p (t b) -> p t b", b=B),
                                                   op0=ALU.mult, op1=ALU.add).then_inc(outs_used, 1)

                def run(i, first=False):
                    for q in range(2):
                        for t in range(K):
                            for g in range(2):
                                dve.wait_ge(full_done[g], i * (2 * K) + (q * K + t + 1))
                                cut = slice(g * W, (g + 1) * W)
                                nc.vector.tensor_tensor(s_lo[:, q * K + t, cut], s_full[:, g, t % 2, :],
                                                        s_hi[:, q * K + t, cut], ALU.subtract).then_inc(lo_done[g], 1)
                        if not (first and q == 0):
                            dve.wait_ge(outs_ready, i * 2 + q)
                            outs(bass.ds(i * (2 * K) + (q - 1) * K, K), 1 - q)

                run(0, first=True)
                with dve.Fori(1, NCH // 2) as i:
                    run(i)
                dve.wait_ge(outs_ready, NCH)
                outs(slice(T - K, T), 1)

        y_ready, xb_s = S.sems.new("l0_y_ready", "l0_xb")
        with nc.Block(no_gpsimd_drain=True) as block:

            @block.tensor
            def _(pe):
                for g in range(NQ):
                    nc.tensor.matmul(ps[:, g, :], w_o[:], outsT[:, g * QW:(g + 1) * QW], start=True, stop=True)\
                        .then_inc(y_ready, 1)

            @block.vector
            def _(dve):
                nc.vector.tensor_scalar(sq[:], S.xT[:], 2.0, b_out, ALU.mult, ALU.add).then_inc(xb_s, 1)
                dve.wait_ge(xb_s, 1)
                for g in range(NQ):
                    dve.wait_ge(y_ready, g + 1)
                    cut = slice(g * QW, (g + 1) * QW)
                    nc.vector.tensor_tensor(S.rT[:, cut], sq[:, cut], ps[:, g, :], ALU.add)


GE = 42
SENTINEL, TAKEN = -1e30, -2e30


class Router:

    def __init__(self, nc, S, ctx, tag, E, combT, w_router, top_k, score, weigh, bias=None, groups=None, shared=0):
        def sb(name, shape, dt=F32):
            return ctx.enter_context(nc.sbuf_tensor(f"{tag}_{name}", shape, dt))

        self.nc, self.S, self.E, self.combT, self.w_router, self.top_k = nc, S, E, combT, w_router, top_k
        self.score, self.weigh, self.bias, self.groups, self.shared = score, weigh, bias, groups, shared
        self.NG = NG = combT.shape[1]
        self.EX = NG * GE
        self.wr, self.bias_sb = sb("w", [P, E]), sb("bias", [P, E])
        self.sc, self.raw, self.replaced = sb("sc", [P, NT, E + 8]), sb("raw", [P, NT, E]), sb("rep", [P, NT, E + 8])
        self.top, self.want = sb("top", [P, NT, 8]), sb("want", [P, NT, 8])
        self.gsc, self.gmask = sb("gsc", [P, NT, 16]), sb("gmask", [P, NT, 8])
        self.total, self.rec = sb("sum", [P, NT]), sb("rec", [P, NT])
        self.comb, self.parts = sb("comb", [P, NT, self.EX]), sb("parts", [P, NT, NG, 3, GE], BF16)
        self.got, self.logits, self.score_s, self.step_s, self.biased, self.exp_s, self.weighed, self.scaled, \
            self.part0, self.rest1, self.part1, self.part2, self.comb_up, out_dve, out_act = S.sems.new(
                *(f"{tag}_{n}" for n in ("got", "logits", "score", "step", "biased", "exp", "weighed", "scaled", "part0",
                                         "rest1", "part1", "part2", "comb_up", "comb_out_dve", "comb_out_act")))
        self.comb_out = [out_dve, out_act]
        self.halves = [slice(0, NT // 2), slice(NT // 2, NT)]

    def comb_v(self, half):
        return self.comb[:, self.halves[half], :].rearrange("p i (g e) -> p i g e", e=GE)

    def sync(self, sp):
        sp.dma_start(self.wr[:], self.w_router).then_inc(self.got, 16)
        if self.bias is not None:
            sp.dma_start(self.bias_sb[:], self.bias).then_inc(self.got, 16)

    def tensor(self, pe, seed):
        nc, ps, E = self.nc, self.S.psum, self.E
        pe.wait_ge(self.got, 16 if self.bias is None else 32)
        for i in range(NT):
            last = nc.tensor.matmul(ps[:, i // 2, (i % 2) * E:(i % 2 + 1) * E], self.S.xT[:, i * P:(i + 1) * P],
                                    self.wr[:], start=True, stop=True)
            if i % 2:
                last.then_inc(self.logits, 1)
        pe.wait_ge(self.score_s, NT // 2)
        seed()
        n = 0
        for half in range(2):
            pe.wait_ge(self.part2, half + 1)
            for g in range(self.NG):
                if n >= 4:
                    pe.wait_ge(self.comb_out[n % 2], (n - 4) // 2 + 1)
                bank = ps[:, 4 + n % 4, :].bitcast(BF16)
                for j in range(8):
                    last = nc.tensor.transpose(bank[0:3 * GE, j * P:(j + 1) * P],
                                               self.parts[:, 8 * half + j, g].rearrange("p a e -> p (a e)"),
                                               self.S.identb[:])
                last.then_inc(self.comb_up, 1)
                n += 1
        for engine in range(2):
            pe.wait_ge(self.comb_out[engine], self.NG)

    def scalar(self, act):
        nc, ps, E = self.nc, self.S.psum, self.E
        halves = self.halves

        if self.score != "bias_sigmoid":
            for b in range(NT // 2):
                act.wait_ge(self.logits, b + 1)
                dst = self.raw if self.score == "sigmoid_bias" else self.sc
                nc.scalar.activation(dst[:, 2 * b:2 * b + 2, 0:E], ps[:, b, 0:2 * E].rearrange("p (i e) -> p i e", e=E),
                                     ACT.Sigmoid if self.score == "sigmoid_bias" else ACT.Copy).then_inc(self.score_s, 1)
        else:
            for h in range(2):
                act.wait_ge(self.biased, h + 1)
                nc.scalar.activation(self.sc[:, halves[h], 0:E], self.raw[:, halves[h], :], ACT.Sigmoid)\
                    .then_inc(self.exp_s, 1)
        if self.weigh == "softmax":
            for h in range(2):
                act.wait_ge(self.biased, h + 1)
                nc.scalar.activation(self.raw[:, halves[h], :], self.raw[:, halves[h], :], ACT.Exp).then_inc(self.exp_s, 1)
        for h in range(2):
            act.wait_ge(self.weighed, h + 1)
            for i in range(h * NT // 2, (h + 1) * NT // 2):
                last = nc.scalar.activation(self.comb[:, i, 0:E], self.comb[:, i, 0:E], ACT.Copy, scale=self.rec[:, i:i + 1])
            last.then_inc(self.scaled, 1)
            act.wait_ge(self.scaled, h + 1)
            nc.scalar.activation(self.parts[:, halves[h], :, 0, :], self.comb_v(h), ACT.Copy).then_inc(self.part0, 1)
            act.wait_ge(self.rest1, h + 1)
            nc.scalar.activation(self.parts[:, halves[h], :, 1, :], self.comb_v(h), ACT.Copy).then_inc(self.part1, 1)
        for n in range(1, 2 * self.NG, 2):
            act.wait_ge(self.comb_up, n + 1)
            half, g = n // self.NG, n % self.NG
            nc.scalar.activation(self.combT[0:3 * GE, g, half * 1024:(half + 1) * 1024],
                                 ps[:, 4 + n % 4, :].bitcast(BF16)[0:3 * GE, :], ACT.Copy).then_inc(self.comb_out[1], 1)

    def vector(self, dve):
        nc, ps, E, top_k = self.nc, self.S.psum, self.E, self.top_k
        sc, raw, comb = self.sc, self.raw, self.comb
        count = [0]

        def step(ins):
            count[0] += 1
            ins.then_inc(self.step_s, 1)
            dve.wait_ge(self.step_s, count[0])

        def choose(h, values, width, k, taken, into):
            tiles = range(h * NT // 2, (h + 1) * NT // 2)
            for i in tiles:
                last = nc.vector.max(self.top[:, i, :], values[:, i, 0:width])
            step(last)
            want = self.top
            if k < 8:
                want = self.want
                step(nc.vector.tensor_copy(want[:, self.halves[h], 0:k], self.top[:, self.halves[h], 0:k]))
            for i in tiles:
                last = nc.vector.match_replace(into[:, i, :], want[:, i, :], values[:, i, :], taken)
            step(last)

        def scores(h):
            half = self.halves[h]
            wide = self.bias_sb[:].unsqueeze(1).broadcast_to([P, NT // 2, E])
            if self.bias is not None:
                dve.wait_ge(self.got, 32)
            if self.score == "bias_sigmoid":
                for b in range(4 * h, 4 * h + 4):
                    dve.wait_ge(self.logits, b + 1)
                    last = nc.vector.tensor_tensor(raw[:, 2 * b:2 * b + 2, :],
                                                   ps[:, b, 0:2 * E].rearrange("p (i e) -> p i e", e=E),
                                                   self.bias_sb[:].unsqueeze(1).broadcast_to([P, 2, E]), ALU.add)\
                        .then_inc(self.score_s, 1)
                dve.wait_ge(self.score_s, 4 * h + 4)
                nc.vector.tensor_copy(self.total[:, half], raw[:, half, 0]).then_inc(self.biased, 1)
            elif self.score == "sigmoid_bias":
                dve.wait_ge(self.score_s, 4 * h + 4)
                step(nc.vector.tensor_tensor(raw[:, half, :], raw[:, half, :], wide, ALU.add))
                by_group = raw[:, half, :].rearrange("p i (g e) -> p i g e", g=8)
                step(nc.vector.tensor_reduce(self.gsc[:, half, 0:8], by_group, AX.X, ALU.max))
                choose(h, self.gsc, 8, self.groups, TAKEN, self.replaced[:, :, 0:16])
                step(nc.vector.tensor_tensor(self.gmask[:, half, :], self.replaced[:, half, 0:8], self.gsc[:, half, 0:8],
                                             ALU.not_equal))
                step(nc.vector.tensor_tensor(sc[:, half, 0:E].rearrange("p i (g e) -> p i g e", g=8), by_group,
                                             self.gmask[:, half, :].unsqueeze(3).broadcast_to([P, NT // 2, 8, E // 8]),
                                             ALU.mult))
            else:
                dve.wait_ge(self.score_s, 4 * h + 4)

        def weights(h):
            half = self.halves[h]
            if self.score == "bias_sigmoid":
                dve.wait_ge(self.exp_s, h + 1)
            chosen, values, total = comb[:, half, 0:E], sc[:, half, 0:E], self.total[:, half]
            if self.weigh == "softmax":
                choose(h, sc, E, top_k, TAKEN, self.replaced)
                nc.vector.tensor_tensor(chosen, self.replaced[:, half, 0:E], values, ALU.not_equal)
                nc.vector.tensor_tensor(raw[:, half, :], values, self.top[:, half, 0:1].broadcast_to([P, NT // 2, E]),
                                        ALU.subtract).then_inc(self.biased, 1)
                dve.wait_ge(self.exp_s, h + 1)
                step(nc.vector.tensor_tensor(chosen, chosen, raw[:, half, :], ALU.mult))
                step(nc.vector.tensor_reduce(total, chosen, AX.X, ALU.add))
                nc.vector.reciprocal(self.rec[:, half], total).then_inc(self.weighed, 1)
            else:
                choose(h, sc, E, top_k, 0.0, self.replaced)
                nc.vector.tensor_tensor(chosen, values, self.replaced[:, half, 0:E], ALU.subtract)
                step(nc.vector.tensor_reduce(total, self.top[:, half, 0:top_k], AX.X, ALU.add))
                small, factor = self.weigh
                step(nc.vector.tensor_scalar(total, total, small, 1.0 / factor, ALU.add, ALU.mult))
                nc.vector.reciprocal(self.rec[:, half], total).then_inc(self.weighed, 1)

        def rest(h, part):
            dve.wait_ge(self.part0 if part == 0 else self.part1, h + 1)
            out = self.comb_v(h) if part == 0 else self.parts[:, self.halves[h], :, 2, :]
            nc.vector.tensor_tensor(out, self.comb_v(h), self.parts[:, self.halves[h], :, part, :], ALU.subtract)\
                .then_inc(self.rest1 if part == 0 else self.part2, 1)

        nc.vector.memset(comb[:, :, E:], 0.0)
        nc.vector.memset(sc[:, :, E:], SENTINEL)
        nc.vector.memset(self.gsc[:, :, 8:], SENTINEL)
        step(nc.vector.memset(self.want[:, :, :], SENTINEL))
        if self.shared:
            step(nc.vector.memset(comb[:, :, E:E + self.shared], 1.0))
        scores(0)
        scores(1)
        weights(0)
        weights(1)

        def turned(first, last):
            for n in range(first, last):
                if n % 2 == 0:
                    dve.wait_ge(self.comb_up, n + 1)
                    half, g = n // self.NG, n % self.NG
                    nc.vector.tensor_copy(self.combT[0:3 * GE, g, half * 1024:(half + 1) * 1024],
                                          ps[:, 4 + n % 4, :].bitcast(BF16)[0:3 * GE, :]).then_inc(self.comb_out[0], 1)

        rest(0, 0)
        rest(0, 1)
        rest(1, 0)
        turned(0, self.NG)
        rest(1, 1)
        turned(self.NG, 2 * self.NG)


def experts_phase(nc, S, ctx, tag, weights, selector, combT, func, gated, UB, route):
    U, _, COLS = weights.shape
    NSEL = selector.shape[1]
    LAG = 3
    ps = S.psum
    acc = [ps[:, n, :] for n in range(NQ)]
    sel_got, zeroed = S.sems.new(f"{tag}_sel_got", f"{tag}_zeroed")
    gate_done, up_done, comb_done, act_done, hu_done, hw_done, hi_done, lo_done, down_done, split_hi, split_done, \
        split_start = S.sems.new(*(f"{tag}_{n}" for n in ("gate", "up", "combed", "act", "hu", "hw", "hi", "lo", "down",
                                                          "split_hi", "split", "split_start")))
    slot_got = [S.sems.new(f"{tag}_slot{s}") for s in range(UB)]
    x_hi, x_lo = S.x_hi, S.x_lo

    def sb(name, shape, dt):
        return ctx.enter_context(nc.sbuf_tensor(f"{tag}_{name}", shape, dt))

    sel = sb("sel", [P, NSEL, P], BF16)
    stage = sb("stage", [P, UB, COLS], F32)
    w_hi, w_lo = sb("whi", [P, UB, COLS], F16), sb("wlo", [P, UB, COLS], F16)
    h, hu, hw = sb("h", [P, 2, QW], F32), sb("hu", [P, 2, QW], F32), sb("hw", [P, 2, QW], F32)
    hw_hi, hw_lo = sb("hwhi", [P, 4, QW], F16), sb("hwlo", [P, 4, QW], F16)

    def open_sums():
        for n in range(NQ):
            nc.tensor.matmul(acc[n], S.ident[:], S.xT[:, n * QW:(n + 1) * QW], start=True, stop=False,
                             skip_group_check=True)

    runs = []
    for g in range((U + NSEL - 1) // NSEL):
        runs.append((g * NSEL, (min(U, (g + 1) * NSEL) - g * NSEL) // UB, g))
    assert sum(r[1] for r in runs) * UB == U

    with nc.Block(no_gpsimd_drain=True) as block:

        @block.sync
        def _(sp):
            route.sync(sp)
            sp.dma_start(sel[0:3 * GE], selector).then_inc(sel_got, 16)
            for u0, bodies, _ in runs:
                with sp.Fori(0, bodies) as j:
                    for s in range(UB):
                        sp.wait_ge(split_done, j * UB + (u0 + s + 1))
                        sp.dma_start(stage[:, s, :], weights[bass.ds(j * UB + (u0 + s), 1)]
                                     .rearrange("u p c -> p (u c)")).then_inc(slot_got[s], 16)

        @block.gpsimd
        def _(pool):
            nc.gpsimd.memset(w_hi[:, UB - 1, :], 0.0)
            nc.gpsimd.memset(w_lo[:, UB - 1, :], 0.0)
            nc.gpsimd.memset(hw[:, 1, :], 0.0)
            nc.gpsimd.memset(hw_hi[:, 1:4, :], 0.0)
            nc.gpsimd.memset(hw_lo[:, 1:4, :], 0.0).then_inc(zeroed, 1)
            pool.wait_ge(zeroed, 1)
            pool.sem_inc(split_done, UB)
            for u0, bodies, _ in runs:
                with pool.Fori(0, bodies) as j:
                    for s in range(UB):
                        u = j * UB + (u0 + s)
                        pool.wait_ge(down_done, j * (4 * UB) + 4 * (u0 + s) + LAG)
                        pool.wait_ge(slot_got[s], j * 16 + (u0 // UB * 16 + 16))
                        pool.sem_inc(split_start, 1)
                        nc.gpsimd.tensor_copy(w_hi[:, s, :], stage[:, s, :]).then_inc(split_hi, 1)
                        pool.wait_ge(split_hi, u + 1)
                        nc.gpsimd.tensor_tensor(w_lo[:, s, :], stage[:, s, :], w_hi[:, s, :], ALU.subtract)\
                            .then_inc(split_done, 1)

        @block.tensor
        def _(pe):
            pe.sem_inc(down_done, 4 * (UB - 1))
            route.tensor(pe, open_sums)
            pe.wait_ge(zeroed, 1)
            pe.wait_ge(sel_got, 16)

            def product(out, cols, s, n):
                cut = slice(n * QW, (n + 1) * QW)
                for a, b in ((w_hi, x_hi), (w_hi, x_lo), (w_lo, x_hi)):
                    last = nc.tensor.matmul(out, a[:, s, cols], b[:, cut], start=(a is w_hi and b is x_hi),
                                            stop=(a is w_lo))
                return last

            def down(s, n, k4):
                for a, b in ((w_hi, hw_hi), (w_hi, hw_lo), (w_lo, hw_hi)):
                    last = nc.tensor.matmul(acc[n], a[:, s, COLS - P:COLS], b[:, k4, :], start=False, stop=False,
                                            skip_group_check=True)
                return last.then_inc(down_done, 1)

            for u0, bodies, g in runs:
                with pe.Fori(0, bodies) as j:
                    for s in range(UB):
                        pe.wait_ge(split_done, j * UB + (u0 + s + 1 + UB))
                        for n in range(NQ):
                            k = 4 * s + n
                            kk = j * (4 * UB) + (4 * u0 + k)
                            R = 3 * k if gated else None
                            hb = ps[:, 4 + (R % 4 if gated else k % 2), :]
                            cb = ps[:, 4 + ((R + 2) % 4 if gated else 2 + k % 2), :]
                            pe.wait_ge(hw_done, kk + 1)
                            product(hb, slice(0, P), s, n).then_inc(gate_done, 1)
                            if gated:
                                pe.wait_ge(act_done, kk + 1)
                                product(ps[:, 4 + (R + 1) % 4, :], slice(P, 2 * P), s, n).then_inc(up_done, 1)
                                pe.wait_ge(hu_done, kk + 1)
                            nc.tensor.matmul(cb, sel[0:3 * GE, bass.ds(j * UB + s, 1), :].rearrange("p u m -> p (u m)"),
                                             combT[0:3 * GE, g, n * QW:(n + 1) * QW], start=True, stop=True)\
                                .then_inc(comb_done, 1)
                            pe.wait_ge(lo_done, kk + 1)
                            down((s if n >= LAG else s - 1) % UB, (n - LAG) % NQ, (k - LAG) % 4)
            for n in range(NQ - LAG, NQ):
                pe.wait_ge(lo_done, 4 * U + n)
                down(UB - 1, n, n)

        @block.scalar
        def _(act):
            route.scalar(act)
            act.wait_ge(zeroed, 1)
            act.sem_inc(act_done, 1)

            def high(k):
                nc.scalar.activation(hw_hi[:, k % 4, :], hw[:, k % 2, :], ACT.Copy).then_inc(hi_done, 1)

            for u0, bodies, _ in runs:
                with act.Fori(0, bodies) as j:
                    for k in range(4 * UB):
                        kk = j * (4 * UB) + (4 * u0 + k)
                        act.wait_ge(gate_done, kk + 1)
                        nc.scalar.activation(h[:, k % 2, :], ps[:, 4 + (3 * k % 4 if gated else k % 2), :], func)\
                            .then_inc(act_done, 1)
                        act.wait_ge(hw_done, kk + 2)
                        high(k - 1)
            act.wait_ge(hw_done, 4 * U + 2)
            high(4 * U - 1)
            act.wait_ge(down_done, 4 * (UB - 1) + 4 * U + LAG)
            for n in range(NQ):
                nc.scalar.activation(S.rT[:, n * QW:(n + 1) * QW], acc[n], ACT.Copy)

        @block.vector
        def _(dve):
            route.vector(dve)
            dve.wait_ge(zeroed, 1)
            dve.sem_inc(hw_done, 2)
            dve.sem_inc(lo_done, LAG - 1)
            if gated:
                dve.sem_inc(hu_done, 1)

            def low(k):
                nc.vector.tensor_tensor(hw_lo[:, k % 4, :], hw[:, k % 2, :], hw_hi[:, k % 4, :], ALU.subtract)\
                    .then_inc(lo_done, 1)

            for u0, bodies, _ in runs:
                with dve.Fori(0, bodies) as j:
                    for k in range(4 * UB):
                        kk = j * (4 * UB) + (4 * u0 + k)
                        src = h
                        dve.wait_ge(act_done, kk + 2)
                        dve.wait_ge(lo_done, kk + 2)
                        if gated:
                            dve.wait_ge(up_done, kk + 1)
                            nc.vector.tensor_tensor(hu[:, k % 2, :], h[:, k % 2, :], ps[:, 4 + (3 * k + 1) % 4, :],
                                                    ALU.mult).then_inc(hu_done, 1)
                            src = hu
                            dve.wait_ge(hu_done, kk + 2)
                        dve.wait_ge(comb_done, kk + 1)
                        cb = ps[:, 4 + ((3 * k + 2) % 4 if gated else 2 + k % 2), :]
                        nc.vector.tensor_tensor(hw[:, k % 2, :], src[:, k % 2, :], cb, ALU.mult).then_inc(hw_done, 1)
                        dve.wait_ge(hi_done, kk + 1)
                        low(k - 1)
            dve.wait_ge(hi_done, 4 * U + 1)
            low(4 * U - 1)


def moe(nc, S, tag, E, weights, selector, func, gated, UB, **routing):
    U = weights.shape[0]
    NG = (U + selector.shape[1] - 1) // selector.shape[1]
    with ExitStack() as ctx:
        combT = ctx.enter_context(nc.sbuf_tensor(f"{tag}_combT", [P, NG, N], BF16))
        route = Router(nc, S, ctx, f"{tag}r", E, combT, **routing)
        experts_phase(nc, S, ctx, tag, weights, selector, combT, func, gated, UB, route)


def l0_ffn(nc, S, A):
    moe(nc, S, "m0", 8, A["m0_w"], A["c_sel_halves"], ACT.Gelu, False, 4,
        w_router=A["m0_router"], top_k=2, score="logits", weigh="softmax")


def l1_ffn(nc, S, A):
    moe(nc, S, "m1", 64, A["m1_w"], A["c_sel_pairs"], ACT.Silu, True, 3,
        w_router=A["m1_router"], top_k=6, score="sigmoid_bias", weigh=(1e-8, 1.0), bias=A["m1_bias"], groups=4, shared=2)


def l2_ffn(nc, S, A):
    moe(nc, S, "m2", 160, A["m2_w"], A["c_sel_pairs"], ACT.Silu, False, 3,
        w_router=A["m2_router"], top_k=8, score="bias_sigmoid", weigh=(1e-9, 2.5), bias=A["m2_bias"], shared=1)


def pipeline(eng, n, lag, step, unroll=2, head=None):
    head = head or max(4, unroll)
    for k in range(head):
        step(0, k)
    with eng.Fori(0, (n - head) // unroll) as j:
        for k in range(head, head + unroll):
            step(j, k)
    for k in range(n, n + lag):
        step(0, k)


def live(j, k, n):
    return not isinstance(j, int) or 0 <= k < n


def wait(eng, sem, j, k, unroll=2):
    if not isinstance(j, int):
        eng.wait_ge(sem, j * unroll + k)
    elif k > 0:
        eng.wait_ge(sem, k)


def split_on(dve, sem, count, hi, lo, full):
    nc = dve.bass
    nc.vector.tensor_copy(hi, full).then_inc(sem, 1)
    dve.wait_ge(sem, count)
    return nc.vector.tensor_tensor(lo, full, hi, ALU.subtract)


def products(nc, out, lhs, rhs, first=True, last=True, skip=False):
    (a_hi, a_lo), (b_hi, b_lo) = lhs, rhs
    nc.tensor.matmul(out, a_hi, b_hi, start=first, stop=False, skip_group_check=skip)
    nc.tensor.matmul(out, a_hi, b_lo, start=False, stop=False, skip_group_check=skip)
    return nc.tensor.matmul(out, a_lo, b_hi, start=False, stop=last, skip_group_check=skip)


def l1_attn(nc, S, A):
    H, L, D, CH = 16, 64, 8, 128
    NCH = T // CH
    NP = H // 2
    VW = 2 * D + 2
    SC = D ** -0.5
    ps = S.psum
    WN = 4 * P + H * L + NP * P
    with (nc.sbuf_tensor("la_w", [P, WN], F32) as w,
          nc.sbuf_tensor("la_whi", [P, WN], F16) as w_hi,
          nc.sbuf_tensor("la_wlo", [P, WN], F16) as w_lo,
          nc.sbuf_tensor("la_rope", [P, 2, NCH * L], F32) as rope,
          nc.sbuf_tensor("la_mask", [P, 512], BF16) as mask,
          nc.sbuf_tensor("la_own", [P, 2 * D], F32) as own,
          nc.sbuf_tensor("la_khi", [P, B, NCH, L], F16) as k_hi,
          nc.sbuf_tensor("la_klo", [P, B, NCH, L], F16) as k_lo,
          nc.sbuf_tensor("la_vhi", [P, B, NP, NCH, VW], F16) as v_hi,
          nc.sbuf_tensor("la_vlo", [P, B, NP, NCH, VW], F16) as v_lo,
          nc.sbuf_tensor("la_athi", [P, B, NP, VW], F16) as at_hi,
          nc.sbuf_tensor("la_atlo", [P, B, NP, VW], F16) as at_lo,
          nc.sbuf_tensor("la_wT", [P, N], F32) as wT):

        def cols(a, n=P):
            return w_hi[:, a:a + n], w_lo[:, a:a + n]

        W_K, W_KR, W_V, W_P = (cols(n * P) for n in range(4))
        W_G = [cols(4 * P + n * 512, 512) for n in range(2)]
        Q = [cols(4 * P + H * L + n * P) for n in range(NP)]

        got, parts_s, k_up, v_up, v_high, rope_s, done_s = S.sems.new(
            "la_got", "la_parts", "la_kup", "la_vup", "la_vhigh", "la_rope", "la_kv")
        with (nc.sbuf_tensor("la_kc", [P, 2, 512], F32) as kc,
              nc.sbuf_tensor("la_kr", [P, 2, 512], F32) as kr,
              nc.Block(no_gpsimd_drain=True) as block):
            seen = [x[:].rearrange("p (b n c) -> p b n c", b=B, n=NCH)[:, :, :, 0:L] for x in (S.x_hi, S.x_lo)]

            @block.sync
            def _(sp):
                for dst, src in ((w[:], "la_w"), (rope[:], "la_rope"), (mask[:], "la_mask"), (own[:], "la_own"),
                                 (at_hi[:], "la_ones_hi"), (at_lo[:], "la_zeros")):
                    sp.dma_start(dst, A[src]).then_inc(got, 16)
                sp.wait_ge(got, 96)

            @block.tensor
            def _(pe):
                pe.wait_ge(parts_s, 2)
                for half in range(2):
                    cut = slice(4 * half, 4 * half + 4)
                    for n, wk in enumerate((W_K, W_KR)):
                        last = products(nc, ps[:, 2 * half + n, :], wk, (seen[0][:, cut], seen[1][:, cut]))
                    last.then_inc(k_up, 1)
                for b in range(B):
                    if b >= 4:
                        pe.wait_ge(done_s, b - 3)
                    for n in range(NCH):
                        last = products(nc, ps[n * L:(n + 1) * L, 4 + b % 4, 0:P], (seen[0][:, b, n], seen[1][:, b, n]),
                                        W_V)
                    last.then_inc(v_up, 1)

            @block.scalar
            def _(act):
                for b in range(B):
                    act.wait_ge(v_up, b + 1)
                    for n in range(NCH):
                        r = slice(n * L, (n + 1) * L)
                        last = nc.scalar.activation(v_hi[r, b, :, n, 0:2 * D],
                                                    ps[r, 4 + b % 4, 0:P].rearrange("p (c d) -> p c d", c=NP), ACT.Copy)
                    last.then_inc(v_high, 1)

            @block.vector
            def _(dve):
                for n in range(NCH):
                    r, other = slice(n * L, (n + 1) * L), slice((1 - n) * L, (2 - n) * L)
                    nc.vector.memset(v_hi[other, :, :, n, :], 0.0)
                    nc.vector.memset(v_lo[other, :, :, n, :], 0.0)
                    nc.vector.memset(v_hi[r, :, :, n, 2 * D:VW], 1.0)
                    nc.vector.memset(v_lo[r, :, :, n, 2 * D:VW], 0.0)
                dve.wait_ge(got, 96)
                split_on(dve, parts_s, 1, w_hi[:], w_lo[:], w[:]).then_inc(parts_s, 1)
                n = 0
                for half in range(2):
                    dve.wait_ge(k_up, half + 1)
                    for m, t in enumerate((kc, kr)):
                        nc.vector.tensor_tensor(t[:, half, :].rearrange("p (b n) -> p b n", b=4),
                                                ps[:, 2 * half + m, :].rearrange("p (b n) -> p b n", b=4),
                                                rope[:, m:m + 1, :].broadcast_to([P, 4, NCH * L]), ALU.mult)\
                            .then_inc(rope_s, 1)
                    n += 2
                    dve.wait_ge(rope_s, n)
                    nc.vector.tensor_tensor(kc[:, half, :], kc[:, half, :], kr[:, half, :], ALU.add).then_inc(rope_s, 1)
                    n += 1
                    dve.wait_ge(rope_s, n)
                    flat = [t[:, 4 * half:4 * half + 4].rearrange("p b n c -> p (b n c)") for t in (k_hi, k_lo)]
                    n += 1
                    split_on(dve, rope_s, n, flat[0], flat[1], kc[:, half, :])
                for b in range(B):
                    dve.wait_ge(v_high, b + 1)
                    for n in range(NCH):
                        r = slice(n * L, (n + 1) * L)
                        last = nc.vector.tensor_tensor(v_lo[r, b, :, n, 0:2 * D],
                                                       ps[r, 4 + b % 4, 0:P].rearrange("p (c d) -> p c d", c=NP),
                                                       v_hi[r, b, :, n, 0:2 * D], ALU.subtract)
                    last.then_inc(done_s, 1)

        s_up, mx_s, sub_s, exp_s, t_up, t_hi, t_lo, o_up, at_s, small = S.sems.new(
            *(f"lb_{n}" for n in ("s_up", "max", "sub", "exp", "t_up", "t_hi", "t_lo", "o_up", "at", "small")))
        with (nc.sbuf_tensor("lb_mx", [P, 2, NP * NCH], F32) as mx,
              nc.sbuf_tensor("lb_z", [P, 2, 1024], F32) as z,
              nc.sbuf_tensor("lb_e", [P, 2, 1024], F32) as e,
              nc.sbuf_tensor("lb_thi", [P, 2, 1024], F16) as pt_hi,
              nc.sbuf_tensor("lb_tlo", [P, 2, 1024], F16) as pt_lo,
              nc.sbuf_tensor("lb_rec", [P, NP, NCH], F32) as rec,
              nc.sbuf_tensor("lb_o", [P, NP, NCH, 2 * D], F32) as o,
              nc.Block(no_gpsimd_drain=True) as block):

            def scores(q):
                return ps[:, 2 * q:2 * q + 2, :].rearrange("p a n -> p (a n)")

            turned = ps[:, 4:6, :].rearrange("p a n -> p (a n)")

            @block.tensor
            def _(pe):
                def step(j, k):
                    if live(j, k, B):
                        q = k % 2
                        wait(pe, sub_s, j, k - 1)
                        keys = [t[:, bass.ds(j * 2 + k, 1)].rearrange("p b n c -> p (b n c)") for t in (k_hi, k_lo)]
                        for m in range(2):
                            nc.tensor.matmul(ps[:, 2 * q + m, :], S.identb[:], mask[:], start=True, stop=False,
                                             skip_group_check=True)
                            for c in range(4):
                                last = products(nc, ps[:, 2 * q + m, c * P:(c + 1) * P], Q[4 * m + c], keys,
                                                first=False, last=(c == 3), skip=True)
                        last.then_inc(s_up, 1)
                    if live(j, k - 1, B):
                        wait(pe, exp_s, j, k)
                        wait(pe, t_lo, j, k - 1)
                        for c in range(NP):
                            last = nc.tensor.transpose(ps[:, 4 + c // 4, c % 4 * P:(c % 4 + 1) * P],
                                                       e[:, (k - 1) % 2, c * P:(c + 1) * P], S.ident[:])
                        last.then_inc(t_up, 1)
                    if live(j, k - 2, B):
                        wait(pe, t_lo, j, k - 1)
                        wait(pe, at_s, j, k - 3)
                        for c in range(NP):
                            lhs = [t[:, k % 2, c * P:(c + 1) * P] for t in (pt_hi, pt_lo)]
                            rhs = [t[:, bass.ds(j * 2 + (k - 2), 1), c].rearrange("p b n v -> p (b n v)")
                                   for t in (v_hi, v_lo)]
                            last = products(nc, ps[:, 6 + k % 2, c * NCH * VW:(c + 1) * NCH * VW], lhs, rhs)
                        last.then_inc(o_up, 1)
                pipeline(pe, B, 2, step)

            @block.scalar
            def _(act):
                def step(j, k):
                    if live(j, k - 1, B):
                        wait(act, t_up, j, k)
                        wait(act, o_up, j, k - 2)
                        nc.scalar.activation(pt_hi[:, (k - 1) % 2, :], turned, ACT.Copy).then_inc(t_hi, 1)
                    if live(j, k, B):
                        wait(act, sub_s, j, k + 1)
                        wait(act, t_up, j, k - 1)
                        nc.scalar.activation(e[:, k % 2, :], z[:, k % 2, :], ACT.Exp, scale=SC).then_inc(exp_s, 1)
                pipeline(act, B, 1, step)

            @block.vector
            def _(dve):
                def step(j, k):
                    if live(j, k, B):
                        q = k % 2
                        wait(dve, s_up, j, k + 1)
                        s4 = scores(q).rearrange("p (c n) -> p c n", n=L)
                        nc.vector.tensor_reduce(mx[:, q, :], s4, AX.X, ALU.max).then_inc(mx_s, 1)
                        wait(dve, mx_s, j, k + 1)
                        wait(dve, exp_s, j, k - 1)
                        nc.vector.tensor_tensor(z[:, q, :].rearrange("p (c n) -> p c n", n=L), s4,
                                                mx[:, q, :].unsqueeze(2).broadcast_to([P, NP * NCH, L]), ALU.subtract)\
                            .then_inc(sub_s, 1)
                    if live(j, k - 1, B):
                        q = (k - 1) % 2
                        wait(dve, t_hi, j, k)
                        nc.vector.tensor_tensor(pt_lo[:, q, :], turned, pt_hi[:, q, :], ALU.subtract).then_inc(t_lo, 1)
                    if live(j, k - 2, B):
                        q = k % 2
                        sums = ps[:, 6 + q, 0:NP * NCH * VW].rearrange("p (c n v) -> p c n v", c=NP, n=NCH)
                        wait(dve, o_up, j, k - 1)
                        nc.vector.reciprocal(rec[:], sums[:, :, :, 2 * D]).then_inc(small, 1)
                        many(dve, 1, j, k)
                        nc.vector.tensor_tensor(o[:], sums[:, :, :, 0:2 * D],
                                                rec[:].unsqueeze(3).broadcast_to([P, NP, NCH, 2 * D]), ALU.mult)\
                            .then_inc(small, 1)
                        many(dve, 2, j, k)
                        nc.vector.tensor_tensor(o[:, :, 0, :], o[:, :, 0, :], o[:, :, 1, :], ALU.add).then_inc(small, 1)
                        many(dve, 3, j, k)
                        nc.vector.tensor_tensor(o[:, :, 1, :], o[:, :, 0, :], own[:].unsqueeze(1).broadcast_to([P, NP, 2 * D]),
                                                ALU.mult).then_inc(small, 1)
                        many(dve, 4, j, k)
                        hi, lo = [t[:, bass.ds(j * 2 + (k - 2), 1), :, 0:2 * D].rearrange("p b c v -> p (b c) v")
                                  for t in (at_hi, at_lo)]
                        nc.vector.tensor_copy(hi, o[:, :, 1, :]).then_inc(small, 1)
                        many(dve, 5, j, k)
                        nc.vector.tensor_tensor(lo, o[:, :, 1, :], hi, ALU.subtract).then_inc(at_s, 1)

                def many(dve, n, j, k):
                    dve.wait_ge(small, j * 10 + (5 * (k - 2) + n))

                pipeline(dve, B, 2, step)

        g_up, mx_s, sub_s, exp_s, t_up, t_hi, t_lo, o_up, rec_s, row_s, w_up, w_out = S.sems.new(
            *(f"lc_{n}" for n in ("g_up", "max", "sub", "exp", "t_up", "t_hi", "t_lo", "o_up", "rec", "row", "w_up",
                                  "w_out")))
        with (nc.sbuf_tensor("lc_mx", [P, 2, H], F32) as mx,
              nc.sbuf_tensor("lc_z", [P, 2, 1024], F32) as z,
              nc.sbuf_tensor("lc_e", [P, 2, 1024], F32) as e,
              nc.sbuf_tensor("lc_thi", [P, 2, 1024], F16) as et_hi,
              nc.sbuf_tensor("lc_tlo", [P, 2, 1024], F16) as et_lo,
              nc.sbuf_tensor("lc_rec", [P, 2, NP, 2], F32) as rec,
              nc.sbuf_tensor("lc_row", [P, 2, P], F32) as row,
              nc.Block(no_gpsimd_drain=True) as block):
            turned = ps[:, 4:6, :].rearrange("p a n -> p (a n)")

            @block.tensor
            def _(pe):
                def step(j, k):
                    if live(j, k, NT):
                        wait(pe, sub_s, j, k - 1)
                        x = [t[:, bass.ds(j * (2 * P) + k * P, P)] for t in (S.x_hi, S.x_lo)]
                        for m in range(2):
                            last = products(nc, ps[:, 2 * (k % 2) + m, :], x, W_G[m])
                        last.then_inc(g_up, 1)
                    if live(j, k - 1, NT):
                        wait(pe, exp_s, j, k)
                        wait(pe, t_lo, j, k - 1)
                        for c in range(NP):
                            last = nc.tensor.transpose(ps[:, 4 + c // 4, c % 4 * P:(c % 4 + 1) * P],
                                                       e[:, (k - 1) % 2, c * P:(c + 1) * P], S.ident[:])
                        last.then_inc(t_up, 1)
                    if live(j, k - 2, NT):
                        wait(pe, t_lo, j, k - 1)
                        wait(pe, row_s, j, k - 2)
                        seq = j + (k - 2) // 2
                        for c in range(NP):
                            lhs = [t[:, k % 2, c * P:(c + 1) * P] for t in (et_hi, et_lo)]
                            rhs = [t[:, bass.ds(seq, 1), c].rearrange("p b v -> p (b v)") for t in (at_hi, at_lo)]
                            last = products(nc, ps[:, 6, c * VW:(c + 1) * VW], lhs, rhs)
                        last.then_inc(o_up, 1)
                    if live(j, k - 3, NT):
                        wait(pe, row_s, j, k - 2)
                        wait(pe, w_out, j, k - 3)
                        nc.tensor.transpose(ps[:, 7, 0:P], row[:, (k - 3) % 2, :], S.ident[:]).then_inc(w_up, 1)
                pipeline(pe, NT, 3, step)

            @block.scalar
            def _(act):
                def step(j, k):
                    if live(j, k - 1, NT):
                        wait(act, t_up, j, k)
                        wait(act, o_up, j, k - 2)
                        nc.scalar.activation(et_hi[:, (k - 1) % 2, :], turned, ACT.Copy).then_inc(t_hi, 1)
                    if live(j, k, NT):
                        wait(act, sub_s, j, k + 1)
                        wait(act, t_up, j, k - 1)
                        nc.scalar.activation(e[:, k % 2, :], z[:, k % 2, :], ACT.Exp, scale=SC).then_inc(exp_s, 1)
                    if live(j, k - 3, NT):
                        wait(act, w_up, j, k - 2)
                        nc.scalar.activation(wT[:, bass.ds(j * (2 * P) + (k - 3) * P, P)], ps[:, 7, 0:P], ACT.Copy)\
                            .then_inc(w_out, 1)
                pipeline(act, NT, 3, step)

            @block.vector
            def _(dve):
                def step(j, k):
                    if live(j, k, NT):
                        q = k % 2
                        wait(dve, g_up, j, k + 1)
                        g3 = ps[:, 2 * q:2 * q + 2, :].rearrange("p a (c n) -> p (a c) n", n=L)
                        nc.vector.tensor_reduce(mx[:, q, :], g3, AX.X, ALU.max).then_inc(mx_s, 1)
                        wait(dve, mx_s, j, k + 1)
                        wait(dve, exp_s, j, k - 1)
                        nc.vector.tensor_tensor(z[:, q, :].rearrange("p (c n) -> p c n", n=L), g3,
                                                mx[:, q, :].unsqueeze(2).broadcast_to([P, H, L]), ALU.subtract)\
                            .then_inc(sub_s, 1)
                    if live(j, k - 1, NT):
                        q = (k - 1) % 2
                        wait(dve, t_hi, j, k)
                        nc.vector.tensor_tensor(et_lo[:, q, :], turned, et_hi[:, q, :], ALU.subtract).then_inc(t_lo, 1)
                    if live(j, k - 2, NT):
                        q = k % 2
                        mix = ps[:, 6, 0:NP * VW].rearrange("p (c v) -> p c v", c=NP)
                        wait(dve, o_up, j, k - 1)
                        nc.vector.reciprocal(rec[:, q], mix[:, :, 2 * D:VW]).then_inc(rec_s, 1)
                        wait(dve, rec_s, j, k - 1)
                        wait(dve, w_up, j, k - 3)
                        nc.vector.tensor_tensor(row[:, q, :].rearrange("p (c h d) -> p c h d", c=NP, h=2),
                                                mix[:, :, 0:2 * D].rearrange("p c (h d) -> p c h d", h=2),
                                                rec[:, q].unsqueeze(3).broadcast_to([P, NP, 2, D]), ALU.mult)\
                            .then_inc(row_s, 1)
                pipeline(dve, NT, 2, step)

        wp_s, y_up = S.sems.new("ld_parts", "ld_y_up")
        with (nc.sbuf_tensor("ld_hi", [P, N], F16) as wt_hi,
              nc.sbuf_tensor("ld_lo", [P, N], F16) as wt_lo,
              nc.Block(no_gpsimd_drain=True) as block):

            @block.vector
            def _(dve):
                split_on(dve, wp_s, 1, wt_hi[:], wt_lo[:], wT[:]).then_inc(wp_s, 1)
                for n in range(NQ):
                    cut = slice(n * QW, (n + 1) * QW)
                    dve.wait_ge(y_up, n + 1)
                    nc.vector.tensor_tensor(S.rT[:, cut], S.xT[:, cut], ps[:, n, :], ALU.add)

            @block.tensor
            def _(pe):
                pe.wait_ge(wp_s, 2)
                for n in range(NQ):
                    cut = slice(n * QW, (n + 1) * QW)
                    products(nc, ps[:, n, :], W_P, (wt_hi[:, cut], wt_lo[:, cut])).then_inc(y_up, 1)


def l2_attn(nc, S, A):
    H, DK, DV = 4, 32, 64
    HV = H * DV
    TB = T // P
    PAIRS = 3 * P
    ps = S.psum
    WN = 2 * P + 2 * HV + H
    with ExitStack() as ctx:
        def sb(name, shape, dt):
            return ctx.enter_context(nc.sbuf_tensor(name, shape, dt))

        q_hi = sb("lg_qhi", [P, H, N], F16)
        q_lo = sb("lg_qlo", [P, H, N], F16)
        k_hi = sb("lg_khi", [P, N], F16)
        k_lo = sb("lg_klo", [P, N], F16)
        v_hi = sb("lg_vhi", [P, NT, HV], F16)
        v_lo = sb("lg_vlo", [P, NT, HV], F16)
        gate = sb("lg_gate", [P, NT, HV], F32)
        og = sb("lg_og", [P, NT, HV], F32)
        sq = sb("lg_sq", [P, 2, TB * HV], F32)
        ms = sb("lg_ms", [P, NT, H], F32)
        g_hi = sb("lg_ghi", [P, B, TB, H], F16)
        g_lo = sb("lg_glo", [P, B, TB, H], F16)
        G = sb("lg_G", [P, TB, B, H], F32)
        wo = sb("lg_wo", [P, 2, P], F32)
        wo_hi = sb("lg_wohi", [P, 2, P], F16)
        wo_lo = sb("lg_wolo", [P, 2, P], F16)
        norm_w = sb("lg_norm", [P, 1], F32)
        tri = sb("lg_tri", [P, 2 * PAIRS], F16)
        mask = sb("lg_mask", [P, PAIRS], BF16)

        got, zero_s, parts_s, qk_up, qk_hi, qk_lo, v_up, v_high, v_done, z_s, e_s, log_s, cum_s = S.sems.new(
            *(f"lg_{n}" for n in ("got", "zero", "parts", "qk_up", "qk_hi", "qk_lo", "v_up", "v_high", "v_done", "z",
                                  "e", "log", "cum")))
        with (nc.sbuf_tensor("lg_w", [P, WN], F32) as w,
              nc.sbuf_tensor("lg_whi", [P, WN], F16) as w_hi,
              nc.sbuf_tensor("lg_wlo", [P, WN], F16) as w_lo,
              nc.sbuf_tensor("lg_bgk", [P, H], F32) as bgk,
              nc.sbuf_tensor("lg_z", [P, NT, H], F32) as z,
              nc.sbuf_tensor("lg_abs", [P, NT, H], F32) as za,
              nc.sbuf_tensor("lg_e", [P, NT, H], F32) as e,
              nc.sbuf_tensor("lg_l", [P, NT, H], F32) as lg,
              nc.Block(no_gpsimd_drain=True) as block):

            def cols(a, n):
                return w_hi[:, a:a + n], w_lo[:, a:a + n]

            W_Q, W_K, W_V, W_G = cols(0, P), cols(P, P), cols(2 * P, HV + H), cols(2 * P + HV + H, HV)

            @block.sync
            def _(sp):
                for dst, src in ((w[:], "lg_w"), (bgk[:], "lg_bgk"), (wo[:], "lg_wo"), (norm_w[:], "lg_norm"),
                                 (tri[:], "lg_tri"), (mask[:], "lg_mask")):
                    sp.dma_start(dst, A[src]).then_inc(got, 16)
                sp.wait_ge(got, 96)

            @block.gpsimd
            def _(pool):
                nc.gpsimd.memset(q_hi[:].rearrange("p h n -> p (h n)").bitcast(F32), 0.0).then_inc(zero_s, 1)
                nc.gpsimd.memset(q_lo[:].rearrange("p h n -> p (h n)").bitcast(F32), 0.0).then_inc(zero_s, 1)

            @block.tensor
            def _(pe):
                pe.wait_ge(parts_s, 2)
                for n in range(NQ):
                    x = [t[:, n * QW:(n + 1) * QW] for t in (S.x_hi, S.x_lo)]
                    products(nc, ps[:, n, :], W_Q, x)
                    products(nc, ps[:, 4 + n, :], W_K, x).then_inc(qk_up, 1)
                for i in range(NT):
                    x = [t[:, i * P:(i + 1) * P] for t in (S.x_hi, S.x_lo)]
                    a = 2 * (i % 4)
                    if i < 4:
                        pe.wait_ge(qk_lo, NQ)
                    else:
                        pe.wait_ge(v_done, i - 3)
                    products(nc, ps[:, a, 0:HV + H], x, W_V)
                    products(nc, ps[:, a + 1, 0:HV], x, W_G).then_inc(v_up, 1)
                pe.wait_ge(log_s, 6)
                g2 = [t[:].rearrange("p b a h -> p a b h") for t in (g_hi, g_lo)]
                for a in range(TB):
                    out = ps[:, a, 0:B * H].rearrange("p (b h) -> p b h", b=B)
                    terms = [(tri[:, 0:P], a)] + [(tri[:, P:2 * P], 0)] * a
                    for m, (lhs, src) in enumerate(terms):
                        for n, g in enumerate(g2):
                            last = nc.tensor.matmul(out, lhs, g[:, src], start=(m == n == 0),
                                                    stop=(m == len(terms) - 1 and n == 1))
                last.then_inc(cum_s, 1)

            @block.scalar
            def _(act):
                act.wait_ge(zero_s, 2)
                for n in range(NQ):
                    cut = slice(n * QW, (n + 1) * QW)
                    act.wait_ge(qk_up, n + 1)
                    for h in range(H):
                        r = slice(h * DK, (h + 1) * DK)
                        nc.scalar.activation(q_hi[r, h, cut], ps[r, n, :], ACT.Copy)
                    nc.scalar.activation(k_hi[:, cut], ps[:, 4 + n, :], ACT.Copy).then_inc(qk_hi, 1)
                for i in range(NT):
                    act.wait_ge(v_up, i + 1)
                    a = 2 * (i % 4)
                    nc.scalar.activation(v_hi[:, i, :], ps[:, a, 0:HV], ACT.Copy)
                    nc.scalar.activation(gate[:, i, :], ps[:, a + 1, 0:HV], ACT.Silu).then_inc(v_high, 1)
                act.wait_ge(z_s, 1)
                nc.scalar.activation(e[:], za[:], ACT.Exp).then_inc(e_s, 1)
                act.wait_ge(e_s, 1)
                nc.scalar.activation(lg[:], e[:], ACT.Ln, bias=S.one).then_inc(e_s, 1)

            @block.vector
            def _(dve):
                dve.wait_ge(got, 96)
                split_on(dve, parts_s, 1, w_hi[:], w_lo[:], w[:]).then_inc(parts_s, 1)
                nc.vector.tensor_scalar(wo[:], wo[:], norm_w[:, 0:1], None, ALU.mult).then_inc(log_s, 1)
                dve.wait_ge(log_s, 1)
                split_on(dve, log_s, 2, wo_hi[:], wo_lo[:], wo[:])
                for n in range(NQ):
                    cut = slice(n * QW, (n + 1) * QW)
                    dve.wait_ge(qk_hi, n + 1)
                    for h in range(H):
                        r = slice(h * DK, (h + 1) * DK)
                        nc.vector.tensor_tensor(q_lo[r, h, cut], ps[r, n, :], q_hi[r, h, cut], ALU.subtract)
                    nc.vector.tensor_tensor(k_lo[:, cut], ps[:, 4 + n, :], k_hi[:, cut], ALU.subtract).then_inc(qk_lo, 1)
                for i in range(NT):
                    a = 2 * (i % 4)
                    dve.wait_ge(v_high, i + 1)
                    nc.vector.tensor_tensor(z[:, i, :], ps[:, a, HV:HV + H], bgk[:], ALU.add)
                    nc.vector.tensor_tensor(v_lo[:, i, :], ps[:, a, 0:HV], v_hi[:, i, :], ALU.subtract).then_inc(v_done, 1)
                dve.wait_ge(v_done, NT)
                nc.vector.scalar_tensor_tensor(out=za[:], in0=z[:], scalar=-1.0, in1=z[:], op0=ALU.mult,
                                               op1=ALU.min).then_inc(z_s, 1)
                dve.wait_ge(z_s, 1)
                nc.vector.tensor_scalar(z[:], z[:], 0.0, None, ALU.min).then_inc(z_s, 1)
                dve.wait_ge(z_s, 2)
                dve.wait_ge(e_s, 2)
                nc.vector.tensor_tensor(z[:], z[:], lg[:], ALU.subtract).then_inc(log_s, 1)
                dve.wait_ge(log_s, 3)
                nc.vector.tensor_scalar(z[:], z[:], 1.0 / 16, None, ALU.mult).then_inc(log_s, 1)
                dve.wait_ge(log_s, 4)
                flat = [t[:].rearrange("p b a h -> p (b a) h") for t in (g_hi, g_lo)]
                split_on(dve, log_s, 5, flat[0], flat[1], z[:]).then_inc(log_s, 1)
                dve.wait_ge(cum_s, 1)
                for a in range(TB):
                    nc.vector.tensor_copy(G[:, a].rearrange("p b h -> p (b h)"), ps[:, a, 0:B * H])

        gs_up, sc_up, dec_s, exp_s, at_s, hi_s, lo_s, o_up, sq_s, og_s = S.sems.new(
            *(f"lh_{n}" for n in ("gs_up", "sc_up", "dec", "exp", "at", "hi", "lo", "o_up", "sq", "og")))
        U = 2 * H
        with (nc.sbuf_tensor("lh_dec", [P, 2, PAIRS], F32) as dec,
              nc.sbuf_tensor("lh_d", [P, 2, PAIRS], F32) as d,
              nc.sbuf_tensor("lh_at", [P, 2, PAIRS], F32) as at,
              nc.sbuf_tensor("lh_athi", [P, 4, PAIRS], F16) as at_hi,
              nc.sbuf_tensor("lh_atlo", [P, 4, PAIRS], F16) as at_lo,
              nc.Block(no_gpsimd_drain=True) as block):

            @block.tensor
            def _(pe):
                def step(j, k):
                    if live(j, k, B * H):
                        seq, h = j * 2 + k // H, k % H
                        decay, score = ps[:, k % 2, 0:PAIRS], ps[:, 2 + k % 2, :]
                        wait(pe, dec_s, j, k - 1, U)
                        nc.tensor.matmul(decay, S.identb[:], mask[:], start=True, stop=False, skip_group_check=True)
                        for a in range(TB):
                            for n, g in enumerate((g_hi, g_lo)):
                                col = g[:, bass.ds(seq, 1), a, h:h + 1].rearrange("p b h -> p (b h)").broadcast_to([P, P])
                                last = nc.tensor.matmul(decay[:, a * P:PAIRS], col,
                                                        tri[:, a * PAIRS + a * P:(a + 1) * PAIRS],
                                                        start=False, stop=(a == n == 1), skip_group_check=True)
                        last.then_inc(gs_up, 1)
                        wait(pe, at_s, j, k - 1, U)
                        for a in range(TB):
                            lhs = [t[:, bass.ds(seq * T + a * P, P)] for t in (k_hi, k_lo)]
                            rhs = [t[:, h, bass.ds(seq * T + a * P, T - a * P)] for t in (q_hi, q_lo)]
                            last = products(nc, score[:, a * T:a * T + T - a * P], lhs, rhs)
                        last.then_inc(sc_up, 1)
                    if live(j, k - 3, B * H):
                        seq, h, c = j * 2 + (k - 3) // H, (k - 3) % H, (k - 3) % 4
                        wait(pe, lo_s, j, k - 2, U)
                        if h == 0:
                            wait(pe, og_s, j, (k - 3) // H - 1, 2)
                        bank = ps[:, 4 + ((k - 3) // H) % 2, :]
                        for a, terms in enumerate((((0, 0),), ((1, 0), (2, 1)))):
                            out = bank[:, (a * H + h) * DV:(a * H + h + 1) * DV]
                            for m, (pair, src) in enumerate(terms):
                                lhs = [t[:, c, pair * P:(pair + 1) * P] for t in (at_hi, at_lo)]
                                rhs = [t[:, bass.ds(seq * TB + src, 1), h * DV:(h + 1) * DV]
                                       .rearrange("p i v -> p (i v)") for t in (v_hi, v_lo)]
                                last = products(nc, out, lhs, rhs, first=(m == 0), last=(m == len(terms) - 1))
                        last.then_inc(o_up, 1)
                pipeline(pe, B * H, 3, step, U)

            @block.scalar
            def _(act):
                def step(j, k):
                    if live(j, k, B * H):
                        wait(act, dec_s, j, k + 1, U)
                        wait(act, at_s, j, k - 1, U)
                        nc.scalar.activation(d[:, k % 2, :], dec[:, k % 2, :], ACT.Exp).then_inc(exp_s, 1)
                    if live(j, k - 1, B * H):
                        wait(act, at_s, j, k, U)
                        wait(act, o_up, j, k - 4, U)
                        nc.scalar.activation(at_hi[:, (k - 1) % 4, :], at[:, (k - 1) % 2, :], ACT.Copy).then_inc(hi_s, 1)
                    if k % H == 3 and live(j, k - 4, B * H):
                        b = (k - 4) // H
                        wait(act, o_up, j, H * (b + 1), U)
                        wait(act, og_s, j, b - 1, 2)
                        nc.scalar.activation(sq[:, b % 2, :], ps[:, 4 + b % 2, :], ACT.Square).then_inc(sq_s, 1)
                pipeline(act, B * H, 4, step, U)

            @block.vector
            def _(dve):
                def step(j, k):
                    if live(j, k, B * H):
                        wait(dve, gs_up, j, k + 1, U)
                        wait(dve, exp_s, j, k - 1, U)
                        seq, h = j * 2 + k // H, k % H
                        for a, (lo, hi) in enumerate(((0, T), (T, PAIRS))):
                            mine = G[:, a, bass.ds(seq, 1), h:h + 1].rearrange("p b h -> p (b h)")
                            last = nc.vector.tensor_scalar(dec[:, k % 2, lo:hi], ps[:, k % 2, lo:hi], mine, 0.0,
                                                           ALU.subtract, ALU.min)
                        last.then_inc(dec_s, 1)
                    if live(j, k - 1, B * H):
                        c = (k - 1) % 2
                        wait(dve, exp_s, j, k, U)
                        wait(dve, sc_up, j, k, U)
                        wait(dve, lo_s, j, k - 2, U)
                        nc.vector.scalar_tensor_tensor(out=at[:, c, :], in0=ps[:, 2 + c, 0:PAIRS], scalar=DK ** -0.5,
                                                       in1=d[:, c, :], op0=ALU.mult, op1=ALU.mult).then_inc(at_s, 1)
                    if live(j, k - 2, B * H):
                        wait(dve, hi_s, j, k - 1, U)
                        nc.vector.tensor_tensor(at_lo[:, (k - 2) % 4, :], at[:, k % 2, :], at_hi[:, (k - 2) % 4, :],
                                                ALU.subtract).then_inc(lo_s, 1)
                    if k % H == 3 and live(j, k - 4, B * H):
                        b = (k - 4) // H
                        wait(dve, sq_s, j, b + 1, 2)
                        two = bass.ds(j * (2 * TB) + b * TB, TB)
                        nc.vector.tensor_reduce(ms[:, two, :].rearrange("p i h -> p (i h)"),
                                                sq[:, b % 2, :].rearrange("p (i v) -> p i v", v=DV), AX.X, ALU.add)
                        nc.vector.tensor_tensor(og[:, two, :].rearrange("p i v -> p (i v)"), ps[:, 4 + b % 2, :],
                                                gate[:, two, :].rearrange("p i v -> p (i v)"), ALU.mult).then_inc(og_s, 1)
                pipeline(dve, B * H, 4, step, U)

        sd_s, rs_s, on_s, t_up, t_hi, t_lo, y_up = S.sems.new(
            *(f"li_{n}" for n in ("std", "rstd", "on", "t_up", "t_hi", "t_lo", "y_up")))
        with (nc.sbuf_tensor("li_sd", [P, NT, H], F32) as sd,
              nc.sbuf_tensor("li_rs", [P, NT, H], F32) as rs,
              nc.sbuf_tensor("li_hi", [P, NQ, 2, QW], F16) as on_hi,
              nc.sbuf_tensor("li_lo", [P, NQ, 2, QW], F16) as on_lo,
              nc.Block(no_gpsimd_drain=True) as block):

            @block.scalar
            def _(act):
                nc.scalar.activation(sd[:], ms[:], ACT.Sqrt, bias=S.eps_ap(1e-5), scale=1.0 / DV).then_inc(sd_s, 1)
                for n in range(NQ):
                    act.wait_ge(t_up, n + 1)
                    nc.scalar.activation(on_hi[:, n], ps[:, 2 * (n % 2):2 * (n % 2) + 2, :], ACT.Copy).then_inc(t_hi, 1)

            @block.vector
            def _(dve):
                dve.wait_ge(sd_s, 1)
                nc.vector.reciprocal(rs[:], sd[:]).then_inc(rs_s, 1)
                dve.wait_ge(rs_s, 1)
                for n in range(NQ):
                    four = slice(4 * n, 4 * n + 4)
                    o4 = og[:, four, :].rearrange("p i (h v) -> p (i h) v", h=H)
                    nc.vector.tensor_tensor(o4, o4, rs[:, four, :].rearrange("p i h -> p (i h)").unsqueeze(2)
                                            .broadcast_to([P, 4 * H, DV]), ALU.mult).then_inc(on_s, 1)
                for n in range(NQ):
                    dve.wait_ge(t_hi, n + 1)
                    nc.vector.tensor_tensor(on_lo[:, n], ps[:, 2 * (n % 2):2 * (n % 2) + 2, :], on_hi[:, n],
                                            ALU.subtract).then_inc(t_lo, 1)
                for n in range(NQ):
                    cut = slice(n * QW, (n + 1) * QW)
                    dve.wait_ge(y_up, n + 1)
                    nc.vector.tensor_tensor(S.rT[:, cut], S.xT[:, cut], ps[:, 4 + n, :], ALU.add)

            @block.tensor
            def _(pe):
                for n in range(NQ):
                    pe.wait_ge(on_s, n + 1)
                    if n >= 2:
                        pe.wait_ge(t_lo, n - 1)
                    for m in range(2):
                        for i in range(4):
                            last = nc.tensor.transpose(ps[:, 2 * (n % 2) + m, i * P:(i + 1) * P],
                                                       og[:, 4 * n + i, m * P:(m + 1) * P], S.ident[:])
                    last.then_inc(t_up, 1)
                for n in range(NQ):
                    pe.wait_ge(t_lo, n + 1)
                    for m in range(2):
                        last = products(nc, ps[:, 4 + n, :], (wo_hi[:, m, :], wo_lo[:, m, :]),
                                        (on_hi[:, n, m, :], on_lo[:, n, m, :]), first=(m == 0), last=(m == 1))
                    last.then_inc(y_up, 1)


def l3_attn(nc, S, A):
    DEPTH = A["lj_w"].shape[0]
    H, DH, FF = 8, 16, 4
    ps = S.psum
    WN = (4 + 2 * FF) * P
    with ExitStack() as ctx:
        def sb(name, shape, dt):
            return ctx.enter_context(nc.sbuf_tensor(name, shape, dt))

        x0 = sb("lj_x0", [P, N], F32)
        cols = sb("lj_cols", [P, DEPTH, 5], F32)
        own = sb("lj_own", [P, P], F32)
        w = sb("lj_w", [P, WN], F32)
        w_hi, w_lo = sb("lj_whi", [P, WN], F16), sb("lj_wlo", [P, WN], F16)
        W = [(w_hi[:, n * P:(n + 1) * P], w_lo[:, n * P:(n + 1) * P]) for n in range(4 + 2 * FF)]
        W_Q, W_K, W_V = W[:3]
        W_O = w[:, 3 * P:4 * P]

        got = S.sems.new("lj_got")
        with nc.Block(no_gpsimd_drain=True) as block:

            @block.sync
            def _(sp):
                sp.dma_start(cols[:], A["lj_cols"]).then_inc(got, 16)
                sp.dma_start(own[:], A["lj_own"]).then_inc(got, 16)
                sp.wait_ge(got, 32)

            @block.vector
            def _(dve):
                nc.vector.tensor_copy(x0[:], S.xT[:])

        first = len(S.sems.held)
        with nc.Fori(0, DEPTH) as layer:
            def column(n):
                return cols[:, bass.ds(layer, 1), n:n + 1].rearrange("p l c -> p (l c)")

            w_got, w_high = S.sems.new("lj_w_got", "lj_w_high")

            def load_weights(sp):
                sp.dma_start(w[:], A["lj_w"][bass.ds(layer, 1)].rearrange("l p n -> p (l n)")).then_inc(w_got, 16)
                sp.wait_ge(w_got, 16)

            def split_weights(pool):
                pool.wait_ge(w_got, 16)
                nc.gpsimd.tensor_copy(w_hi[:], w[:]).then_inc(w_high, 1)
                pool.wait_ge(w_high, 1)
                nc.gpsimd.tensor_tensor(w_lo[:], w[:], w_hi[:], ALU.subtract).then_inc(w_high, 1)
                pool.wait_ge(w_high, 2)

            layernorm_phase(nc, S, S.xT, S.rT, gain=column(0), shift=column(1), sync=load_weights, pool=split_weights)
            linear_attention(nc, S, W_Q, W_K, W_V, W_O, own, column(2), H, DH)
            layernorm_phase(nc, S, S.xT, S.rT, gain=column(3), shift=column(4))
            leaky_network(nc, S, W[4:4 + FF], W[4 + FF:])
            S.sems.clear(first)

        with nc.Block(no_gpsimd_drain=True) as block:

            @block.vector
            def _(dve):
                nc.vector.tensor_tensor(S.rT[:], S.xT[:], x0[:], ALU.add)


def linear_attention(nc, S, W_Q, W_K, W_V, W_O, own, b_o, H, DH):
    ps = S.psum
    k_up, k_max, k_exp, q_up, q_max, q_sub, q_exp, q_sum, q_rec, q_on, v_up, v_on = S.sems.new(
        *(f"lk_{n}" for n in ("k_up", "k_max", "k_exp", "q_up", "q_max", "q_sub", "q_exp", "q_sum", "q_rec", "q_on",
                              "v_up", "v_on")))
    kt_up, kt_on, c_up, c_on, qt_up, qt_on, w_up, k_rec, w_on, y_up = S.sems.new(
        *(f"ll_{n}" for n in ("kt_up", "kt_on", "c_up", "c_on", "qt_up", "qt_on", "w_up", "k_rec", "w_on", "y_up")))
    TB = T // P
    with ExitStack() as ctx:
        def sb(name, shape, dt):
            return ctx.enter_context(nc.sbuf_tensor(name, shape, dt))

        ke, q = sb("lk_ke", [P, N], F32), sb("lk_q", [P, NT * H, DH], F32)
        neg_max, k_sum, rec = sb("lk_nm", [P, B], F32), sb("lk_ks", [P, B], F32), sb("lk_rec", [P, B], F32)
        qm, qs, qr = sb("lk_qm", [P, NT * H], F32), sb("lk_qs", [P, NT * H], F32), sb("lk_qr", [P, NT * H], F32)
        v, kr, qt = sb("lk_v", [P, N], F32), sb("lk_kr", [P, N], F32), sb("lk_qt", [P, N], F32)
        c, cw = sb("lk_c", [P, B * P], F32), sb("lk_cw", [P, B * P], F32)
        block = ctx.enter_context(nc.Block(no_gpsimd_drain=True))
        x = (S.x_hi, S.x_lo)

        def cut(pair, n, width=QW):
            return tuple(t[:, n * width:(n + 1) * width] for t in pair)

        @block.tensor
        def _(pe):
            for n in range(NQ):
                products(nc, ps[:, n, :], W_K, cut(x, n)).then_inc(k_up, 1)
            for i in range(NT):
                last = products(nc, ps[:, 4 + i // 4, i % 4 * P:(i % 4 + 1) * P], cut(x, i, P), W_Q)
                if i % 4 == 3:
                    last.then_inc(q_up, 1)
            for i in range(NT):
                if i % 4 == 0:
                    pe.wait_ge(k_exp, 2 * (i // 4) + 2)
                last = products(nc, ps[:, i // 4, i % 4 * P:(i % 4 + 1) * P], cut(x, i, P), W_V)
                if i % 4 == 3:
                    last.then_inc(v_up, 1)
            for i in range(NT):
                if i % 4 == 0:
                    pe.wait_ge(q_sub, i // 4 + 1)
                last = nc.tensor.transpose(ps[:, 4 + i // 4, i % 4 * P:(i % 4 + 1) * P], ke[:, i * P:(i + 1) * P], S.ident[:])
                if i % 4 == 3:
                    last.then_inc(kt_up, 1)
            for b in range(B):
                if b == 0:
                    pe.wait_ge(v_on, NQ)
                if b % 2 == 0:
                    pe.wait_ge(kt_on, b // 2 + 1)
                for a in range(TB):
                    rows = slice((TB * b + a) * P, (TB * b + a + 1) * P)
                    last = nc.tensor.matmul(ps[:, b // 4, b % 4 * P:(b % 4 + 1) * P], v[:, rows], kr[:, rows],
                                            start=(a == 0), stop=(a == TB - 1))
                if b % 4 == 3:
                    last.then_inc(c_up, 1)
            for i in range(NT):
                if i % 4 == 0:
                    pe.wait_ge(q_on, i // 4 + 1)
                last = nc.tensor.transpose(ps[:, 4 + i // 4, i % 4 * P:(i % 4 + 1) * P],
                                           q[:, i * H:(i + 1) * H, :].rearrange("p h d -> p (h d)"), S.ident[:])
                if i % 4 == 3:
                    last.then_inc(qt_up, 1)
            for b in range(B):
                pe.wait_ge(c_on, b // 4 + 1)
                last = nc.tensor.matmul(ps[:, 2 + b // 4, b % 4 * P:(b % 4 + 1) * P], c[:, b * P:(b + 1) * P], W_O)
                if b % 4 == 3:
                    last.then_inc(w_up, 1)
            for b in range(B):
                if b % 4 == 0:
                    pe.wait_ge(w_on, b // 4 + 1)
                if b % 2 == 0:
                    pe.wait_ge(qt_on, b // 2 + 1)
                last = nc.tensor.matmul(ps[:, 4 + b // 2, b % 2 * T:(b % 2 + 1) * T], cw[:, b * P:(b + 1) * P],
                                        qt[:, b * T:(b + 1) * T])
                if b % 2:
                    last.then_inc(y_up, 1)

        @block.scalar
        def _(act):
            for b in range(B):
                act.wait_ge(k_max, b // 2 + 1)
                nc.scalar.activation(ke[:, b * T:(b + 1) * T], ps[:, b // 2, b % 2 * T:(b % 2 + 1) * T], ACT.Exp,
                                     bias=neg_max[:, b:b + 1], accum_out=k_sum[:, b:b + 1]).then_inc(k_exp, 1)
            for n in range(NQ):
                g = slice(n * 4 * H, (n + 1) * 4 * H)
                act.wait_ge(q_sub, n + 1)
                nc.scalar.activation(q[:, g, :], q[:, g, :], ACT.Exp).then_inc(q_exp, 1)
            for n in range(NQ):
                act.wait_ge(v_up, n + 1)
                nc.scalar.activation(v[:, n * QW:(n + 1) * QW], ps[:, n, :], ACT.Copy).then_inc(v_on, 1)
            for n in range(NQ):
                act.wait_ge(kt_up, n + 1)
                nc.scalar.activation(kr[:, n * QW:(n + 1) * QW], ps[:, 4 + n, :], ACT.Copy).then_inc(kt_on, 1)
            for n in range(NQ):
                act.wait_ge(qt_up, n + 1)
                nc.scalar.activation(qt[:, n * QW:(n + 1) * QW], ps[:, 4 + n, :], ACT.Copy).then_inc(qt_on, 1)

        @block.vector
        def _(dve):
            for n in range(NQ):
                dve.wait_ge(k_up, n + 1)
                nc.vector.tensor_reduce(neg_max[:, 2 * n:2 * n + 2], ps[:, n, :].rearrange("p (b t) -> p b t", b=2), AX.X,
                                        ALU.max, negate=True).then_inc(k_max, 1)
            for n in range(NQ):
                g = slice(n * 4 * H, (n + 1) * 4 * H)
                rows = ps[:, 4 + n, :].rearrange("p (g d) -> p g d", d=DH)
                dve.wait_ge(q_up, n + 1)
                nc.vector.tensor_reduce(qm[:, g], rows, AX.X, ALU.max).then_inc(q_max, 1)
                dve.wait_ge(q_max, n + 1)
                nc.vector.tensor_tensor(q[:, g, :], rows, qm[:, g].unsqueeze(2).broadcast_to([P, 4 * H, DH]), ALU.subtract)\
                    .then_inc(q_sub, 1)
            dve.wait_ge(q_exp, NQ)
            nc.vector.tensor_reduce(qs[:], q[:], AX.X, ALU.add).then_inc(q_sum, 1)
            dve.wait_ge(q_sum, 1)
            nc.vector.reciprocal(qr[:], qs[:]).then_inc(q_rec, 1)
            dve.wait_ge(q_rec, 1)
            for n in range(NQ):
                g = slice(n * 4 * H, (n + 1) * 4 * H)
                nc.vector.tensor_tensor(q[:, g, :], q[:, g, :], qr[:, g].unsqueeze(2).broadcast_to([P, 4 * H, DH]),
                                        ALU.mult).then_inc(q_on, 1)
            dve.wait_ge(k_exp, B)
            nc.vector.reciprocal(rec[:], k_sum[:]).then_inc(k_rec, 1)
            for m in range(2):
                dve.wait_ge(c_up, m + 1)
                nc.vector.tensor_tensor(c[:, m * QW:(m + 1) * QW].rearrange("p (b d) -> p b d", b=4),
                                        ps[:, m, :].rearrange("p (b d) -> p b d", b=4),
                                        own[:].unsqueeze(1).broadcast_to([P, 4, P]), ALU.mult).then_inc(c_on, 1)
            dve.wait_ge(k_rec, 1)
            for m in range(2):
                dve.wait_ge(w_up, m + 1)
                nc.vector.tensor_tensor(cw[:, m * QW:(m + 1) * QW].rearrange("p (b d) -> p b d", b=4),
                                               ps[:, 2 + m, :].rearrange("p (b d) -> p b d", b=4),
                                               rec[:, 4 * m:4 * m + 4].unsqueeze(2).broadcast_to([P, 4, P]), ALU.mult).then_inc(w_on, 1)
            for n in range(NQ):
                run = slice(n * QW, (n + 1) * QW)
                dve.wait_ge(y_up, n + 1)
                nc.vector.scalar_tensor_tensor(out=S.xT[:, run], in0=ps[:, 4 + n, :], scalar=b_o, in1=S.xT[:, run],
                                               op0=ALU.add, op1=ALU.add)


def leaky_network(nc, S, W1, W2):
    ps = S.psum
    FF = len(W1)
    M = NQ * FF
    LAG = 3
    up, slope_s, leaky_s, hi_s, lo_s, down_s = S.sems.new(
        *(f"lm_{n}" for n in ("up", "slope", "leaky", "hi", "lo", "down")))
    with (nc.sbuf_tensor("lm_slope", [P, 2, QW], F32) as slope,
          nc.sbuf_tensor("lm_h", [P, 4, QW], F32) as h,
          nc.sbuf_tensor("lm_hhi", [P, 4, QW], F16) as h_hi,
          nc.sbuf_tensor("lm_hlo", [P, 4, QW], F16) as h_lo,
          nc.Block(no_gpsimd_drain=True) as block):

        @block.tensor
        def _(pe):
            for k in range(M + LAG):
                if k < M:
                    cut = slice(k // FF * QW, (k // FF + 1) * QW)
                    if k >= 4:
                        pe.wait_ge(leaky_s, k - 3)
                    products(nc, ps[:, 4 + k % 4, :], W1[k % FF], (S.x_hi[:, cut], S.x_lo[:, cut])).then_inc(up, 1)
                if k >= LAG:
                    i = k - LAG
                    pe.wait_ge(lo_s, i + 1)
                    last = products(nc, ps[:, i // FF, :], W2[i % FF], (h_hi[:, i % 4, :], h_lo[:, i % 4, :]),
                                    first=(i % FF == 0), last=(i % FF == FF - 1))
                    last.then_inc(down_s, 1)

        @block.scalar
        def _(act):
            for k in range(M + 1):
                if k < M:
                    act.wait_ge(up, k + 1)
                    if k >= 2:
                        act.wait_ge(leaky_s, k - 1)
                    nc.scalar.activation(slope[:, k % 2, :], ps[:, 4 + k % 4, :], ACT.Copy, scale=0.01).then_inc(slope_s, 1)
                if k >= 1:
                    i = k - 1
                    act.wait_ge(leaky_s, i + 1)
                    if i >= 4:
                        act.wait_ge(down_s, i - 3)
                    nc.scalar.activation(h_hi[:, i % 4, :], h[:, i % 4, :], ACT.Copy).then_inc(hi_s, 1)

        @block.vector
        def _(dve):
            for k in range(M + 1):
                if k < M:
                    dve.wait_ge(slope_s, k + 1)
                    if k >= 4:
                        dve.wait_ge(lo_s, k - 3)
                    nc.vector.tensor_tensor(h[:, k % 4, :], ps[:, 4 + k % 4, :], slope[:, k % 2, :], ALU.max)\
                        .then_inc(leaky_s, 1)
                if k >= 1:
                    i = k - 1
                    dve.wait_ge(hi_s, i + 1)
                    nc.vector.tensor_tensor(h_lo[:, i % 4, :], h[:, i % 4, :], h_hi[:, i % 4, :], ALU.subtract)\
                        .then_inc(lo_s, 1)
            for n in range(NQ):
                cut = slice(n * QW, (n + 1) * QW)
                dve.wait_ge(down_s, FF * (n + 1))
                nc.vector.tensor_tensor(S.xT[:, cut], S.xT[:, cut], ps[:, n, :], ALU.add)


def l3_ffn(nc, S, A):
    H, DH, E = 8, 16, 4
    HG, QT = H // 4, T // E
    TB = T // P
    SC = C ** -0.5
    ps = S.psum
    WN = (2 * HG + 2) * E * P
    UN = B * H
    R = 2 * H
    with ExitStack() as ctx:
        def sb(name, shape, dt):
            return ctx.enter_context(nc.sbuf_tensor(name, shape, dt))

        w = sb("lq_w", [P, WN], F32)
        w_hi, w_lo = sb("lq_whi", [P, WN], F16), sb("lq_wlo", [P, WN], F16)
        cols = sb("lq_cols", [P, 2 + 2 * HG + E], F32)
        v_b = sb("lq_vb", [P, P], F32)
        x2 = sb("lq_x2", [P, N], F32)
        q32, k32, v32 = (sb(f"lq_{n}32", [P, 2 * T], F32) for n in "qkv")
        q_hi, q_lo, k_hi, k_lo, v_hi, v_lo = (sb(f"lq_{n}", [P, 2, 2 * T], F16) for n in ("qhi", "qlo", "khi", "klo", "vhi", "vlo"))
        neg = sb("lq_neg", [P, 4, TB], F32)
        sums = sb("lq_sums", [P, 2, TB, H], F32)
        rec = sb("lq_rec", [P, TB, H], F32)
        e = sb("lq_e", [P, 2, TB * T], F32)
        p_hi, p_lo = sb("lq_phi", [P, 4, TB * T], F16), sb("lq_plo", [P, 4, TB * T], F16)
        rows = sb("lq_rows", [P, TB, P], F32)
        o_hi, o_lo = sb("lq_ohi", [P, T], F16), sb("lq_olo", [P, T], F16)

        w_got, w_s = S.sems.new("lq_got", "lq_w_parts")

        def load(sp):
            sp.dma_start(cols[:], A["lq_cols"]).then_inc(w_got, 16)
            sp.dma_start(w[:], A["lq_w"]).then_inc(w_got, 16)
            sp.dma_start(v_b[:], A["lq_vb"]).then_inc(w_got, 16)
            sp.wait_ge(w_got, 48)

        with nc.Block(no_gpsimd_drain=True) as block:

            @block.sync
            def _(sp):
                load(sp)

            @block.scalar
            def _(act):
                act.wait_ge(w_got, 48)
                for n in range(4):
                    cut = slice(n * WN // 4, (n + 1) * WN // 4)
                    nc.scalar.activation(w_hi[:, cut], w[:, cut], ACT.Copy).then_inc(w_s, 1)

            @block.vector
            def _(dve):
                nc.vector.tensor_scalar(x2[:], S.xT[:], 2.0, None, ALU.mult)
                dve.wait_ge(w_got, 48)
                nc.vector.tensor_scalar(cols[:, 2:2 + HG], cols[:, 2:2 + HG], SC, None, ALU.mult)
                for n in range(4):
                    cut = slice(n * WN // 4, (n + 1) * WN // 4)
                    dve.wait_ge(w_s, n + 1)
                    nc.vector.tensor_tensor(w_lo[:, cut], w[:, cut], w_hi[:, cut], ALU.subtract)

        layernorm_phase(nc, S, S.xT, S.rT, gain=cols[:, 0:1], shift=cols[:, 1:2])

        def weight(kind, n):
            at = (kind * HG * E if kind < 2 else 2 * HG * E + (kind - 2) * E) + n
            return w_hi[:, at * P:(at + 1) * P], w_lo[:, at * P:(at + 1) * P]

        q_up, q_ev, k_up, k_ev, v_up, v_ev, parts_hi, parts, s_up, mx_s, exp_s, t_up, hi_s, lo_s, o_up, rec_s, rows_s, ot_up, \
            ot_hi, ot_lo, y_up, y_ev = S.sems.new(*(f"lq_{n}" for n in (
                "q_up", "q_ev", "k_up", "k_ev", "v_up", "v_ev", "parts_hi", "parts", "s_up", "max", "exp", "t_up", "hi",
                "lo", "o_up", "rec", "rows", "ot_up", "ot_hi", "ot_lo", "y_up", "y_ev")))
        pool_start = S.sems.new("lq_pool_start")
        block = ctx.enter_context(nc.Block(no_gpsimd_drain=True))

        def start(j, k):
            return j * (2 * T) + k * T

        @block.tensor
        def _(pe):
            def step(j, k):
                if k % H == 0 and live(j, k, UN):
                    b = k // H
                    x = [[t[:, bass.ds(start(j, b) + n * QT, QT)] for t in (S.x_hi, S.x_lo)] for n in range(E)]
                    wait(pe, v_ev, j, b)
                    for kind, sem in ((0, q_up), (1, k_up)):
                        if kind:
                            wait(pe, y_ev, j, b - 2)
                        for n in range(E):
                            for a in range(HG):
                                last = products(nc, ps[:, 6 + kind, a * T + n * QT:a * T + (n + 1) * QT],
                                                weight(kind, n * HG + a), x[n])
                        last.then_inc(sem, 1)
                    wait(pe, q_ev, j, b + 1)
                    for i in range(TB):
                        xt = [t[:, bass.ds(start(j, b) + i * P, P)] for t in (S.x_hi, S.x_lo)]
                        at = (2 * HG * E + 2 * i) * P
                        last = products(nc, ps[:, 6, i * T:(i + 1) * T], xt, (w_hi[:, at:at + 2 * P], w_lo[:, at:at + 2 * P]))
                    last.then_inc(v_up, 1)
                if live(j, k - 8, UN):
                    u = k - 8
                    b, a, r = u // H, u % H // 4, slice(u % 4 * 32, u % 4 * 32 + 32)
                    wait(pe, exp_s, j, u - 1, R)
                    if u % H == 0:
                        wait(pe, parts, j, b + 1)
                    for i in range(TB):
                        last = products(nc, ps[:, u % 2, i * T:(i + 1) * T],
                                        [t[r, b % 2, a * T + i * P:a * T + (i + 1) * P] for t in (q_hi, q_lo)],
                                        [t[r, b % 2, a * T:(a + 1) * T] for t in (k_hi, k_lo)])
                    last.then_inc(s_up, 1)
                if live(j, k - 10, UN):
                    u = k - 10
                    wait(pe, exp_s, j, u + 1, R)
                    wait(pe, lo_s, j, u - 1, R)
                    for c in range(TB):
                        for i in range(TB):
                            last = nc.tensor.transpose(ps[:, 2 + u % 2, c * T + i * P:c * T + (i + 1) * P],
                                                       e[:, u % 2, i * T + c * P:i * T + (c + 1) * P], S.ident[:])
                    last.then_inc(t_up, 1)
                if live(j, k - 12, UN):
                    u = k - 12
                    b, h = u // H, u % H
                    wait(pe, lo_s, j, u + 1, R)
                    if h == 0:
                        wait(pe, ot_lo, j, b - 1)
                    for i in range(TB):
                        for c in range(TB):
                            last = products(nc, ps[:, 4 + b % 2, i * P + h * DH:i * P + (h + 1) * DH],
                                            [t[:, u % 4, c * T + i * P:c * T + (i + 1) * P] for t in (p_hi, p_lo)],
                                            [t[:, b % 2, c * P + h * DH:c * P + (h + 1) * DH] for t in (v_hi, v_lo)],
                                            first=(c == 0), last=(c == TB - 1))
                    last.then_inc(o_up, 1)
                if k % H == 4 and live(j, k - 20, UN):
                    b = k // H - 2
                    wait(pe, rows_s, j, b + 1)
                    for i in range(TB):
                        last = nc.tensor.transpose(ps[:, 4 + b % 2, T + i * P:T + (i + 1) * P], rows[:, i, :], S.ident[:])
                    last.then_inc(ot_up, 1)
                if k % H == 6 and live(j, k - 22, UN):
                    b = k // H - 2
                    wait(pe, ot_lo, j, b + 1)
                    wait(pe, k_ev, j, b + 3 if not isinstance(j, int) else min(b + 3, B))
                    for n in range(E):
                        cut = slice(n * QT, (n + 1) * QT)
                        last = products(nc, ps[:, 7, cut], weight(3, n), (o_hi[:, cut], o_lo[:, cut]))
                    last.then_inc(y_up, 1)
            pipeline(pe, UN, 23, step, R, 2 * R)

        @block.scalar
        def _(act):
            def step(j, k):
                if live(j, k - 8, UN):
                    u = k - 8
                    b, h = u // H, u % H
                    wait(act, mx_s, j, u + 1, R)
                    wait(act, t_up, j, u - 1, R)
                    if h == 0:
                        wait(act, rows_s, j, b - 1)
                    for i in range(TB):
                        last = nc.scalar.activation(e[:, u % 2, i * T:(i + 1) * T], ps[:, u % 2, i * T:(i + 1) * T], ACT.Exp,
                                                    bias=neg[:, u % 4, i:i + 1], accum_out=sums[:, b % 2, i, h:h + 1])
                    last.then_inc(exp_s, 1)
                if live(j, k - 10, UN):
                    u = k - 10
                    wait(act, t_up, j, u + 1, R)
                    wait(act, o_up, j, u - 3, R)
                    nc.scalar.activation(p_hi[:, u % 4, :], ps[:, 2 + u % 2, :], ACT.Copy).then_inc(hi_s, 1)
                if k % H == 5 and live(j, k - 21, UN):
                    b = k // H - 2
                    wait(act, ot_up, j, b + 1)
                    wait(act, y_up, j, b)
                    nc.scalar.activation(o_hi[:], ps[:, 4 + b % 2, T:2 * T], ACT.Copy).then_inc(ot_hi, 1)
            pipeline(act, UN, 23, step, R, 2 * R)

        @block.gpsimd
        def _(pool):
            def step(j, k):
                if k % H == 0 and live(j, k, UN):
                    b = k // H
                    wait(pool, v_ev, j, b + 1)
                    wait(pool, s_up, j, H * (b - 1), R)
                    pool.sem_inc(pool_start, 1)
                    nc.gpsimd.tensor_copy(q_hi[:, b % 2, :], q32[:])
                    nc.gpsimd.tensor_copy(k_hi[:, b % 2, :], k32[:])
                    wait(pool, o_up, j, H * (b - 1), R)
                    pool.sem_inc(pool_start, 1)
                    nc.gpsimd.tensor_copy(v_hi[:, b % 2, 0:2 * P], v32[:, 0:2 * P]).then_inc(parts_hi, 1)
            pipeline(pool, UN, 0, step, R, 2 * R)

        @block.vector
        def _(dve):
            def step(j, k):
                if k % H == 0 and live(j, k, UN):
                    b = k // H
                    wait(dve, parts, j, b)
                    wait(dve, q_up, j, b + 1)
                    for a in range(HG):
                        cut = slice(a * T, (a + 1) * T)
                        last = nc.vector.tensor_scalar(q32[:, cut], ps[:, 6, cut], SC, cols[:, 2 + a:3 + a], ALU.mult, ALU.add)
                    last.then_inc(q_ev, 1)
                    wait(dve, k_up, j, b + 1)
                    for a in range(HG):
                        cut = slice(a * T, (a + 1) * T)
                        last = nc.vector.tensor_scalar(k32[:, cut], ps[:, 7, cut], cols[:, 2 + HG + a:3 + HG + a], None, ALU.add)
                    last.then_inc(k_ev, 1)
                    wait(dve, v_up, j, b + 1)
                    for n in range(2):
                        r = slice(n * QT, (n + 1) * QT)
                        last = nc.vector.tensor_tensor(v32[r, :2 * P].rearrange("p (i d) -> p i d", i=TB),
                                                       ps[r, 6, :].rearrange("p (i m) -> p i m", i=TB)[:, :, n * P:(n + 1) * P],
                                                       v_b[r].unsqueeze(1).broadcast_to([QT, TB, P]), ALU.add)
                    last.then_inc(v_ev, 1)
                if k % H == 6 and live(j, k - 6, UN):
                    b = k // H
                    wait(dve, parts_hi, j, b + 1)
                    for lo, hi, full in ((q_lo, q_hi, q32), (k_lo, k_hi, k32), (v_lo, v_hi, v32)):
                        m = 2 * P if full is v32 else 2 * T
                        last = nc.vector.tensor_tensor(lo[:, b % 2, 0:m], full[:, 0:m], hi[:, b % 2, 0:m], ALU.subtract)
                    last.then_inc(parts, 1)
                if live(j, k - 8, UN):
                    u = k - 8
                    wait(dve, s_up, j, u + 1, R)
                    nc.vector.tensor_reduce(neg[:, u % 4, :], ps[:, u % 2, :].rearrange("p (i n) -> p i n", i=TB), AX.X,
                                            ALU.max, negate=True).then_inc(mx_s, 1)
                if live(j, k - 11, UN):
                    u = k - 11
                    wait(dve, hi_s, j, u + 1, R)
                    nc.vector.tensor_tensor(p_lo[:, u % 4, :], ps[:, 2 + u % 2, :], p_hi[:, u % 4, :], ALU.subtract)\
                        .then_inc(lo_s, 1)
                if k % H == 3 and live(j, k - 19, UN):
                    b = k // H - 2
                    wait(dve, o_up, j, H * (b + 1), R)
                    nc.vector.reciprocal(rec[:], sums[:, b % 2]).then_inc(rec_s, 1)
                    wait(dve, rec_s, j, b + 1)
                    wait(dve, ot_up, j, b)
                    nc.vector.tensor_tensor(rows[:].rearrange("p i (h d) -> p (i h) d", h=H),
                                            ps[:, 4 + b % 2, 0:T].rearrange("p (g d) -> p g d", d=DH),
                                            rec[:].rearrange("p i h -> p (i h)").unsqueeze(2).broadcast_to([P, TB * H, DH]),
                                            ALU.mult).then_inc(rows_s, 1)
                if k % H == 5 and live(j, k - 21, UN):
                    b = k // H - 2
                    wait(dve, ot_hi, j, b + 1)
                    nc.vector.tensor_tensor(o_lo[:], ps[:, 4 + b % 2, T:2 * T], o_hi[:], ALU.subtract).then_inc(ot_lo, 1)
                if k % H == 7 and live(j, k - 23, UN):
                    b = k // H - 2
                    wait(dve, y_up, j, b + 1)
                    for n in range(E):
                        at = bass.ds(start(j, b) + n * QT, QT)
                        c = 2 + 2 * HG + n
                        last = nc.vector.scalar_tensor_tensor(out=S.rT[:, at], in0=ps[:, 7, n * QT:(n + 1) * QT],
                                                              scalar=cols[:, c:c + 1], in1=x2[:, at], op0=ALU.add,
                                                              op1=ALU.add)
                    last.then_inc(y_ev, 1)
            pipeline(dve, UN, 24, step, R, 2 * R)


def build(nc, A, out):
    S = State()
    S.sems = Sems(nc)
    S.eps = [1e-5, 1e-4, 1.0]
    with (nc.psum_tensor("ps", [P, 8, 512], F32) as ps,
          nc.sbuf_tensor("xT", [P, N], F32) as xT,
          nc.sbuf_tensor("rT", [P, N], F32) as rT,
          nc.sbuf_tensor("x_hi", [P, N], F16) as x_hi,
          nc.sbuf_tensor("x_lo", [P, N], F16) as x_lo,
          nc.sbuf_tensor("ident", [P, P], F32) as ident,
          nc.sbuf_tensor("identb", [P, P], BF16) as identb,
          nc.sbuf_tensor("epsilons", [P, 3], F32) as epsilons):
        S.psum, S.xT, S.rT, S.ident, S.identb, S.epsilons = ps, xT, rT, ident, identb, epsilons
        S.x_hi, S.x_lo = x_hi, x_lo
        S.eps_ap = lambda e: epsilons[:, S.eps.index(e):S.eps.index(e) + 1]
        S.one = S.eps_ap(1.0)
        load_phase(nc, S, A)
        stages = [l0_attn, l0_ffn, l1_attn, l1_ffn, l2_attn, l2_ffn, l3_attn, l3_ffn]
        for k in STAGES:
            stages[int(k)](nc, S, A)
            layernorm_phase(nc, S, rT, xT, out=out if k == STAGES[-1] else None)
            if k != STAGES[-1]:
                S.sems.give_back()


def layout(I):
    bf16 = mybir.dt.np(BF16)
    L = {}
    f = np.float32
    L["c_ident"] = np.eye(P, dtype=f)
    L["c_identb"] = np.eye(P, dtype=bf16)
    L["L0_attn_tokens"] = I["L0_attn_tokens"]
    a = np.zeros((2, 64, 8, 2, 64), f)
    b = np.zeros((16, 8, 8, 2, 64), f)
    c = np.zeros((2, 64, 8, 16, 8), f)
    for h in range(16):
        a[h % 2, :, h // 2, h % 2, :] = I["L0_attn_a"][h]
        b[h, :, h // 2, h % 2, :] = I["L0_attn_b"][h]
        c[h % 2, :, h // 2, h, :] = I["L0_attn_c"][h]
    L["L0_attn_a"] = a.reshape(P, 8, P)
    L["L0_attn_b"] = b.reshape(P, 8, P)
    L["L0_attn_c"] = c.reshape(P, 8, P)
    L["L0_attn_w_out"] = I["L0_attn_w_out"].T
    L["L0_attn_cols"] = np.stack([I["L0_attn_norm_w"], I["L0_attn_skip"].reshape(-1), I["L0_attn_b_out"]], axis=1)
    w1 = I["L0_ffn_w1"].reshape(8, P, 2, P).transpose(0, 2, 1, 3).reshape(16, P, P)
    w2 = I["L0_ffn_w2"].reshape(16, P, P)
    L["m0_w"] = np.concatenate([w1, w2], axis=2)
    L["m0_router"] = I["L0_ffn_router_w"].T

    def ups(w):
        return w.reshape(-1, P, P).transpose(0, 2, 1)

    def downs(w):
        return w.transpose(0, 2, 1).reshape(-1, P, P)

    eg = np.concatenate([I["L1_ffn_eg_w"].reshape(-1, P), I["L1_ffn_sg_w"]])
    eu = np.concatenate([I["L1_ffn_eu_w"].reshape(-1, P), I["L1_ffn_su_w"]])
    sd = I["L1_ffn_sd_w"].reshape(P, 2, 64).transpose(1, 0, 2)
    ed = np.concatenate([I["L1_ffn_ed_w"], sd])
    L["m1_w"] = np.concatenate([ups(eg), ups(eu), downs(ed)], axis=2)
    L["m1_router"] = I["L1_ffn_gate_w"].T
    L["m1_bias"] = np.repeat(I["L1_ffn_gate_bias"][None], P, axis=0)
    z = np.zeros((64, P), f)
    eg = np.concatenate([I["L2_ffn_w_gate"].reshape(-1, P), I["L2_ffn_w_gate_shared"], z])
    ed = np.concatenate([I["L2_ffn_w_down"], I["L2_ffn_w_down_shared"][None], z.reshape(1, P, 64)])
    L["m2_w"] = np.concatenate([ups(eg), downs(ed)], axis=2)
    L["m2_router"] = I["L2_ffn_router_w"].T
    L["m2_bias"] = np.repeat(I["L2_ffn_expert_bias"][None], P, axis=0)
    e = np.arange(3 * GE)[:, None, None] % GE
    m = np.arange(P)[None, None, :]
    L["c_sel_halves"] = (e == np.arange(16)[None, :, None] // 2 + 0 * m).astype(bf16)
    L["c_sel_pairs"] = (e == 2 * np.arange(GE // 2)[None, :, None] + m // 64).astype(bf16)
    w_k = I["L1_attn_W_k"]
    turned = w_k.reshape(64, 2, P)[:, ::-1].reshape(P, P)
    q = np.zeros((16, 8, 8, 2, 64), f)
    lat = I["L1_attn_latent_queries"][0]
    for h in range(16):
        q[h, :, h // 2, h % 2, :] = lat[:, h, :].T
    L["la_w"] = np.concatenate([w_k.T, turned.T, I["L1_attn_W_v"].T, I["L1_attn_W_p"].T, I["L1_attn_W_g"].T,
                                q.reshape(P, 8 * P)], axis=1)
    steps = (np.arange(2)[:, None] * P + np.arange(64)).reshape(-1)
    inv = (1.0 / 10000.0 ** (np.arange(0, 8, 2, dtype=f) / 8)).astype(f)
    ang = inv[np.arange(P) % 8 // 2][:, None] * steps[None, :].astype(f)
    sign = np.where(np.arange(P) % 2, 1.0, -1.0).astype(f)[:, None]
    L["la_rope"] = np.stack([np.cos(ang), np.sin(ang) * sign], axis=1).astype(f)
    seen = np.arange(64)[None, :] <= np.arange(P)[:, None] % 64
    L["la_mask"] = np.tile(np.where(seen, 0.0, -1e30), (1, 8)).astype(bf16)
    pair = (np.arange(P)[:, None] // 64 == np.arange(16)[None, :] // 8)
    L["la_own"] = pair.astype(f)
    ones = np.zeros((P, 8, 8, 18), np.float16)
    ones[:, :, :, 16:18] = pair[:, None, None, ::8]
    L["la_ones_hi"] = ones
    L["la_zeros"] = np.zeros((P, 8, 8, 18), np.float16)
    L["lg_w"] = np.concatenate([I["L2_attn_Wq"], I["L2_attn_Wk"], I["L2_attn_Wv"], I["L2_attn_Wgk"], I["L2_attn_Wg"]], axis=1)
    L["lg_bgk"] = np.repeat(I["L2_attn_bgk"][None], P, axis=0)
    L["lg_wo"] = I["L2_attn_Wo"].reshape(2, P, P).transpose(1, 0, 2)
    L["lg_norm"] = np.tile(I["L2_attn_gnorm_w"], 2)[:, None]
    upto = np.triu(np.ones((P, P), np.float16))
    one, none = np.ones((P, P), np.float16), np.zeros((P, P), np.float16)
    L["lg_tri"] = np.concatenate([upto, one, one, none, upto, upto], axis=1)
    later = np.where(upto > 0, 0.0, -1e30).astype(bf16)
    L["lg_mask"] = np.concatenate([later, none.astype(bf16), later], axis=1)
    L["lj_w"] = np.concatenate([I["L3_attn_wq"], I["L3_attn_wk"], I["L3_attn_wv"], I["L3_attn_wo"], I["L3_attn_w1"]]
                               + [I["L3_attn_w2"][:, n * P:(n + 1) * P] for n in range(4)], axis=2)
    L["lj_cols"] = np.stack([I["L3_attn_" + n] for n in ("ln1_w", "ln1_b", "bo", "ln2_w", "ln2_b")], axis=2)\
        .transpose(1, 0, 2)
    L["lj_own"] = (np.arange(P)[:, None] // 16 == np.arange(P)[None, :] // 16).astype(f)

    def spread(w):
        out = np.zeros((len(w), 2, 4, 32), f)
        out[..., :16] = w.reshape(-1, 2, 4, 16)
        return out.reshape(-1, 2 * P)

    def first(w, n, both=False):
        out = np.zeros_like(w)
        m = P >> n
        out[:m, :m if both else None] = w[:m, :m if both else None]
        return out

    L["lq_w"] = np.concatenate([first(spread(I["L3_ffn_" + s].T), n) for s in ("q_w", "k_w") for n in range(4)]
                               + [first(I["L3_ffn_v_w"].T, n) for n in range(4)]
                               + [first(I["L3_ffn_o_w"].T, n, True) for n in range(4)], axis=1)
    o_b = np.zeros((4, P), f)
    for n in range(4):
        o_b[n, :P >> n] = I["L3_ffn_o_b"][:P >> n]
    L["lq_cols"] = np.concatenate([I["L3_ffn_norm_w"][None], I["L3_ffn_norm_b"][None]]
                                  + [spread(I["L3_ffn_" + s][None]).reshape(2, P) for s in ("q_b", "k_b")] + [o_b]).T
    L["lq_vb"] = np.repeat(I["L3_ffn_v_b"][None], P, axis=0)
    return L


def kernel(**inputs):
    import concourse.bacc as _bacc
    from concourse.bass_utils import run_bass_kernel_spmd as _run

    I = {k: np.asarray(v) for k, v in inputs.items()}
    L = layout(I)
    nc = _bacc.Bacc("TRN2", target_bir_lowering=False, num_devices=1)
    arrays, A = {}, {}
    for name, a in L.items():
        a = np.ascontiguousarray(a)
        arrays[f"in_{name}"] = a
        A[name] = nc.dram_tensor(f"in_{name}", a.shape, mybir.dt.from_np(a.dtype), kind="ExternalInput").ap()
    out = nc.dram_tensor("out", (B, T, C), F32, kind="ExternalOutput").ap()
    build(nc, A, out)
    r = _run(nc, [arrays], core_ids=[0])
    return r.results[0]["out"]
```
